# Optimizing a Trainium2 kernel written in Bass

```python
import numpy as np
import jax
import jax.numpy as jnp

def _softmax(x, axis=-1):
    return jax.nn.softmax(x, axis=axis)

def _gelu(x):
    return jax.nn.gelu(x, approximate=True)

def _silu(x):
    return jax.nn.silu(x)

def _sigmoid(x):
    return jax.nn.sigmoid(x)

def _layernorm(x, axis=-1, eps=1e-05):
    m = jnp.mean(x, axis=axis, keepdims=True)
    v = jnp.var(x, axis=axis, keepdims=True)
    return (x - m) / jnp.sqrt(v + eps)

def _scatter_add(tgt, idx, src, axis=0):
    return tgt.at[idx].add(src)

def _segment_sum(src, seg, n):
    return jax.ops.segment_sum(src, seg, n)
kernel_name = 'mk_cond_resid_d2_seqx_r4_fb6a28'

def setup_inputs(seed: int=0):
    np.random.seed(seed)
    _w = jnp.asarray

    def _rec_inputs():
        import jax
        import jax.numpy as jnp
        _rk = jax.random.key(seed)
        x = -5.13e-06 + 0.01765 * jax.random.normal(jax.random.fold_in(_rk, 1), (4, 512, 256), jnp.float32)
        _lenS = 512 - jax.random.randint(jax.random.fold_in(_rk, 7), (4,), 0, max(1, 512 // 4) + 1, jnp.int32)
        _lenS2 = 512 - jax.random.randint(jax.random.fold_in(_rk, 8), (4,), 0, max(1, 512 // 4) + 1, jnp.int32)
        cond_1024 = 0.0061147 + 1.02565 * jax.random.normal(jax.random.fold_in(_rk, 11), (4, 256), jnp.float32)
        return (x, cond_1024)
    x, cond_1024 = _rec_inputs()

    def _L0_cond_setup():
        import math
        import jax, jax.numpy as jnp
        import numpy as np
        EPS = 1e-07
        MAX_TANH_ARG = 1.0 - 1e-05

        def _norm(x):
            return jnp.sqrt(jnp.sum(x * x, axis=-1, keepdims=True)).clip(EPS)

        def logmap0(x):
            n = _norm(x)
            return jnp.arctanh(jnp.clip(n, EPS, MAX_TANH_ARG)) * x / n

        def expmap0(v):
            n = _norm(v)
            return jnp.tanh(n) * v / n

        def mobius_add(x, y):
            x2 = jnp.sum(x * x, -1, keepdims=True)
            y2 = jnp.sum(y * y, -1, keepdims=True)
            xy = jnp.sum(x * y, -1, keepdims=True)
            num = (1 + 2 * xy + y2) * x + (1 - x2) * y
            den = (1 + 2 * xy + x2 * y2).clip(EPS)
            return num / den

        def plin(x, w, b):
            return expmap0(logmap0(x) @ w + b)

        def layer_norm(x, eps=1e-06):
            m = x.mean(-1, keepdims=True)
            v = ((x - m) ** 2).mean(-1, keepdims=True)
            return (x - m) / jnp.sqrt(v + eps)

        def _beta(a, b):
            return math.exp(math.lgamma(a) + math.lgamma(b) - math.lgamma(a + b))
        D, H, FF = (256, 16, 1024)
        HD = D // H
        BETA_N = _beta(D / 2, 0.5)
        BETA_H = _beta(HD / 2, 0.5)

        def _to_heads(p):
            B, S, _ = p.shape
            t = logmap0(p).reshape(B, S, H, HD) * (BETA_H / BETA_N)
            return expmap0(jnp.transpose(t, (0, 2, 1, 3)))

        def _from_heads(ph):
            B, _, S, _ = ph.shape
            t = logmap0(ph) * (BETA_N / BETA_H)
            t = jnp.transpose(t, (0, 2, 1, 3)).reshape(B, S, D)
            return expmap0(t)
        key = jax.random.key(seed)
        ks = jax.random.split(key, 20)
        B, S = (4, 256)
        x = expmap0(0.02 * jax.random.normal(ks[0], (B, S, D), jnp.float32))
        t_emb = jax.random.normal(ks[1], (B, 1, D), jnp.float32)
        g = lambda k, sh: 0.02 * jax.random.normal(k, sh, jnp.float32)
        return {'x': x, 't_emb': t_emb, 'w_q': g(ks[2], (D, D)), 'b_q': jnp.zeros((D,), jnp.float32), 'w_k': g(ks[3], (D, D)), 'b_k': jnp.zeros((D,), jnp.float32), 'w_v': g(ks[4], (D, D)), 'b_v': jnp.zeros((D,), jnp.float32), 'w_o': g(ks[5], (D, D)), 'b_o': jnp.zeros((D,), jnp.float32), 'w_f1': g(ks[6], (D, FF)), 'b_f1': jnp.zeros((FF,), jnp.float32), 'w_f2': g(ks[7], (FF, D)), 'b_f2': jnp.zeros((D,), jnp.float32), 'w_ada': g(ks[8], (D, 6 * D)), 'b_ada': jnp.zeros((6 * D,), jnp.float32)}
    _L0_cond_all = _L0_cond_setup()
    _L0_cond_in = {k: v for k, v in _L0_cond_all.items() if k in ('w_q', 'b_q', 'w_k', 'b_k', 'w_v', 'b_v', 'w_o', 'b_o', 'w_f1', 'b_f1', 'w_f2', 'b_f2', 'w_ada', 'b_ada')}
    del _L0_cond_all

    def _L1_cond_setup():
        import jax, jax.numpy as jnp
        import numpy as np
        D = 256
        H = 256
        N = 64
        T = 128

        def _lstm(x, h0, Wx, Wh, b):
            xW = jnp.einsum('ntd,dk->tnk', x, Wx) + b
            c0 = jnp.zeros_like(h0)
            Hdim = h0.shape[1]

            def step(carry, xw_t):
                prev_h, prev_c = carry
                a = xw_t + prev_h @ Wh
                i = jax.nn.sigmoid(a[:, 0:Hdim])
                f = jax.nn.sigmoid(a[:, Hdim:2 * Hdim])
                o = jax.nn.sigmoid(a[:, 2 * Hdim:3 * Hdim])
                g = jnp.tanh(a[:, 3 * Hdim:4 * Hdim])
                next_c = f * prev_c + i * g
                next_h = o * jnp.tanh(next_c)
                return ((next_h, next_c), next_h)
            _, hs = jax.lax.scan(step, (h0, c0), xW)
            return jnp.transpose(hs, (1, 0, 2))
        key = jax.random.key(seed)
        k1, k2, k3, k4 = jax.random.split(key, 4)
        x = jax.random.normal(k1, (N, T, D), dtype=jnp.float32)
        h0 = jax.random.normal(k2, (N, H), dtype=jnp.float32)
        Wx = jax.random.normal(k3, (D, 4 * H), dtype=jnp.float32) / np.sqrt(D)
        Wh = jax.random.normal(k4, (H, 4 * H), dtype=jnp.float32) / np.sqrt(H)
        b = jnp.zeros((4 * H,), dtype=jnp.float32)
        return {'x': x, 'h0': h0, 'Wx': Wx, 'Wh': Wh, 'b': b}
    _L1_cond_all = _L1_cond_setup()
    _L1_cond_in = {k: v for k, v in _L1_cond_all.items() if k in ('Wx', 'Wh', 'b')}
    del _L1_cond_all
    return {'x': x, 'cond_1024': cond_1024, 'L0_cond_w_q': _L0_cond_in['w_q'], 'L0_cond_b_q': _L0_cond_in['b_q'], 'L0_cond_w_k': _L0_cond_in['w_k'], 'L0_cond_b_k': _L0_cond_in['b_k'], 'L0_cond_w_v': _L0_cond_in['w_v'], 'L0_cond_b_v': _L0_cond_in['b_v'], 'L0_cond_w_o': _L0_cond_in['w_o'], 'L0_cond_b_o': _L0_cond_in['b_o'], 'L0_cond_w_f1': _L0_cond_in['w_f1'], 'L0_cond_b_f1': _L0_cond_in['b_f1'], 'L0_cond_w_f2': _L0_cond_in['w_f2'], 'L0_cond_b_f2': _L0_cond_in['b_f2'], 'L0_cond_w_ada': _L0_cond_in['w_ada'], 'L0_cond_b_ada': _L0_cond_in['b_ada'], 'L1_cond_Wx': _L1_cond_in['Wx'], 'L1_cond_Wh': _L1_cond_in['Wh'], 'L1_cond_b': _L1_cond_in['b']}

def reference(x, cond_1024, L0_cond_w_q, L0_cond_b_q, L0_cond_w_k, L0_cond_b_k, L0_cond_w_v, L0_cond_b_v, L0_cond_w_o, L0_cond_b_o, L0_cond_w_f1, L0_cond_b_f1, L0_cond_w_f2, L0_cond_b_f2, L0_cond_w_ada, L0_cond_b_ada, L1_cond_Wx, L1_cond_Wh, L1_cond_b):
    import jax
    import jax.numpy as jnp

    def _L0_cond_ref(x, t_emb, w_q, b_q, w_k, b_k, w_v, b_v, w_o, b_o, w_f1, b_f1, w_f2, b_f2, w_ada, b_ada):
        import math
        import jax, jax.numpy as jnp
        import numpy as np
        EPS = 1e-07
        MAX_TANH_ARG = 1.0 - 1e-05

        def _norm(x):
            return jnp.sqrt(jnp.sum(x * x, axis=-1, keepdims=True)).clip(EPS)

        def logmap0(x):
            n = _norm(x)
            return jnp.arctanh(jnp.clip(n, EPS, MAX_TANH_ARG)) * x / n

        def expmap0(v):
            n = _norm(v)
            return jnp.tanh(n) * v / n

        def mobius_add(x, y):
            x2 = jnp.sum(x * x, -1, keepdims=True)
            y2 = jnp.sum(y * y, -1, keepdims=True)
            xy = jnp.sum(x * y, -1, keepdims=True)
            num = (1 + 2 * xy + y2) * x + (1 - x2) * y
            den = (1 + 2 * xy + x2 * y2).clip(EPS)
            return num / den

        def plin(x, w, b):
            return expmap0(logmap0(x) @ w + b)

        def layer_norm(x, eps=1e-06):
            m = x.mean(-1, keepdims=True)
            v = ((x - m) ** 2).mean(-1, keepdims=True)
            return (x - m) / jnp.sqrt(v + eps)

        def _beta(a, b):
            return math.exp(math.lgamma(a) + math.lgamma(b) - math.lgamma(a + b))
        D, H, FF = (256, 16, 1024)
        HD = D // H
        BETA_N = _beta(D / 2, 0.5)
        BETA_H = _beta(HD / 2, 0.5)

        def _to_heads(p):
            B, S, _ = p.shape
            t = logmap0(p).reshape(B, S, H, HD) * (BETA_H / BETA_N)
            return expmap0(jnp.transpose(t, (0, 2, 1, 3)))

        def _from_heads(ph):
            B, _, S, _ = ph.shape
            t = logmap0(ph) * (BETA_N / BETA_H)
            t = jnp.transpose(t, (0, 2, 1, 3)).reshape(B, S, D)
            return expmap0(t)
        ada = t_emb @ w_ada + b_ada
        sh_msa, sc_msa, g_msa, sh_mlp, sc_mlp, g_mlp = jnp.split(ada, 6, axis=-1)
        residual = x
        xn = layer_norm(logmap0(x))
        xm = expmap0(xn * (1 + sc_msa) + sh_msa)
        q = _to_heads(plin(xm, w_q, b_q))
        k = _to_heads(plin(xm, w_k, b_k))
        v = _to_heads(plin(xm, w_v, b_v))
        qt, kt, vt = (logmap0(q), logmap0(k), logmap0(v))
        scores = jnp.einsum('bhqd,bhkd->bhqk', qt, kt) / math.sqrt(HD)
        attn = jax.nn.softmax(scores, axis=-1)
        out_h = expmap0(jnp.einsum('bhqk,bhkd->bhqd', attn, vt))
        attn_out = plin(_from_heads(out_h), w_o, b_o)
        attn_t = g_msa * logmap0(attn_out)
        x = mobius_add(residual, expmap0(attn_t))
        residual = x
        xn = layer_norm(logmap0(x))
        xm = expmap0(xn * (1 + sc_mlp) + sh_mlp)
        ff = plin(plin(xm, w_f1, b_f1), w_f2, b_f2)
        ff_t = g_mlp * logmap0(ff)
        return mobius_add(residual, expmap0(ff_t))

    def _L1_cond_ref(x, h0, Wx, Wh, b):
        import jax, jax.numpy as jnp
        import numpy as np
        D = 256
        H = 256
        N = 64
        T = 128

        def _lstm(x, h0, Wx, Wh, b):
            xW = jnp.einsum('ntd,dk->tnk', x, Wx) + b
            c0 = jnp.zeros_like(h0)
            Hdim = h0.shape[1]

            def step(carry, xw_t):
                prev_h, prev_c = carry
                a = xw_t + prev_h @ Wh
                i = jax.nn.sigmoid(a[:, 0:Hdim])
                f = jax.nn.sigmoid(a[:, Hdim:2 * Hdim])
                o = jax.nn.sigmoid(a[:, 2 * Hdim:3 * Hdim])
                g = jnp.tanh(a[:, 3 * Hdim:4 * Hdim])
                next_c = f * prev_c + i * g
                next_h = o * jnp.tanh(next_c)
                return ((next_h, next_c), next_h)
            _, hs = jax.lax.scan(step, (h0, c0), xW)
            return jnp.transpose(hs, (1, 0, 2))
        return _lstm(x, h0, Wx, Wh, b)
    x = x + _L0_cond_ref(x, cond_1024[:, None, :], L0_cond_w_q, L0_cond_b_q, L0_cond_w_k, L0_cond_b_k, L0_cond_w_v, L0_cond_b_v, L0_cond_w_o, L0_cond_b_o, L0_cond_w_f1, L0_cond_b_f1, L0_cond_w_f2, L0_cond_b_f2, L0_cond_w_ada, L0_cond_b_ada)
    x = x + _L1_cond_ref(x, cond_1024, L1_cond_Wx, L1_cond_Wh, L1_cond_b)
    return x

_drawn_inputs = setup_inputs


def setup_inputs(seed=0):
    import zlib

    import numpy as np

    out = dict(_drawn_inputs(seed))
    spreads = {'L0_cond_b_q': (0.0, 2.0),
     'L0_cond_b_k': (0.0, 2.0),
     'L0_cond_b_v': (0.0, 0.1),
     'L0_cond_b_o': (0.0, 0.1),
     'L0_cond_b_f1': (0.0, 0.1),
     'L0_cond_b_f2': (0.0, 0.1),
     'L0_cond_b_ada': (0.0, 0.1),
     'L1_cond_b': (0.0, 0.1)}
    factors = {'L0_cond_w_q': 127.65, 'L0_cond_w_k': 37.548}
    for name, (base, spread) in spreads.items():
        noise = np.random.default_rng([zlib.crc32(name.encode()), seed]).standard_normal(out[name].shape)
        drawn = base * np.exp(spread * noise) if base else spread * noise
        out[name] = jnp.asarray(drawn.astype(out[name].dtype))
    for name, factor in factors.items():
        out[name] = (out[name] * factor).astype(out[name].dtype)
    return out
```

```python
import math
from contextlib import ExitStack

import numpy as np

import concourse.bass as bass
from concourse import mybir

F32 = mybir.dt.float32
F16 = mybir.dt.float16
I32 = mybir.dt.int32
ALU = mybir.AluOpType
ACT = mybir.ActivationFunctionType
AX = mybir.AxisListType

B, T, D, H, FF, P = 4, 512, 256, 16, 1024, 128
HD = D // H
KD = D // P
KF = FF // P
NB = T // P
NT = B * NB
HP = H // 2
GC = 4 * D // P

EPS, LN_EPS = 1e-7, 1e-6
MAX_TANH = float(np.float32(1.0 - 1e-5))
REACH = float(np.arctanh(np.float64(MAX_TANH)))


def _beta(a, b):
    return math.exp(math.lgamma(a) + math.lgamma(b) - math.lgamma(a + b))


HEAD = _beta(HD / 2, 0.5) / _beta(D / 2, 0.5)
TINY = 1e-30
QK_UP = 256.0
H_UP = 2.0 ** 14
SERIES_BELOW = 0.01


class Chain:

    def __init__(self, eng, sem, held, per_round):
        self.eng, self.sem, self.held, self.per_round, self.base, self.n = eng, sem, held, per_round, 0, 0

    def round(self, number):
        self.base, self.n = (number - 1) * self.per_round, 0

    def link(self, ins):
        self.n += 1
        ins.then_inc(self.sem, 1)
        self.eng.wait_ge(self.sem, self.base + self.n)
        self.eng.sem_inc(self.held, 1)

    def full(self):
        assert self.n == self.per_round, (self.n, self.per_round)


def bass_hyperbolic_block_then_lstm(nc, x, cond, w_q, b_q, w_k, b_k, w_v, b_v, w_o, b_o, w_f1, b_f1, w_f2, b_f2,
                                    w_ada, b_ada, w_x, w_h, b_l, out):
    ctx = ExitStack()
    with ctx:
        def sb(name, shape, dt=F32):
            return ctx.enter_context(nc.sbuf_tensor(name, shape, dt))

        def sem(name):
            return ctx.enter_context(nc.semaphore(name))

        wqkv = sb("wqkv", [P, KD, 3, D])
        wo = sb("wo", [P, KD, D])
        wf1 = sb("wf1", [P, KD, FF])
        wf2 = sb("wf2", [P, KF, D])
        wx = sb("wx", [P, KD, 4 * D])
        wh16 = sb("wh16", [P, 2, KD, 4 * D], F16)
        bqkv = sb("bqkv", [P, 3, D])
        bo = sb("bo", [P, D])
        bf1 = sb("bf1", [P, FF])
        bf2 = sb("bf2", [P, D])
        blc = sb("blc", [P, GC])
        badac = sb("badac", [P, 6 * KD])
        ident = sb("ident", [P, P])
        ident16 = sb("ident16", [P, P], F16)
        ones = sb("ones", [P, P])
        adac = sb("adac", [P, 6 * KD, B])
        gates = sb("gates", [P, 2, B, D])
        xs = sb("xs", [P, NT, D])
        qhl = sb("qhl", [P, NT, H, 2 * HD], F16)
        kT = sb("kT", [P, B, HP, T], F16)
        vs = sb("vs", [P, B, NB, H, HD + 1])
        xsq = sb("xsq", [P, NT])
        kap = sb("kap", [P, NT])
        kmn = sb("kmn", [P, NT])
        hs = sb("hs", [P, KD, B, P])
        arena = sb("arena", [P, P * GC * B])
        xw = arena[:, 0:P * GC * B].rearrange("p (t g b) -> p t g b", g=GC, b=B)
        wada = arena[:, 0:KD * 6 * D].rearrange("p (k n) -> p k n", k=KD)
        big = sb("big", [P, 2, NB, 2 * P])
        wh = big[:, :, :, :].rearrange("p a b c -> p (a b c)").rearrange("p (k n) -> p k n", k=KD)
        lin = sb("lin", [P, 3, D])
        tmp = sb("tmp", [P, FF])
        xn = sb("xn", [P, D])
        uT = sb("uT", [P, KD, P])
        usq = sb("usq", [P, KD, P])
        fT = sb("fT", [P, KF, P])
        qk = sb("qk", [P, 2, D])
        stack = sb("stack", [P, H, 2, 2 * HD], F16)
        x2 = sb("x2", [P, D])
        x3 = sb("x3", [P, D])
        ot = sb("ot", [P, B * D])
        blc2 = sb("blc2", [P, GC])
        qbd = sb("qbd", [P, HP, 2 * P], F16)
        sc = sb("sc", [P, 640])
        cst = sb("cst", [P, 3, 64])
        c0 = sb("c0", [B, D])
        c0T = sb("c0T", [P, KD, B])
        c0B = sb("c0B", [P, KD, B, P])
        h0c = sb("h0c", [P, GC, B])
        mv6 = sb("mv6", [P, 6])
        mv = sb("mv", [P, NT + 1, 2])
        big1 = sb("big1", [P, 8])
        bits = sb("bits", [P, 1], I32)
        msk = sb("msk", [P, 1], I32)
        h16 = sb("h16", [P, KD, B, 2], F16)
        h32 = sb("h32", [P, KD * B])
        gA = sb("gA", [P, 48]); gF = sb("gF", [P, 24]); gO = sb("gO", [P, 24])
        tA = sb("tA", [P, 16]); tO = sb("tO", [P, 8]); oU = sb("oU", [P, 8])
        coef = sb("coef", [P, 16, 3])
        cmul = sb("cmul", [P, 8, 4]); cadd = sb("cadd", [P, 8, 4]); cnew = sb("cnew", [P, 8, 4])
        tC = sb("tC", [P, 8])

        bank = [ctx.enter_context(nc.psum_tensor(f"bank{i}", [P, 512], F32)) for i in range(8)]
        pA, pF, pO = bank[5], bank[6], bank[7]

        def half_words(i):
            return bank[i][:, :].bitcast(F16)

        names = """held achain ada_s adap c0t c0t_s consts dinit gp gp_s h0p hsc l_A l_F l_O l_c l_cc l_gA l_gF l_gO l_h0 l_h32 l_hi l_hs l_ig l_init l_lo l_oU l_tA l_tC l_tF l_tO l_x0 ld_b ld_c ld_h ld_w ld_x ln1 ln1z lnr o_T o_d o_free o_s p_f p_h p_hk p_kT p_kc p_lin p_mm p_n p_nh p_ns p_qk p_s1 p_sq p_ss p_su p_uT p_usq p_v p_xT p_xn pchain pk st1 t_AV t_E t_L t_S t_X t_XT t_XX t_Xc t_a t_a2 t_ab t_ab2 t_ar t_ar2 t_done t_f t_f1 t_fT t_fc t_fs t_ga t_ga2 t_km t_m1 t_m2 t_mo t_n1 t_n2 t_n3 t_n4 t_nm t_ns t_o t_oT t_oc t_op t_q t_qT t_qc t_r t_s6 t_sf t_so t_sq t_sqf t_ss t_st t_th t_th2 t_tot t_uT t_us t_w1 t_w2 t_x2 t_xT t_xa t_xa2 t_xn t_xw t_z vchain w16 wmax""".split()
        s = {n: sem("s_" + n) for n in names}

        def hold(eng, name, value):
            eng.wait_ge(s[name], value)
            eng.sem_inc(s["held"], 1)

        at = {}

        def num(name, w=1):
            if name not in at:
                at[name] = (sum(v[1] for v in at.values()), w)
                assert sum(v[1] for v in at.values()) <= 640
            o, w = at[name]
            return sc[:, o:o + w]

        HALF_DOWN, HALF_UP, DOWN = 0, 1, 2

        def power(ch, dst, src, which, w):
            ch.link(nc.gpsimd.tensor_tensor(dst, src, cst[:, which, 0:w], ALU.pow))

        def to_ratio(ch, w, m, var, nsq, done):
            g = nc.gpsimd
            a, b, c = num(f"a{w}", w), num(f"b{w}", w), num(f"c{w}", w)
            nc_, nd = num(f"nc{w}", w), num(f"nd{w}", w)
            ch.link(g.tensor_tensor(a, m, m, ALU.mult))
            ch.link(g.tensor_tensor(b, a, var, ALU.add))
            ch.link(g.tensor_scalar(nsq, b, float(D), None, ALU.mult))
            power(ch, a, nsq, HALF_UP, w)
            ch.link(g.tensor_scalar(nd, a, EPS, None, ALU.max))
            ch.link(g.tensor_scalar(nc_, nd, MAX_TANH, None, ALU.min))
            ch.link(g.tensor_scalar(a, nc_, 1.0, None, ALU.add))
            ch.link(g.tensor_scalar(b, nc_, -1.0, 1.0, ALU.mult, ALU.add))
            power(ch, c, b, DOWN, w)
            g.tensor_tensor(num(f"z{w}", w), a, c, ALU.mult).then_inc(done, 1)

        def to_norm(ch, w, m, var, k_out, km_out, done):
            g = nc.gpsimd
            a, b, c = num(f"a{w}", w), num(f"b{w}", w), num(f"c{w}", w)
            nc_, nd, lam, L = num(f"nc{w}", w), num(f"nd{w}", w), num(f"lam{w}", w), num(f"L{w}", w)
            n2, ser = num(f"n2{w}", w), num(f"ser{w}", w)
            power(ch, a, nd, DOWN, w)
            ch.link(g.tensor_tensor(b, L, a, ALU.mult))
            ch.link(g.tensor_scalar(lam, b, 0.5, None, ALU.mult))
            ch.link(g.tensor_tensor(n2, nc_, nc_, ALU.mult))
            ch.link(g.tensor_scalar(ser, n2, 1.0 / 9, 1.0 / 7, ALU.mult, ALU.add))
            for term in (1.0 / 5, 1.0 / 3, 1.0):
                ch.link(g.tensor_tensor(a, ser, n2, ALU.mult))
                ch.link(g.tensor_scalar(ser, a, term, None, ALU.add))
            ch.link(g.tensor_scalar(c, n2, SERIES_BELOW, None, ALU.is_lt))
            ch.link(g.tensor_tensor(a, ser, lam, ALU.subtract))
            ch.link(g.tensor_tensor(b, a, c, ALU.mult))
            ch.link(g.tensor_tensor(a, lam, b, ALU.add))
            ch.link(g.tensor_tensor(b, a, a, ALU.mult))
            ch.link(g.tensor_tensor(c, b, var, ALU.mult))
            ch.link(g.tensor_scalar(b, c, LN_EPS, None, ALU.add))
            power(ch, c, b, HALF_DOWN, w)
            ch.link(g.tensor_tensor(b, a, c, ALU.mult))
            ch.link(g.tensor_tensor(a, b, m, ALU.mult))
            ch.link(g.tensor_copy(k_out, b))
            g.tensor_scalar(km_out, a, -1.0, None, ALU.mult).then_inc(done, 1)

        def clip(ch, dst, nsq, w, a, b, done=None):
            g = nc.gpsimd
            ch.link(g.tensor_scalar(a, nsq, TINY, None, ALU.max))
            power(ch, b, a, HALF_DOWN, w)
            last = g.tensor_scalar(dst, b, REACH, 1.0, ALU.mult, ALU.min)
            if done is None:
                ch.link(last)
            else:
                last.then_inc(done, 1)

        block = ctx.enter_context(nc.Block())

        WLOADS = 8
        TILE_LINKS = 81

        @block.sync
        def _(sp):
            sp.dma_start(c0[:], cond).then_inc(s["ld_c"], 16)
            sp.dma_start(wada, w_ada.rearrange("(k p) n -> p k n", p=P)).then_inc(s["ld_c"], 16)
            sp.dma_start(badac[:], b_ada.rearrange("(c p) -> p c", p=P), allow_slow_non_contiguous=True).then_inc(s["ld_c"], 16)
            for b in range(B):
                sp.dma_start(xs[:].rearrange("p (j b) d -> p b j d", b=B)[:, b],
                             x[b].rearrange("(j p) d -> p j d", p=P)).then_inc(s["ld_x"], 16)
            for i, w in enumerate((w_q, w_k, w_v)):
                sp.dma_start(wqkv[:, :, i, :], w.rearrange("(k p) n -> p k n", p=P)).then_inc(s["ld_w"], 16)
            sp.dma_start(wo[:], w_o.rearrange("(k p) n -> p k n", p=P)).then_inc(s["ld_w"], 16)
            sp.dma_start(wf1[:], w_f1.rearrange("(k p) n -> p k n", p=P)).then_inc(s["ld_w"], 16)
            sp.dma_start(wf2[:], w_f2.rearrange("(k p) n -> p k n", p=P)).then_inc(s["ld_w"], 16)
            sp.dma_start(wx[:], w_x.rearrange("(k p) n -> p k n", p=P)).then_inc(s["ld_w"], 16)
            sp.dma_start(blc[:], b_l.rearrange("(c p) -> p c", p=P), allow_slow_non_contiguous=True).then_inc(s["ld_w"], 16)
            sp.sem_inc(s["o_free"], 1)
            with sp.Fori(0, NB) as j:
                for b in range(B):
                    sp.wait_ge(s["o_s"], B * j + b + 1)
                    sp.dma_start(out[b, bass.ds(j * P, P), :], ot[:, b * D:(b + 1) * D]).then_inc(s["o_d"], 16)
                sp.wait_ge(s["o_d"], 16 * B * (j + 1))
                sp.sem_inc(s["o_free"], 1)
            sp.wait_ge(s["o_d"], 16 * NT)

        @block.gpsimd
        def _(pool):
            g = nc.gpsimd
            g.memset(hs[:], 0.0).then_inc(s["l_hs"], 1)
            g.memset(ones[:], 1.0).then_inc(s["pchain"], 1)
            hold(pool, "pchain", 1)
            g.affine_select(out=ident[:], in_=ones[:], compare_op=ALU.is_equal, fill=0.0, base=0,
                            pattern=[[-1, P]], channel_multiplier=1).then_inc(s["pchain"], 1)
            hold(pool, "pchain", 2)
            g.tensor_copy(ident16[:], ident[:]).then_inc(s["consts"], 1)
            for i, e in enumerate((-0.5, 0.5, -1.0)):
                g.memset(cst[:, i, :], e).then_inc(s["pchain"], 1)
            hold(pool, "pchain", 5)
            ch = Chain(pool, s["pchain"], s["held"], 0)
            ch.base = 5
            hold(pool, "st1", 1)
            m16, v16 = mv[:, 0:NT, 0], mv[:, 0:NT, 1]
            to_ratio(ch, NT, m16, v16, xsq[:], s["ln1z"])
            hold(pool, "ln1z", 1)
            hold(pool, "lnr", 1)
            to_norm(ch, NT, m16, v16, kap[:], kmn[:], s["ln1"])

            ch = Chain(pool, s["hsc"], s["held"], 8)
            with pool.Fori(1, NT + 1) as n:
                ch.round(n)
                hold(pool, "p_ns", n)
                clip(ch, num("su"), num("nu"), 1, num("ca"), num("cb"), s["p_su"])
                hold(pool, "p_lin", n)
                g.tensor_tensor(tmp[:, 0:3 * D], lin[:].rearrange("p a d -> p (a d)"), lin[:].rearrange("p a d -> p (a d)"), ALU.mult).then_inc(s["p_sq"], 1)
                hold(pool, "p_ss", n)
                clip(ch, num("c3", 3), num("tot", 3), 3, num("cc3", 3), num("cd3", 3))
                ch.link(g.tensor_scalar(num("ct", 3), num("c3", 3), HEAD, None, ALU.mult))
                ch.link(g.tensor_scalar(num("nha", 48), num("ss", 48), TINY, None, ALU.max))
                power(ch, num("nhb", 48), num("nha", 48), HALF_DOWN, 48)
                g.tensor_scalar(num("nh", 48), num("nhb", 48), REACH, None, ALU.mult).then_inc(s["p_nh"], 1)
                ch.full()

            def square_of_gated(n, b, which, res, ga):
                g.tensor_tensor(qk[:, 1], qk[:, 0], gates[:, which, bass.ds(b, 1), :].rearrange("p o d -> p (o d)"),
                                ALU.mult).then_inc(s[ga], 1)

            def mobius(ch, n, nsq_x, n1, n2, th, ar, sums, ab):
                for q in sums:
                    hold(pool, q, n)
                clip(ch, num("s1"), num("n1"), 1, num("ca"), num("cb"))
                ch.link(g.tensor_scalar(num("ca"), num("n2"), TINY, None, ALU.max))
                power(ch, num("n2i"), num("ca"), HALF_DOWN, 1)
                ch.link(g.tensor_tensor(num("cb"), num("ca"), num("n2i"), ALU.mult))
                g.tensor_tensor(num("ar"), num("cb"), num("s1"), ALU.mult).then_inc(s[ar], 1)
                hold(pool, th, n)
                ch.link(g.tensor_tensor(num("fac"), num("th"), num("n2i"), ALU.mult))
                ch.link(g.tensor_tensor(num("y2"), num("th"), num("th"), ALU.mult))
                ch.link(g.tensor_tensor(num("xy"), num("fac"), num("xa"), ALU.mult))
                ch.link(g.tensor_scalar(num("cc"), num("xy"), 2.0, 1.0, ALU.mult, ALU.add))
                ch.link(g.tensor_tensor(num("cd"), num("cc"), num("y2"), ALU.add))
                ch.link(g.tensor_tensor(num("ca"), nsq_x, num("y2"), ALU.mult))
                ch.link(g.tensor_tensor(num("cb"), num("ca"), num("cc"), ALU.add))
                ch.link(g.tensor_scalar(num("ca"), num("cb"), EPS, None, ALU.max))
                power(ch, num("den"), num("ca"), DOWN, 1)
                ch.link(g.tensor_tensor(num("al"), num("cd"), num("den"), ALU.mult))
                ch.link(g.tensor_scalar(num("cb"), nsq_x, -1.0, 1.0, ALU.mult, ALU.add))
                ch.link(g.tensor_tensor(num("cc"), num("cb"), num("fac"), ALU.mult))
                g.tensor_tensor(num("be"), num("cc"), num("den"), ALU.mult).then_inc(s[ab], 1)

            hold(pool, "p_hk", NT)
            hold(pool, "p_kc", NT + 1)
            ch = Chain(pool, s["achain"], s["held"], TILE_LINKS)
            with pool.Fori(0, NB) as j:
                with pool.Fori(0, B) as b:
                    k = j * B + b
                    n = k + 1
                    ch.round(n)
                    hold(pool, "t_done", n)
                    for dup in range(2):
                        last = g.tensor_copy(stack[:, :, dup, :], qhl[:, bass.ds(k, 1), :, :].rearrange("p o h e -> p (o h) e"))
                    last.then_inc(s["t_q"], 1)
                    hold(pool, "t_o", n)
                    g.tensor_tensor(xn[:], qk[:, 0], qk[:, 0], ALU.mult).then_inc(s["t_sq"], 1)
                    hold(pool, "t_ss", n)
                    clip(ch, num("fh", H), num("ssh", H), H, num("ha", H), num("hb", H))
                    ch.link(g.tensor_scalar(num("fr", H), num("fh", H), 1.0 / HEAD, None, ALU.mult))
                    ch.link(g.tensor_tensor(num("ha", H), num("fr", H), num("fr", H), ALU.mult))
                    g.tensor_tensor(num("hc", H), num("ha", H), num("ssh", H), ALU.mult).then_inc(s["t_f"], 1)
                    g.tensor_tensor(qk[:, 1].rearrange("p (h e) -> p h e", e=HD), qk[:, 0].rearrange("p (h e) -> p h e", e=HD),
                                    num("fr", H).unsqueeze(2).to_broadcast([P, H, HD]), ALU.mult).then_inc(s["t_op"], 1)
                    hold(pool, "t_tot", n)
                    clip(ch, num("so"), num("no"), 1, num("ca"), num("cb"), s["t_so"])
                    hold(pool, "t_a", n)
                    square_of_gated(n, b, 0, None, "t_ga")
                    ch.link(g.tensor_copy(num("xsq1"), xsq[:, bass.ds(k, 1)]))
                    mobius(ch, n, num("xsq1"), "t_n1", "t_n2", "t_th", "t_ar", ("t_n1", "t_n2", "t_xa"), "t_ab")
                    hold(pool, "t_st", n)
                    to_ratio(ch, 1, mv[:, NT, 0:1], mv[:, NT, 1:2], num("x2sq"), s["t_z"])
                    hold(pool, "t_z", n)
                    hold(pool, "t_L", n)
                    to_norm(ch, 1, mv[:, NT, 0:1], mv[:, NT, 1:2], num("kap"), num("kmn"), s["t_km"])
                    hold(pool, "t_km", n)
                    hold(pool, "t_ns", n)
                    clip(ch, num("su"), num("nu"), 1, num("ca"), num("cb"), s["t_fs"])
                    hold(pool, "t_sqf", 2 * n)
                    ch.link(g.tensor_tensor(num("nf"), num("nf0"), num("nf1"), ALU.add))
                    clip(ch, num("sf"), num("nf"), 1, num("ca"), num("cb"), s["t_sf"])
                    hold(pool, "t_a2", n)
                    square_of_gated(n, b, 1, None, "t_ga2")
                    mobius(ch, n, num("x2sq"), "t_n3", "t_n4", "t_th2", "t_ar2", ("t_n3", "t_n4", "t_xa2"), "t_ab2")
                    hold(pool, "t_X", n)
                    xk = xs[:, bass.ds(k, 1), :].rearrange("p o d -> p (o d)")
                    ch.link(g.tensor_tensor(xn[:], xk, x3[:], ALU.add))
                    g.tensor_copy(xk, xn[:]).then_inc(s["t_XX"], 1)
                    hold(pool, "t_XX", n)
                ch.full()
                with pool.Fori(0, P) as i:
                    m = j * P + i + 1
                    hold(pool, "l_h32", m)
                    g.tensor_copy(hs[:, :, :, bass.ds(i, 1)], h32[:].rearrange("p (k b o) -> p k b o", b=B, o=1)).then_inc(s["l_hs"], 1)

        def gate_cols(bk, g0, n):
            return bk[:, g0 * 12:(g0 + n) * 12].rearrange("p (g b e) -> p g b e", b=B, e=3)

        CHUNK = (6, 7, 0, 1, 2, 3, 4, 5)
        UNIT = (1.0, 1.0) + (0.5,) * 6
        GATES = ((pA, 0, 4, "l_gA", "l_A"), (pF, 4, 2, "l_gF", "l_F"), (pO, 6, 2, "l_gO", "l_O"))

        @block.tensor
        def _(pe):
            mm, tr = nc.tensor.matmul, nc.tensor.transpose
            pe.wait_ge(s["consts"], 1)
            pe.wait_ge(s["ld_c"], 16 * 3)
            for c in range(KD):
                last = tr(bank[0][:, c * B:(c + 1) * B], c0[:, c * P:(c + 1) * P], ident[0:B, 0:B])
            last.then_inc(s["c0t"], 1)
            pe.wait_ge(s["c0t_s"], 2)
            for c in range(6 * KD):
                for kc in range(KD):
                    last = mm(bank[1][:, c * B:(c + 1) * B], wada[:, kc, c * P:(c + 1) * P], c0T[:, kc, :],
                              start=kc == 0, stop=kc == KD - 1)
            last.then_inc(s["adap"], 1)
            for which in range(2):
                for b in range(B):
                    for kc in range(KD):
                        at_ = (which * 3 + 2) * D
                        last = mm(bank[2 + 2 * which + b // 2][:, (b % 2) * D:(b % 2 + 1) * D], c0B[:, kc, b, :],
                                  wada[:, kc, at_:at_ + D], start=kc == 0, stop=kc == KD - 1, skip_group_check=True)
            last.then_inc(s["gp"], 1)
            pe.wait_ge(s["pk"], 1)
            tr(bank[6][0:1, 0:P], big1[:, 2:3], ident[:]).then_inc(s["wmax"], 1)
            pe.wait_ge(s["pk"], 2)
            mm(bank[6][:, 256:257], ones[0:1, :], big1[0:1, 4:5], start=True, stop=True).then_inc(s["wmax"], 1)
            pe.wait_ge(s["ld_h"], 16)
            for gi, c in enumerate(CHUNK):
                for kc in range(KD):
                    last = mm(bank[0][:, 64 + gi * B:64 + (gi + 1) * B], wh[:, kc, c * P:(c + 1) * P], c0T[:, kc, :],
                              start=kc == 0, stop=kc == KD - 1, skip_group_check=True)
            last.then_inc(s["h0p"], 1)

            pe.wait_ge(s["gp_s"], 1)
            pe.wait_ge(s["ld_w"], 16 * WLOADS)
            with pe.Fori(1, NT + 1) as n:
                pe.wait_ge(s["p_xn"], n)
                for c in range(KD):
                    last = tr(bank[0][:, c * P:(c + 1) * P], xn[:, c * P:(c + 1) * P], ident[:])
                last.then_inc(s["p_xT"], 1)
                pe.wait_ge(s["p_uT"], n)
                for i in range(3):
                    for kc in range(KD):
                        last = mm(bank[2 + i][:, 0:D], uT[:, kc, :], wqkv[:, kc, i, :], start=kc == 0, stop=kc == KD - 1)
                last.then_inc(s["p_mm"], 1)
                pe.wait_ge(s["p_usq"], n)
                for c in range(KD):
                    last = mm(bank[1][:, 0:1], usq[:, c, :], ones[:, 0:1], start=c == 0, stop=c == KD - 1)
                last.then_inc(s["p_n"], 1)
                pe.wait_ge(s["p_hk"], n)
                for hp in range(HP):
                    last = tr(half_words(5)[:, hp * P:(hp + 1) * P],
                              stack[:, 2 * hp:2 * hp + 2, :, :].rearrange("p h a e -> p (h a e)"), ident16[:])
                last.then_inc(s["p_kT"], 1)

            pe.wait_ge(s["p_kc"], NT + 1)
            pe.wait_ge(s["p_hk"], NT)
            pe.wait_ge(s["l_init"], 2)
            pe.wait_ge(s["w16"], 1)
            with pe.Fori(0, NB) as j:
                with pe.Fori(0, B) as b:
                    n = j * B + b + 1
                    pe.wait_ge(s["t_q"], n)
                    for hp in range(HP):
                        last = tr(half_words(3)[:, hp * P:(hp + 1) * P],
                                  stack[:, 2 * hp:2 * hp + 2, :, :].rearrange("p h a e -> p (h a e)"), ident16[:])
                    last.then_inc(s["t_qT"], 1)
                    pe.wait_ge(s["t_qc"], 2 * n)
                    for hp in range(HP + 1):
                        if hp < HP:
                            if hp > 0:
                                pe.wait_ge(s["t_E"], HP * (n - 1) + hp)
                            for kc in range(NB):
                                last = mm(bank[kc // 2][:, (kc % 2) * 2 * P:(kc % 2 + 1) * 2 * P],
                                          kT[:, bass.ds(b, 1), hp, kc * P:(kc + 1) * P].rearrange("p o t -> p (o t)"),
                                          qbd[:, hp, :], start=True, stop=True, skip_group_check=True)
                            last.then_inc(s["t_S"], 1)
                        if hp > 0:
                            pe.wait_ge(s["t_E"], HP * (n - 1) + hp)
                            for e in range(2):
                                h = 2 * (hp - 1) + e
                                for kc in range(NB):
                                    last = mm(bank[2][:, h * (HD + 1):(h + 1) * (HD + 1)],
                                              big[:, (hp - 1) % 2, kc, e * P:(e + 1) * P],
                                              vs[:, bass.ds(b, 1), kc, h, :].rearrange("p o e -> p (o e)"),
                                              start=kc == 0, stop=kc == NB - 1, skip_group_check=True)
                            last.then_inc(s["t_AV"], 1)
                    pe.wait_ge(s["t_op"], n)
                    for c in range(KD):
                        last = tr(bank[4][:, c * P:(c + 1) * P], qk[:, 1, c * P:(c + 1) * P], ident[:])
                    last.then_inc(s["t_oT"], 1)
                    pe.wait_ge(s["t_oc"], n)
                    for kc in range(KD):
                        last = mm(bank[3][:, 0:D], uT[:, kc, :], wo[:, kc, :], start=kc == 0, stop=kc == KD - 1)
                    last.then_inc(s["t_mo"], 1)
                    pe.wait_ge(s["t_xn"], n)
                    for c in range(KD):
                        last = tr(bank[4][:, c * P:(c + 1) * P], xn[:, c * P:(c + 1) * P], ident[:])
                    last.then_inc(s["t_xT"], 1)
                    pe.wait_ge(s["t_us"], n)
                    for c in range(KD):
                        last = mm(bank[2][:, 0:1], usq[:, c, :], ones[:, 0:1], start=c == 0, stop=c == KD - 1)
                    last.then_inc(s["t_nm"], 1)
                    for half in range(2):
                        for kc in range(KD):
                            last = mm(bank[3 + half][:, :], uT[:, kc, :], wf1[:, kc, half * 512:(half + 1) * 512],
                                      start=kc == 0, stop=kc == KD - 1)
                        last.then_inc(s["t_m1"], 1)
                    for half in range(2):
                        pe.wait_ge(s["t_f1"], 2 * n - 1 + half)
                        for c in range(KF // 2):
                            cc = half * (KF // 2) + c
                            last = tr(bank[half][:, c * P:(c + 1) * P], tmp[:, cc * P:(cc + 1) * P], ident[:])
                        last.then_inc(s["t_fT"], 1)
                    pe.wait_ge(s["t_fc"], 2 * n)
                    for kc in range(KF):
                        last = mm(bank[3][:, 0:D], fT[:, kc, :], wf2[:, kc, :], start=kc == 0, stop=kc == KF - 1)
                    last.then_inc(s["t_m2"], 1)
                    pe.wait_ge(s["t_XX"], n)
                    for c in range(KD):
                        last = tr(bank[4][:, c * P:(c + 1) * P], xn[:, c * P:(c + 1) * P], ident[:])
                    last.then_inc(s["t_XT"], 1)
                    pe.wait_ge(s["t_Xc"], n)
                    for half in range(2):
                        for gi in range(GC // 2):
                            c = CHUNK[half * (GC // 2) + gi]
                            for kc in range(KD):
                                last = mm(bank[half][:, gi * P:(gi + 1) * P], wx[:, kc, c * P:(c + 1) * P], uT[:, kc, :],
                                          start=kc == 0, stop=kc == KD - 1, skip_group_check=True)
                        last.then_inc(s["t_xw"], 1)
                hold(pe, "l_x0", j + 1)
                with pe.Fori(0, P) as i:
                    m = j * P + i + 1
                    for bk, g0, ng, read, made in GATES:
                        pe.wait_ge(s[read], m)
                        mm(gate_cols(bk, 0, ng)[:, :, :, 2], ident[:],
                           xw[:, bass.ds(i, 1), g0:g0 + ng, :].rearrange("p o g b -> p (o g) b"), start=True, stop=False, skip_group_check=True)
                    pe.wait_ge(s["l_lo"], m)
                    for bk, g0, ng, read, made in GATES:
                        for gi in range(ng):
                            for kc in range(KD):
                                for half in range(2):
                                    last = mm(gate_cols(bk, gi, 1)[:, 0, :, 0:2],
                                              wh16[:, half, kc, (g0 + gi) * P:(g0 + gi + 1) * P],
                                              h16[:, kc, :, :], start=False, stop=gi == ng - 1 and kc == KD - 1 and half == 1,
                                              skip_group_check=True)
                        last.then_inc(s[made], 1)
                pe.wait_ge(s["l_hs"], P * (j + 1) + 1)
                for b in range(B):
                    for kc in range(KD):
                        last = tr(bank[b][:, kc * P:(kc + 1) * P], hs[:, kc, b, :], ident[:])
                    last.then_inc(s["o_T"], 1)
                pe.wait_ge(s["o_s"], B * (j + 1))

        @block.scalar
        def _(act):
            A = nc.scalar.activation
            act.dma_start(wh, w_h.rearrange("(k p) n -> p k n", p=P)).then_inc(s["ld_h"], 16)
            for i, bias in enumerate((b_q, b_k, b_v)):
                act.dma_start(bqkv[:, i, :], bias.partition_broadcast(P)).then_inc(s["ld_b"], 16)
            act.dma_start(bo[:], b_o.partition_broadcast(P)).then_inc(s["ld_b"], 16)
            act.dma_start(bf1[:], b_f1.partition_broadcast(P)).then_inc(s["ld_b"], 16)
            act.dma_start(bf2[:], b_f2.partition_broadcast(P)).then_inc(s["ld_b"], 16)
            for which in range(2):
                at_ = (which * 3 + 2) * D
                for b in range(B):
                    act.dma_start(gates[:, which, b, :], b_ada[at_:at_ + D].partition_broadcast(P)).then_inc(s["ld_b"], 16)
            act.wait_ge(s["ln1z"], 1)
            A(num(f"L{NT}", NT), num(f"z{NT}", NT), ACT.Ln).then_inc(s["lnr"], 1)
            act.wait_ge(s["ada_s"], 1)
            act.sem_inc(s["p_kc"], 1)
            act.sem_inc(s["t_done"], 1)
            with act.Fori(0, B) as b:
                with act.Fori(0, NB) as j:
                    n = b * NB + j + 1
                    act.wait_ge(s["p_xT"], n)
                    for c in range(KD):
                        last = A(uT[:, c, :], bank[0][:, c * P:(c + 1) * P], ACT.Identity,
                                 scale=adac[:, KD + c, bass.ds(b, 1)], bias=adac[:, c, bass.ds(b, 1)])
                    last.then_inc(s["p_uT"], 1)
                    act.wait_ge(s["p_uT"], n)
                    A(usq[:, :, :], uT[:, :, :], ACT.Square).then_inc(s["p_usq"], 1)
                    act.wait_ge(s["p_kT"], n)
                    A(kT[:, bass.ds(b, 1), :, bass.ds(j * P, P)].rearrange("p o h t -> p (o h) t"),
                      half_words(5)[:, 0:HP * P].rearrange("p (h t) -> p h t", h=HP), ACT.Copy).then_inc(s["p_kc"], 1)

            act.wait_ge(s["l_init"], 2)
            with act.Fori(0, NB) as j:
                with act.Fori(0, B) as b:
                    n = j * B + b + 1
                    act.wait_ge(s["t_qT"], n)
                    for e in range(2):
                        r = slice(64 * e, 64 * e + 64)
                        A(qbd[r, :, e * P:(e + 1) * P], half_words(3)[r, 0:HP * P].rearrange("p (h t) -> p h t", h=HP),
                          ACT.Copy).then_inc(s["t_qc"], 1)
                    for hp in range(HP):
                        act.wait_ge(s["t_S"], HP * (n - 1) + hp + 1)
                        if hp >= 2:
                            act.wait_ge(s["t_AV"], HP * (n - 1) + hp - 1)
                        for half in range(2):
                            last = A(big[:, hp % 2, 2 * half:2 * half + 2, :].rearrange("p a b -> p (a b)"), bank[half][:, :],
                                     ACT.Exp, scale=1.0 / (math.sqrt(HD) * QK_UP * QK_UP))
                        last.then_inc(s["t_E"], 1)
                    act.wait_ge(s["t_oT"], n)
                    A(uT[:].rearrange("p c t -> p (c t)"), bank[4][:, 0:D], ACT.Copy).then_inc(s["t_oc"], 1)
                    act.wait_ge(s["t_a"], n)
                    A(lin[:, 0], qk[:, 0], ACT.Square, accum_out=num("n1")).then_inc(s["t_n1"], 1)
                    act.wait_ge(s["t_ga"], n)
                    A(lin[:, 1], qk[:, 1], ACT.Square, accum_out=num("n2")).then_inc(s["t_n2"], 1)
                    act.wait_ge(s["t_ar"], n)
                    A(num("th"), num("ar"), ACT.Tanh).then_inc(s["t_th"], 1)
                    act.wait_ge(s["t_z"], n)
                    A(num("L1"), num("z1"), ACT.Ln).then_inc(s["t_L"], 1)
                    act.wait_ge(s["t_xT"], n)
                    for c in range(KD):
                        last = A(uT[:, c, :], bank[4][:, c * P:(c + 1) * P], ACT.Identity,
                                 scale=adac[:, 4 * KD + c, bass.ds(b, 1)], bias=adac[:, 3 * KD + c, bass.ds(b, 1)])
                    last.then_inc(s["t_uT"], 1)
                    act.wait_ge(s["t_uT"], n)
                    A(usq[:, :, :], uT[:, :, :], ACT.Square).then_inc(s["t_us"], 1)
                    for half in range(2):
                        act.wait_ge(s["t_f1"], 2 * n - 1 + half)
                        last = A(lin[:].rearrange("p a d -> p (a d)")[:, 0:512], tmp[:, half * 512:(half + 1) * 512], ACT.Square,
                                 accum_out=num(f"nf{half}"))
                        last.then_inc(s["t_sqf"], 1)
                        act.wait_ge(s["t_sqf"], 2 * n - 1 + half)
                    for half in range(2):
                        act.wait_ge(s["t_fT"], 2 * n - 1 + half)
                        A(fT[:, half * (KF // 2):(half + 1) * (KF // 2), :].rearrange("p c t -> p (c t)"), bank[half][:, :],
                          ACT.Copy).then_inc(s["t_fc"], 1)
                    act.wait_ge(s["t_a2"], n)
                    A(lin[:, 0], qk[:, 0], ACT.Square, accum_out=num("n1")).then_inc(s["t_n3"], 1)
                    act.wait_ge(s["t_ga2"], n)
                    A(lin[:, 1], qk[:, 1], ACT.Square, accum_out=num("n2")).then_inc(s["t_n4"], 1)
                    act.wait_ge(s["t_ar2"], n)
                    A(num("th"), num("ar"), ACT.Tanh).then_inc(s["t_th2"], 1)
                    act.wait_ge(s["t_XT"], n)
                    A(uT[:].rearrange("p c t -> p (c t)"), bank[4][:, 0:D], ACT.Copy).then_inc(s["t_Xc"], 1)
                    for half in range(2):
                        act.wait_ge(s["t_xw"], 2 * n - 1 + half)
                        for gi in range(GC // 2):
                            gg = half * (GC // 2) + gi
                            last = A(xw[:, :, gg, bass.ds(b, 1)].rearrange("p t o -> p (t o)"), bank[half][:, gi * P:(gi + 1) * P],
                                     ACT.Identity, scale=UNIT[gg], bias=blc2[:, gg:gg + 1])
                    last.then_inc(s["t_done"], 1)
                nc.scalar.preload_act_table_set("exp_and_others")
                with act.Fori(0, P) as i:
                    m = j * P + i + 1
                    act.wait_ge(s["l_gA"], m + 1)
                    A(tA[:], gA[:].rearrange("p (c e) -> p e c", e=3)[:, 2], ACT.Tanh).then_inc(s["l_tA"], 1)
                    act.wait_ge(s["l_gF"], m + 1)
                    A(cmul[:, :, 1], gF[:].rearrange("p (c e) -> p e c", e=3)[:, 2], ACT.Tanh).then_inc(s["l_tF"], 1)
                    act.wait_ge(s["l_gO"], m + 1)
                    A(tO[:], gO[:].rearrange("p (c e) -> p e c", e=3)[:, 2], ACT.Tanh).then_inc(s["l_tO"], 1)
                    act.wait_ge(s["l_c"], m)
                    A(tC[:], cnew[:, :, 3], ACT.Tanh).then_inc(s["l_tC"], 1)

        @block.vector
        def _(v):
            d = nc.vector
            d.memset(qbd[:], 0.0).then_inc(s["l_init"], 1)
            d.memset(vs[:, :, :, :, HD:HD + 1], 1.0).then_inc(s["l_init"], 1)
            d.memset(h16[:], 0.0).then_inc(s["l_lo"], 1)
            d.memset(gA[:], 0.0).then_inc(s["l_gA"], 1)
            d.memset(gF[:], 0.0).then_inc(s["l_gF"], 1)
            d.memset(gO[:], 0.0).then_inc(s["l_gO"], 1)
            d.memset(coef[:, :, 0], 0.0).then_inc(s["dinit"], 1)
            d.memset(coef[:, :, 1], 1.0).then_inc(s["dinit"], 1)
            d.memset(cmul[:, :, 0], 0.0).then_inc(s["dinit"], 1)
            d.memset(cmul[:, :, 2], 1.0).then_inc(s["dinit"], 1)
            d.memset(cmul[:, :, 3], 0.5).then_inc(s["dinit"], 1)
            d.memset(cadd[:], 0.0).then_inc(s["dinit"], 1)
            v.wait_ge(s["ld_x"], 16 * B)
            for k in range(NT):
                d.bn_stats(mv6[:], xs[:, k, :]).then_inc(s["vchain"], 1)
                v.wait_ge(s["vchain"], 2 * k + 1)
                d.bn_aggr(mv[:, k, :], mv6[:]).then_inc(s["vchain"], 1)
                v.wait_ge(s["vchain"], 2 * k + 2)
            d.memset(num("one"), 1.0).then_inc(s["st1"], 1)
            nv = 2 * NT

            def link(ins):
                nonlocal nv
                nv += 1
                ins.then_inc(s["vchain"], 1)
                v.wait_ge(s["vchain"], nv)

            v.wait_ge(s["c0t"], 1)
            d.tensor_copy(c0T[:], bank[0][:, 0:KD * B].rearrange("p (k b) -> p k b", b=B)).then_inc(s["c0t_s"], 1)
            v.wait_ge(s["c0t_s"], 1)
            d.tensor_copy(c0B[:], c0T[:].unsqueeze(3).to_broadcast([P, KD, B, P])).then_inc(s["c0t_s"], 1)
            v.wait_ge(s["adap"], 1)
            link(d.tensor_tensor(adac[:], bank[1][:, 0:6 * KD * B].rearrange("p (c b) -> p c b", b=B),
                                 badac[:].unsqueeze(2).to_broadcast([P, 6 * KD, B]), ALU.add))
            for c in (KD, 4 * KD):
                link(d.tensor_scalar(adac[:, c:c + KD, :], adac[:, c:c + KD, :], 1.0, None, ALU.add))
            d.tensor_scalar(num("two"), num("one"), 2.0, None, ALU.mult).then_inc(s["ada_s"], 1)
            v.wait_ge(s["gp"], 1)
            v.wait_ge(s["ld_b"], 16 * 14)
            for which in range(2):
                for b in range(B):
                    last = d.tensor_tensor(gates[:, which, b, :], bank[2 + 2 * which + b // 2][:, (b % 2) * D:(b % 2 + 1) * D],
                                           gates[:, which, b, :], ALU.add)
            last.then_inc(s["gp_s"], 1)
            v.wait_ge(s["ld_h"], 16)
            link(d.tensor_reduce(big1[:, 0:1], wh, axis=AX.XY, op=ALU.max))
            link(d.tensor_reduce(big1[:, 1:2], wh, axis=AX.XY, op=ALU.min))
            link(d.tensor_scalar(big1[:, 3:4], big1[:, 1:2], -1.0, 2.0 ** -100, ALU.mult, ALU.max))
            d.tensor_tensor(big1[:, 2:3], big1[:, 0:1], big1[:, 3:4], ALU.max).then_inc(s["pk"], 1)
            v.wait_ge(s["wmax"], 1)
            link(d.tensor_reduce(big1[0:1, 5:6], bank[6][0:1, 0:P], axis=AX.X, op=ALU.max))
            d.tensor_scalar(big1[0:1, 4:5].bitcast(I32), big1[0:1, 5:6].bitcast(I32), 0x7F800000, None, ALU.bitwise_and).then_inc(s["pk"], 1)
            v.wait_ge(s["wmax"], 2)
            link(d.tensor_copy(big1[:, 6:7], bank[6][:, 256:257]))
            link(d.reciprocal(big1[:, 7:8], big1[:, 6:7]))
            v.wait_ge(s["dinit"], 6)
            v.wait_ge(s["ld_w"], 16 * WLOADS)
            link(d.tensor_scalar(coef[:, :, 2], coef[:, :, 1], big1[:, 6:7], 1.0 / (H_UP * 2.0 ** 14), ALU.mult, ALU.mult))
            link(d.tensor_scalar(big1[:, 6:7], big1[:, 7:8], 2.0 ** 14, None, ALU.mult))
            for g0 in range(GC):
                c = CHUNK[g0]
                src, w = wh[:, :, c * P:(c + 1) * P], tmp[:, 0:KD * P].rearrange("p (k n) -> p k n", k=KD)
                hi, lo = (wh16[:, half, :, g0 * P:(g0 + 1) * P] for half in range(2))
                link(d.tensor_scalar(w, src, big1[:, 6:7], UNIT[g0], ALU.mult, ALU.mult))
                link(d.tensor_copy(hi, w))
                link(d.tensor_tensor(lo, w, hi, ALU.subtract))
            v.wait_ge(s["h0p"], 1)
            for g0 in range(GC):
                link(d.tensor_scalar(h0c[:, g0, :], bank[0][:, 64 + g0 * B:64 + (g0 + 1) * B], UNIT[g0], None, ALU.mult))
                link(d.tensor_scalar(blc2[:, g0:g0 + 1], blc[:, CHUNK[g0]:CHUNK[g0] + 1], UNIT[g0], None, ALU.mult))
            d.tensor_copy(num("two"), num("one")).then_inc(s["w16"], 1)

            v.wait_ge(s["ln1"], 1)
            v.wait_ge(s["gp_s"], 1)
            with v.Fori(0, B) as b:
                with v.Fori(0, NB) as j:
                    n = b * NB + j + 1
                    k = j * B + b
                    v.wait_ge(s["p_kc"], n)
                    d.tensor_scalar(xn[:], xs[:, bass.ds(k, 1), :].rearrange("p o d -> p (o d)"), kap[:, bass.ds(k, 1)],
                                    kmn[:, bass.ds(k, 1)], ALU.mult, ALU.add).then_inc(s["p_xn"], 1)
                    v.wait_ge(s["p_n"], n)
                    d.tensor_copy(num("nu"), bank[1][:, 0:1]).then_inc(s["p_ns"], 1)
                    v.wait_ge(s["p_mm"], n)
                    v.wait_ge(s["p_su"], n)
                    for i in range(3):
                        last = d.scalar_tensor_tensor(lin[:, i, :], bank[2 + i][:, 0:D], num("su"), bqkv[:, i, :], ALU.mult, ALU.add)
                    last.then_inc(s["p_lin"], 1)
                    v.wait_ge(s["p_sq"], n)
                    d.tensor_reduce(num("ss", 48), tmp[:, 0:3 * D].rearrange("p (h e) -> p h e", e=HD), axis=AX.X, op=ALU.add).then_inc(s["p_s1"], 1)
                    v.wait_ge(s["p_s1"], n)
                    d.tensor_reduce(num("tot", 3), num("ss", 48).rearrange("p (a h) -> p a h", a=3), axis=AX.X, op=ALU.add).then_inc(s["p_ss"], 1)
                    v.wait_ge(s["p_nh"], n)
                    for i in range(3):
                        last = d.tensor_scalar(num("f", 48)[:, i * H:(i + 1) * H], num("nh", 48)[:, i * H:(i + 1) * H],
                                               num("ct", 3)[:, i:i + 1], None, ALU.min)
                    last.then_inc(s["p_f"], 1)
                    v.wait_ge(s["p_f"], n)
                    fb = lambda i: num("f", 48)[:, i * H:(i + 1) * H].unsqueeze(2).to_broadcast([P, H, HD])
                    l3 = lambda i: lin[:, i, :].rearrange("p (h e) -> p h e", e=HD)
                    d.tensor_tensor(vs[:, bass.ds(b, 1), bass.ds(j, 1), :, 0:HD].rearrange("p o r h e -> p (o r h) e"), l3(2), fb(2),
                                    ALU.mult).then_inc(s["p_v"], 1)
                    for i in range(2):
                        last = d.scalar_tensor_tensor(qk[:, i, :].rearrange("p (h e) -> p h e", e=HD), l3(i), QK_UP, fb(i), ALU.mult, ALU.mult)
                    last.then_inc(s["p_qk"], 1)
                    v.wait_ge(s["p_qk"], n)
                    q3, k3 = (qk[:, i, :].rearrange("p (h e) -> p h e", e=HD) for i in range(2))
                    qh, ql = (qhl[:, bass.ds(k, 1), :, i * HD:(i + 1) * HD].rearrange("p o h e -> p (o h) e") for i in range(2))
                    kh, kl = stack[:, :, 0, :], stack[:, :, 1, :]
                    d.tensor_copy(qh, q3)
                    for dup in range(2):
                        last = d.tensor_copy(kh[:, :, dup * HD:(dup + 1) * HD], k3)
                    last.then_inc(s["p_h"], 1)
                    v.wait_ge(s["p_h"], n)
                    d.tensor_tensor(ql, q3, qh, ALU.subtract)
                    for dup in range(2):
                        last = d.tensor_tensor(kl[:, :, dup * HD:(dup + 1) * HD], k3, kh[:, :, dup * HD:(dup + 1) * HD], ALU.subtract)
                    last.then_inc(s["p_hk"], 1)

            with v.Fori(0, NB) as j:
                with v.Fori(0, B) as b:
                    k = j * B + b
                    n = k + 1
                    o3 = bank[2][:, 0:H * (HD + 1)].rearrange("p (h e) -> p h e", e=HD + 1)
                    qk3 = qk[:, 0].rearrange("p (h e) -> p h e", e=HD)
                    v.wait_ge(s["t_AV"], HP * n)
                    d.reciprocal(num("rd", H), o3[:, :, HD]).then_inc(s["t_r"], 1)
                    v.wait_ge(s["t_r"], n)
                    d.tensor_tensor(qk3, o3[:, :, 0:HD], num("rd", H).unsqueeze(2).to_broadcast([P, H, HD]), ALU.mult).then_inc(s["t_o"], 1)
                    v.wait_ge(s["t_sq"], n)
                    d.tensor_reduce(num("ssh", H), xn[:].rearrange("p (h e) -> p h e", e=HD), axis=AX.X, op=ALU.add).then_inc(s["t_ss"], 1)
                    v.wait_ge(s["t_f"], n)
                    d.tensor_reduce(num("no"), num("hc", H), axis=AX.X, op=ALU.add).then_inc(s["t_tot"], 1)
                    xk = xs[:, bass.ds(k, 1), :].rearrange("p o d -> p (o d)")

                    def update(made, scale_ready, scale, bias, bk, a_made, ga_made, res, xa_made, ab, w, w_made, out_made):
                        v.wait_ge(s[made], n)
                        v.wait_ge(s[scale_ready], n)
                        d.scalar_tensor_tensor(qk[:, 0], bk[:, 0:D], scale, bias, ALU.mult, ALU.add).then_inc(s[a_made], 1)
                        v.wait_ge(s[ga_made], n)
                        d.scalar_tensor_tensor(lin[:, 2], res, 1.0, qk[:, 1], ALU.mult, ALU.mult,
                                               accum_out=num("xa")).then_inc(s[xa_made], 1)
                        v.wait_ge(s[ab], n)
                        v.wait_ge(s[xa_made], n)
                        d.tensor_scalar(lin[:, 2], res, num("al"), None, ALU.mult).then_inc(s[w_made], 1)
                        v.wait_ge(s[w_made], n)
                        d.scalar_tensor_tensor(w, qk[:, 1], num("be"), lin[:, 2], ALU.mult, ALU.add).then_inc(s[out_made], 1)

                    update("t_mo", "t_so", num("so"), bo[:], bank[3], "t_a", "t_ga", xk, "t_xa", "t_ab", x2[:], "t_w1", "t_x2")
                    v.wait_ge(s["t_x2"], n)
                    d.bn_stats(mv6[:], x2[:]).then_inc(s["t_s6"], 1)
                    hold(v, "t_s6", n)
                    d.bn_aggr(mv[:, NT, :], mv6[:]).then_inc(s["t_st"], 1)
                    v.wait_ge(s["t_km"], n)
                    d.tensor_scalar(xn[:], x2[:], num("kap"), num("kmn"), ALU.mult, ALU.add).then_inc(s["t_xn"], 1)
                    v.wait_ge(s["t_nm"], n)
                    d.tensor_copy(num("nu"), bank[2][:, 0:1]).then_inc(s["t_ns"], 1)
                    v.wait_ge(s["t_fs"], n)
                    for half in range(2):
                        v.wait_ge(s["t_m1"], 2 * n - 1 + half)
                        d.scalar_tensor_tensor(tmp[:, half * 512:(half + 1) * 512], bank[3 + half][:, :], num("su"),
                                               bf1[:, half * 512:(half + 1) * 512], ALU.mult, ALU.add).then_inc(s["t_f1"], 1)
                    update("t_m2", "t_sf", num("sf"), bf2[:], bank[3], "t_a2", "t_ga2", x2[:], "t_xa2", "t_ab2", x3[:], "t_w2", "t_X")
                v.wait_ge(s["t_done"], B * (j + 1) + 1)
                d.tensor_tensor(xw[:, 0], xw[:, 0], h0c[:], ALU.add).then_inc(s["l_x0"], 1)
                v.wait_ge(s["l_x0"], j + 1)
                d.memset(h0c[:], 0.0).then_inc(s["l_h0"], 1)
                with v.Fori(0, P) as i:
                    m = j * P + i + 1
                    v.wait_ge(s["l_A"], m)
                    d.tensor_tensor_scan(gA[:], coef[:].rearrange("p c e -> p (c e)"), pA[:, 0:48], 0.0, ALU.mult, ALU.add).then_inc(s["l_gA"], 1)
                    v.wait_ge(s["l_F"], m)
                    d.tensor_tensor_scan(gF[:], coef[:, 0:8].rearrange("p c e -> p (c e)"), pF[:, 0:24], 0.0, ALU.mult, ALU.add).then_inc(s["l_gF"], 1)
                    v.wait_ge(s["l_O"], m)
                    d.tensor_tensor_scan(gO[:], coef[:, 0:8].rearrange("p c e -> p (c e)"), pO[:, 0:24], 0.0, ALU.mult, ALU.add).then_inc(s["l_gO"], 1)
                    v.wait_ge(s["l_tA"], m)
                    d.scalar_tensor_tensor(cadd[:, :, 2], tA[:, 8:16], 1.0, tA[:, 0:8], ALU.add, ALU.mult).then_inc(s["l_ig"], 1)
                    v.wait_ge(s["l_ig"], m)
                    v.wait_ge(s["l_tF"], m)
                    d.tensor_tensor_scan(cnew[:].rearrange("p c e -> p (c e)"), cmul[:].rearrange("p c e -> p (c e)"),
                                         cadd[:].rearrange("p c e -> p (c e)"), 0.0, ALU.mult, ALU.add).then_inc(s["l_c"], 1)
                    v.wait_ge(s["l_tO"], m)
                    d.tensor_scalar(oU[:], tO[:], 1.0, 0.5 * H_UP, ALU.add, ALU.mult).then_inc(s["l_oU"], 1)
                    v.wait_ge(s["l_c"], m)
                    d.tensor_copy(cadd[:, :, 0:2], cnew[:, :, 3:4].to_broadcast([P, KD * B, 2])).then_inc(s["l_cc"], 1)
                    v.wait_ge(s["l_oU"], m)
                    v.wait_ge(s["l_cc"], m)
                    v.wait_ge(s["l_hs"], m)
                    v.wait_ge(s["l_tC"], m)
                    hi, lo = (h16[:, :, :, half].rearrange("p k b -> p (k b)") for half in range(2))
                    d.tensor_tensor(hi, oU[:], tC[:], ALU.mult).then_inc(s["l_hi"], 1)
                    d.tensor_tensor(h32[:], oU[:], tC[:], ALU.mult).then_inc(s["l_h32"], 1)
                    v.wait_ge(s["l_h32"], m)
                    d.tensor_tensor(lo, h32[:], hi, ALU.subtract).then_inc(s["l_lo"], 1)
                v.wait_ge(s["o_free"], j + 1)
                for b in range(B):
                    v.wait_ge(s["o_T"], j * B + b + 1)
                    d.scalar_tensor_tensor(ot[:, b * D:(b + 1) * D], bank[b][:, 0:D], 1.0 / H_UP,
                                           xs[:, bass.ds(j * B + b, 1), :].rearrange("p o d -> p (o d)"),
                                           ALU.mult, ALU.add).then_inc(s["o_s"], 1)


_INS = ["x", "cond_1024"] + [f"L0_cond_{n}" for n in ("w_q", "b_q", "w_k", "b_k", "w_v", "b_v", "w_o", "b_o", "w_f1", "b_f1",
                                                        "w_f2", "b_f2", "w_ada", "b_ada")] + ["L1_cond_Wx", "L1_cond_Wh", "L1_cond_b"]


def kernel(**inputs):
    import numpy as _np
    import concourse.bacc as _bacc
    from concourse import mybir as _mybir
    from concourse.bass_utils import run_bass_kernel_spmd as _run

    nc = _bacc.Bacc("TRN2", target_bir_lowering=False, num_devices=1)
    arrays, args = {}, []
    for name in _INS:
        a = _np.ascontiguousarray(inputs[name])
        arrays[f"in_{name}_dram"] = a
        args.append(nc.dram_tensor(f"in_{name}_dram", a.shape, _mybir.dt.from_np(a.dtype), kind="ExternalInput").ap())
    args.append(nc.dram_tensor("out_0_dram", (B, T, D), _mybir.dt.float32, kind="ExternalOutput").ap())
    bass_hyperbolic_block_then_lstm(nc, *args)
    r = _run(nc, [arrays], core_ids=[0])
    return r.results[0]["out_0_dram"]
```

```python
import math
from contextlib import ExitStack

import numpy as np

import concourse.bass as bass
from concourse import mybir

F32 = mybir.dt.float32
F16 = mybir.dt.float16
I32 = mybir.dt.int32
ALU = mybir.AluOpType
ACT = mybir.ActivationFunctionType
AX = mybir.AxisListType

B, T, D, H, FF, P = 4, 512, 256, 16, 1024, 128
HD = D // H
KD = D // P
KF = FF // P
NB = T // P
NT = B * NB
HP = H // 2
GC = 4 * D // P

EPS, LN_EPS = 1e-7, 1e-6
MAX_TANH = float(np.float32(1.0 - 1e-5))
REACH = float(np.arctanh(np.float64(MAX_TANH)))


def _beta(a, b):
    return math.exp(math.lgamma(a) + math.lgamma(b) - math.lgamma(a + b))


HEAD = _beta(HD / 2, 0.5) / _beta(D / 2, 0.5)
TINY = 1e-30
QK_UP = 256.0
H_UP = 2.0 ** 14
SERIES_BELOW = 0.01


class Chain:

    def __init__(self, eng, sem, held, per_round):
        self.eng, self.sem, self.held, self.per_round, self.base, self.n = eng, sem, held, per_round, 0, 0

    def round(self, number):
        self.base, self.n = (number - 1) * self.per_round, 0

    def link(self, ins):
        self.n += 1
        ins.then_inc(self.sem, 1)
        self.eng.wait_ge(self.sem, self.base + self.n)
        self.eng.sem_inc(self.held, 1)

    def full(self):
        assert self.n == self.per_round, (self.n, self.per_round)



GAP = 2 * HP + 1
ATT = B * GAP
NUMBERS = 1100
HSLOTS = 10


def bass_hyperbolic_block_then_lstm(nc, x, cond, w_q, b_q, w_k, b_k, w_v, b_v, w_o, b_o, w_f1, b_f1, w_f2, b_f2,
                                    w_ada, b_ada, w_x, w_h, b_l, out):
    ctx = ExitStack()
    with ctx:
        def sb(name, shape, dt=F32):
            return ctx.enter_context(nc.sbuf_tensor(name, shape, dt))

        def sem(name):
            return ctx.enter_context(nc.semaphore(name))

        wo = sb("wo", [P, KD, D])
        wf1 = sb("wf1", [P, KD, FF])
        wf2 = sb("wf2", [P, KF, D])
        wx = sb("wx", [P, KD, 4 * D])
        wh16 = sb("wh16", [P, 2, KD, 4 * D], F16)
        bo = sb("bo", [P, D])
        bf1 = sb("bf1", [P, FF])
        bf2 = sb("bf2", [P, D])
        blc = sb("blc", [P, GC])
        blc2 = sb("blc2", [P, GC])
        badac = sb("badac", [P, 6 * KD])
        ident = sb("ident", [P, P])
        ident16 = sb("ident16", [P, P], F16)
        ones = sb("ones", [P, P])
        adac = sb("adac", [P, 6 * KD, B])
        gates = sb("gates", [P, 2, B, D])
        cst = sb("cst", [P, 3, NT])
        xs = sb("xs", [P, 2, B, D])
        qhl = sb("qhl", [P, NT, H, 2 * HD], F16)
        kT = sb("kT", [P, B, HP, T], F16)
        vs = sb("vs", [P, B, NB, H, HD + 1])
        xsq = sb("xsq", [P, NT])
        kap = sb("kap", [P, NT + 1])
        kmn = sb("kmn", [P, NT + 1])
        hs = sb("hs", [P, KD, B, P])
        arena = sb("arena", [P, 2, P * GC * B])
        xw = arena[:, :, :].rearrange("p a (t g b) -> p (a t) g b", g=GC, b=B)
        flat = arena[:, :, :].rearrange("p a n -> p (a n)")
        wada = flat[:, 0:KD * 6 * D].rearrange("p (k n) -> p k n", k=KD)
        xin = flat[:, KD * 6 * D:KD * 6 * D + (NT + 1) * D].rearrange("p (t d) -> p t d", d=D)
        big = sb("big", [P, 2, NB, 2 * P])
        wh = big[:, :, :, :].rearrange("p a b c -> p (a b c)").rearrange("p (k n) -> p k n", k=KD)
        place = sb("place", [P, 4 * B * D])
        wqkv = place[:, 0:1536].rearrange("p (k a d) -> p k a d", k=KD, a=3)
        bqkv = place[:, 1536:2304].rearrange("p (a d) -> p a d", a=3)
        lin = place[:, 2304:3072].rearrange("p (a d) -> p a d", a=3)
        qk = place[:, 3072:3584].rearrange("p (a d) -> p a d", a=2)
        o4, a4, ga4, x24 = (place[:, i * B * D:(i + 1) * B * D].rearrange("p (b d) -> p b d", b=B) for i in range(4))
        waste = place[:, 0:2 * D]
        tmp = sb("tmp", [P, FF])
        xn = sb("xn", [P, D])
        uT = sb("uT", [P, 2, KD, P])
        usq = sb("usq", [P, KD, P])
        fT = sb("fT", [P, KF, P])
        c0B = fT[:, :, :].rearrange("p c t -> p (c t)").rearrange("p (k b t) -> p k b t", k=KD, b=B)
        stack = sb("stack", [P, H, 2, 2 * HD], F16)
        qbd = sb("qbd", [P, HP, 2 * P], F16)
        sc = sb("sc", [P, NUMBERS])
        c0 = xn[0:B, :]
        c0T = sb("c0T", [P, KD, B])
        h0c = sb("h0c", [P, GC, B])
        mv6 = sb("mv6", [P, 6])
        mv = sb("mv", [P, NT, 2])
        mv4 = sb("mv4", [P, B, 2])
        ot = place[:, B * D:2 * B * D]
        big1 = sb("big1", [P, 8])
        h16 = sb("h16", [P, KD, B, 2], F16)
        h32 = sb("h32", [P, KD * B])
        gA = sb("gA", [P, 48])
        gF = sb("gF", [P, 24])
        gO = sb("gO", [P, 24])
        tA = sb("tA", [P, 16])
        tO = sb("tO", [P, 8])
        oU = sb("oU", [P, 8])
        coef = sb("coef", [P, 16, 3])
        cmul = sb("cmul", [P, 8, 4])
        cadd = sb("cadd", [P, 8, 4])
        cnew = sb("cnew", [P, 8, 4])
        tC = sb("tC", [P, 8])

        psum = ctx.enter_context(nc.psum_tensor("psum", [P, 8, 512], F32))
        bank = [psum[:, i, :] for i in range(8)]
        pF, pO, pA = bank[5], bank[6], bank[7]

        def x_tile(j, b):
            return xs[:, j % 2, b, :] if isinstance(j, int) else xs[:, bass.ds(j % 2, 1), b, :].rearrange("p o d -> p (o d)")

        def half_words(i):
            return bank[i].bitcast(F16)

        names = """achain ada_s adap c0t c0t_s consts dinit gp gp_s h0_s h0p held hsc l_A l_F l_O l_c l_cc l_gA
            l_gF l_gO l_h32 l_hi l_hs l_ig l_init l_lo l_oU l_tA l_tC l_tF l_tO l_x l_x0 ld_b ld_c ld_h ld_w
            ld_x ld_xs ln1 ln1z lnr o_T o_d o_free o_s p_ct p_f p_h p_h2 p_hk p_kT p_kc p_lin p_ln p_mm p_n p_ns
            p_qk p_r p_s1 p_s2 p_sq p_ss p_su p_uT p_usq p_v p_xT p_xn pchain pk st1 t_AV t_E t_L t_S t_X
            t_XT t_XX t_Xc t_a t_a2 t_ab t_ab2 t_ar t_ar2 t_f t_f1 t_fT t_fc t_fs t_ga t_ga2 t_km t_lh t_m1
            t_m2 t_mo t_n t_n3 t_nm t_ns t_o t_oT t_oc t_op t_q t_qT t_qc t_r t_r4 t_rh t_s1 t_s6 t_sf t_so
            t_sq t_sqf t_ss t_st t_th t_th2 t_tot t_uT t_us t_w t_w2 t_x2 t_x3 t_xT t_xa t_xa2 t_xc t_xn
            t_xw t_z vchain wmax""".split()
        s = {n: sem("s_" + n) for n in names}

        def hold(eng, name, value):
            eng.wait_ge(s[name], value)
            eng.sem_inc(s["held"], 1)

        at = {}

        def num(name, w=1):
            if name not in at:
                at[name] = (sum(v[1] for v in at.values()), w)
                assert sum(v[1] for v in at.values()) <= NUMBERS
            o, w = at[name]
            return sc[:, o:o + w]

        HALF_DOWN, HALF_UP, DOWN = 0, 1, 2

        def power(ch, dst, src, which, w):
            ch.link(nc.gpsimd.tensor_tensor(dst, src, cst[:, which, 0:w], ALU.pow))

        def to_ratio(ch, w, m, var, nsq, done):
            g = nc.gpsimd
            a, b, c = num(f"a{w}", w), num(f"b{w}", w), num(f"c{w}", w)
            nc_, nd = num(f"nc{w}", w), num(f"nd{w}", w)
            ch.link(g.tensor_tensor(a, m, m, ALU.mult))
            ch.link(g.tensor_tensor(b, a, var, ALU.add))
            ch.link(g.tensor_scalar(nsq, b, float(D), None, ALU.mult))
            power(ch, a, nsq, HALF_UP, w)
            ch.link(g.tensor_scalar(nd, a, EPS, None, ALU.max))
            ch.link(g.tensor_scalar(nc_, nd, MAX_TANH, None, ALU.min))
            ch.link(g.tensor_scalar(a, nc_, 1.0, None, ALU.add))
            ch.link(g.tensor_scalar(b, nc_, -1.0, 1.0, ALU.mult, ALU.add))
            power(ch, c, b, DOWN, w)
            g.tensor_tensor(num(f"z{w}", w), a, c, ALU.mult).then_inc(done, 1)

        def to_norm(ch, w, m, var, k_out, km_out, done):
            g = nc.gpsimd
            a, b, c = num(f"a{w}", w), num(f"b{w}", w), num(f"c{w}", w)
            nc_, nd, lam, L = num(f"nc{w}", w), num(f"nd{w}", w), num(f"lam{w}", w), num(f"L{w}", w)
            n2, ser = num(f"n2{w}", w), num(f"ser{w}", w)
            power(ch, a, nd, DOWN, w)
            ch.link(g.tensor_tensor(b, L, a, ALU.mult))
            ch.link(g.tensor_scalar(lam, b, 0.5, None, ALU.mult))
            ch.link(g.tensor_tensor(n2, nc_, nc_, ALU.mult))
            ch.link(g.tensor_scalar(ser, n2, 1.0 / 9, 1.0 / 7, ALU.mult, ALU.add))
            for term in (1.0 / 5, 1.0 / 3, 1.0):
                ch.link(g.tensor_tensor(a, ser, n2, ALU.mult))
                ch.link(g.tensor_scalar(ser, a, term, None, ALU.add))
            ch.link(g.tensor_scalar(c, n2, SERIES_BELOW, None, ALU.is_lt))
            ch.link(g.tensor_tensor(a, ser, lam, ALU.subtract))
            ch.link(g.tensor_tensor(b, a, c, ALU.mult))
            ch.link(g.tensor_tensor(a, lam, b, ALU.add))
            ch.link(g.tensor_tensor(b, a, a, ALU.mult))
            ch.link(g.tensor_tensor(c, b, var, ALU.mult))
            ch.link(g.tensor_scalar(b, c, LN_EPS, None, ALU.add))
            power(ch, c, b, HALF_DOWN, w)
            ch.link(g.tensor_tensor(b, a, c, ALU.mult))
            ch.link(g.tensor_tensor(a, b, m, ALU.mult))
            ch.link(g.tensor_copy(k_out, b))
            g.tensor_scalar(km_out, a, -1.0, None, ALU.mult).then_inc(done, 1)

        def clip(ch, dst, nsq, w, a, b, done=None):
            g = nc.gpsimd
            ch.link(g.tensor_scalar(a, nsq, TINY, None, ALU.max))
            power(ch, b, a, HALF_DOWN, w)
            last = g.tensor_scalar(dst, b, REACH, 1.0, ALU.mult, ALU.min)
            if done is None:
                ch.link(last)
            else:
                last.then_inc(done, 1)

        CHUNK = (2, 3, 4, 5, 6, 7, 0, 1)
        UNIT = (0.5,) * 4 + (1.0,) * 2 + (0.5,) * 2
        GATES = ((pA, 4, 4, "l_A"), (pF, 0, 2, "l_F"), (pO, 2, 2, "l_O"))

        def gate_cols(bk, g0, n):
            return bk[:, g0 * 12:(g0 + n) * 12].rearrange("p (g b e) -> p g b e", b=B, e=3)

        WLOADS = 8
        BLOCK_LINKS = 84

        def carried(j, q):
            return (j - 1) * P + q + 1

        block = ctx.enter_context(nc.Block())

        @block.sync
        def _(sp):
            sp.dma_start(c0, cond).then_inc(s["ld_c"], 16)
            sp.dma_start(wada, w_ada.rearrange("(k p) n -> p k n", p=P)).then_inc(s["ld_c"], 16)
            sp.dma_start(badac[:], b_ada.rearrange("(c p) -> p c", p=P), allow_slow_non_contiguous=True).then_inc(s["ld_c"], 16)
            for b in range(B):
                sp.dma_start(xin[:, 0:NT, :].rearrange("p (j b) d -> p b j d", b=B)[:, b],
                             x[b].rearrange("(j p) d -> p j d", p=P)).then_inc(s["ld_x"], 16)
            for i, w in enumerate((w_q, w_k, w_v)):
                sp.dma_start(wqkv[:, :, i, :], w.rearrange("(k p) n -> p k n", p=P)).then_inc(s["ld_w"], 16)
            sp.dma_start(wo[:], w_o.rearrange("(k p) n -> p k n", p=P)).then_inc(s["ld_w"], 16)
            sp.dma_start(wf1[:], w_f1.rearrange("(k p) n -> p k n", p=P)).then_inc(s["ld_w"], 16)
            sp.dma_start(wf2[:], w_f2.rearrange("(k p) n -> p k n", p=P)).then_inc(s["ld_w"], 16)
            sp.dma_start(wx[:], w_x.rearrange("(k p) n -> p k n", p=P)).then_inc(s["ld_w"], 16)
            sp.dma_start(blc[:], b_l.rearrange("(c p) -> p c", p=P), allow_slow_non_contiguous=True).then_inc(s["ld_w"], 16)
            for j in range(2):
                sp.dma_start(xs[:, j, :, :], x[:, j * P:(j + 1) * P, :].rearrange("b p d -> p b d")).then_inc(s["ld_xs"], 16)
            sp.sem_inc(s["o_free"], 1)

            def out_block(j):
                for b in range(B):
                    sp.wait_ge(s["o_s"], B * j + b + 1)
                    sp.dma_start(out[b, bass.ds(j * P, P), :], ot[:, b * D:(b + 1) * D]).then_inc(s["o_d"], 16)
                sp.wait_ge(s["o_d"], 16 * B * (j + 1))
                sp.sem_inc(s["o_free"], 1)

            with sp.Fori(0, NB - 2) as j:
                out_block(j)
                sp.dma_start(xs[:, bass.ds(j % 2, 1), :, :].rearrange("p o b d -> p (o b) d"),
                             x[:, bass.ds((j + 2) * P, P), :].rearrange("b p d -> p b d")).then_inc(s["ld_xs"], 16)
            with sp.Fori(NB - 2, NB) as j:
                out_block(j)
            sp.wait_ge(s["o_d"], 16 * NT)

        @block.gpsimd
        def _(pool):
            g = nc.gpsimd
            g.memset(ones[:], 1.0).then_inc(s["pchain"], 1)
            hold(pool, "pchain", 1)
            g.affine_select(out=ident[:], in_=ones[:], compare_op=ALU.is_equal, fill=0.0, base=0,
                            pattern=[[-1, P]], channel_multiplier=1).then_inc(s["pchain"], 1)
            hold(pool, "pchain", 2)
            g.tensor_copy(ident16[:], ident[:]).then_inc(s["consts"], 1)
            for i, e in enumerate((-0.5, 0.5, -1.0)):
                g.memset(cst[:, i, :], e).then_inc(s["pchain"], 1)
            hold(pool, "pchain", 5)
            ch = Chain(pool, s["pchain"], s["held"], 0)
            ch.base = 5
            hold(pool, "st1", 1)
            m16, v16 = mv[:, :, 0], mv[:, :, 1]
            to_ratio(ch, NT, m16, v16, xsq[:], s["ln1z"])
            hold(pool, "ln1z", 1)
            hold(pool, "lnr", 1)
            to_norm(ch, NT, m16, v16, kap[:, 0:NT], kmn[:, 0:NT], s["ln1"])

            ch = Chain(pool, s["hsc"], s["held"], 2)
            pool.sem_inc(s["p_v"], 1)
            ch.round(1)
            hold(pool, "p_ns", 1)
            clip(ch, num("su"), num("nu"), 1, num("ca"), num("cb"), s["p_su"])
            with pool.Fori(0, NT) as k:
                ch.round(k + 2)
                hold(pool, "p_f", k + 1)
                g.tensor_tensor(vs[:, bass.ds(k % B, 1), bass.ds(k // B, 1), :, 0:HD].rearrange("p o r h e -> p (o r h) e"),
                                lin[:, 2, :].rearrange("p (h e) -> p h e", e=HD),
                                num("f", 48)[:, 2 * H:3 * H].unsqueeze(2).to_broadcast([P, H, HD]), ALU.mult).then_inc(s["p_v"], 1)
                hold(pool, "p_ns", k + 2)
                clip(ch, num("su"), num("nu"), 1, num("ca"), num("cb"), s["p_su"])
                ch.full()

            def mobius(ch, n, nsq_x, th, ar, ab):
                w = B
                N = lambda name: num(name + "w", w)
                clip(ch, N("s1"), N("n1"), w, N("ca"), N("cb"))
                ch.link(g.tensor_scalar(N("ca"), N("n2"), TINY, None, ALU.max))
                power(ch, N("n2i"), N("ca"), HALF_DOWN, w)
                ch.link(g.tensor_tensor(N("cb"), N("ca"), N("n2i"), ALU.mult))
                g.tensor_tensor(N("ar"), N("cb"), N("s1"), ALU.mult).then_inc(s[ar], 1)
                hold(pool, th, n)
                ch.link(g.tensor_tensor(N("fac"), N("th"), N("n2i"), ALU.mult))
                ch.link(g.tensor_tensor(N("y2"), N("th"), N("th"), ALU.mult))
                ch.link(g.tensor_tensor(N("xy"), N("fac"), N("xa"), ALU.mult))
                ch.link(g.tensor_scalar(N("cc"), N("xy"), 2.0, 1.0, ALU.mult, ALU.add))
                ch.link(g.tensor_tensor(N("cd"), N("cc"), N("y2"), ALU.add))
                ch.link(g.tensor_tensor(N("ca"), nsq_x, N("y2"), ALU.mult))
                ch.link(g.tensor_tensor(N("cb"), N("ca"), N("cc"), ALU.add))
                ch.link(g.tensor_scalar(N("ca"), N("cb"), EPS, None, ALU.max))
                power(ch, N("den"), N("ca"), DOWN, w)
                ch.link(g.tensor_tensor(N("al"), N("cd"), N("den"), ALU.mult))
                ch.link(g.tensor_scalar(N("cb"), nsq_x, -1.0, 1.0, ALU.mult, ALU.add))
                ch.link(g.tensor_tensor(N("cc"), N("cb"), N("fac"), ALU.mult))
                g.tensor_tensor(N("be"), N("cc"), N("den"), ALU.mult).then_inc(s[ab], 1)

            def gate_rows(ready, which, j, done):
                for b in range(B):
                    hold(pool, ready, B * j + b + 1)
                    g.tensor_tensor(ga4[:, b], a4[:, b], gates[:, which, b, :], ALU.mult).then_inc(s[done], 1)

            def pool_block(ch, j):
                n = j + 1
                ch.round(n)
                hold(pool, "t_rh", n)
                rh, fr = num("rh", B * H), num("fr", B * H)
                ch.link(g.tensor_scalar(fr, rh, REACH, 1.0, ALU.mult, ALU.min))
                ch.link(g.tensor_scalar(fr, fr, 1.0 / HEAD, None, ALU.mult))
                ch.link(g.tensor_tensor(num("ha", B * H), fr, fr, ALU.mult))
                g.tensor_tensor(num("hc", B * H), num("ha", B * H), num("ssh", B * H), ALU.mult).then_inc(s["t_f"], 1)
                hold(pool, "t_tot", n)
                clip(ch, num("sow", B), num("now", B), B, num("caw", B), num("cbw", B), s["t_so"])
                gate_rows("t_a", 0, j, "t_ga")
                ch.link(g.tensor_copy(num("xqw", B), xsq[:, bass.ds(B * j, B)] if not isinstance(j, int) else xsq[:, 0:B]))
                hold(pool, "t_n", B * n)
                hold(pool, "t_xa", B * n)
                mobius(ch, n, num("xqw", B), "t_th", "t_ar", "t_ab")
                hold(pool, "t_st", B * n)
                to_ratio(ch, B, mv4[:, :, 0], mv4[:, :, 1], num("x2q", B), s["t_z"])
                hold(pool, "t_z", n)
                hold(pool, "t_L", n)
                to_norm(ch, B, mv4[:, :, 0], mv4[:, :, 1], num("kapw", B), num("kmnw", B), s["t_km"])
                for b in range(B):
                    hold(pool, "t_ns", B * j + b + 1)
                    c1 = slice(b, b + 1)
                    clip(ch, num("suw", B)[:, c1], num("nuw", B)[:, c1], 1, num("ca"), num("cb"), s["t_fs"])
                hold(pool, "t_sqf", 2 * B * n)
                ch.link(g.tensor_tensor(num("nfw", B), num("nf0w", B), num("nf1w", B), ALU.add))
                clip(ch, num("sfw", B), num("nfw", B), B, num("caw", B), num("cbw", B), s["t_sf"])
                gate_rows("t_a2", 1, j, "t_ga2")
                hold(pool, "t_n3", B * n)
                hold(pool, "t_xa2", B * n)
                mobius(ch, n, num("x2q", B), "t_th2", "t_ar2", "t_ab2")
                for b in range(B):
                    hold(pool, "t_X", B * j + b + 1)
                    g.tensor_copy(x_tile(j, b), x24[:, b]).then_inc(s["t_XX"], 1)
                ch.full()

            hold(pool, "p_hk", NT)
            ch = Chain(pool, s["achain"], s["held"], BLOCK_LINKS)
            pool_block(ch, 0)
            with pool.Fori(1, NB) as j:
                pool_block(ch, j)

        @block.tensor
        def _(pe):
            mm, tr = nc.tensor.matmul, nc.tensor.transpose
            pe.wait_ge(s["consts"], 1)
            pe.wait_ge(s["ld_c"], 16 * 3)
            for c in range(KD):
                last = tr(bank[0][:, c * B:(c + 1) * B], c0[:, c * P:(c + 1) * P], ident[0:B, 0:B])
            last.then_inc(s["c0t"], 1)
            pe.wait_ge(s["c0t_s"], 2)
            for c in range(6 * KD):
                for kc in range(KD):
                    last = mm(bank[1][:, c * B:(c + 1) * B], wada[:, kc, c * P:(c + 1) * P], c0T[:, kc, :],
                              start=kc == 0, stop=kc == KD - 1)
            last.then_inc(s["adap"], 1)
            for which in range(2):
                for b in range(B):
                    for kc in range(KD):
                        at_ = (which * 3 + 2) * D
                        last = mm(bank[2 + 2 * which + b // 2][:, (b % 2) * D:(b % 2 + 1) * D], c0B[:, kc, b, :],
                                  wada[:, kc, at_:at_ + D], start=kc == 0, stop=kc == KD - 1, skip_group_check=True)
            last.then_inc(s["gp"], 1)
            pe.wait_ge(s["pk"], 1)
            tr(bank[6][0:1, 0:P], big1[:, 2:3], ident[:]).then_inc(s["wmax"], 1)
            pe.wait_ge(s["pk"], 2)
            mm(bank[6][:, 256:257], ones[0:1, :], big1[0:1, 4:5], start=True, stop=True).then_inc(s["wmax"], 1)
            pe.wait_ge(s["ld_h"], 16)
            for gi, c in enumerate(CHUNK):
                for kc in range(KD):
                    last = mm(bank[0][:, 64 + gi * B:64 + (gi + 1) * B], wh[:, kc, c * P:(c + 1) * P], c0T[:, kc, :],
                              start=kc == 0, stop=kc == KD - 1, skip_group_check=True)
            last.then_inc(s["h0p"], 1)

            def norm_x(k, first):
                pe.wait_ge(s["p_xn"], k + 1)
                if not first:
                    pe.wait_ge(s["p_uT"], k)
                for c in range(KD):
                    last = tr(bank[0][:, c * P:(c + 1) * P], xn[:, c * P:(c + 1) * P], ident[:])
                last.then_inc(s["p_xT"], 1)
                pe.wait_ge(s["p_usq"], k + 1)
                if not first:
                    pe.wait_ge(s["p_ns"], k)
                for c in range(KD):
                    last = mm(bank[1][:, 0:1], usq[:, c, :], ones[:, 0:1], start=c == 0, stop=c == KD - 1)
                last.then_inc(s["p_n"], 1)
                if not first:
                    pe.wait_ge(s["p_lin"], k)
                for i in range(3):
                    for kc in range(KD):
                        last = mm(bank[2 + i][:, 0:D], uT[:, 0, kc, :], wqkv[:, kc, i, :], start=kc == 0, stop=kc == KD - 1)
                last.then_inc(s["p_mm"], 1)

            pe.wait_ge(s["h0_s"], 1)
            pe.wait_ge(s["gp_s"], 1)
            pe.wait_ge(s["ld_w"], 16 * WLOADS)
            pe.sem_inc(s["p_kT"], 1)
            norm_x(0, True)
            with pe.Fori(0, NT) as k:
                norm_x(k + 1, False)
                pe.wait_ge(s["p_hk"], k + 1)
                pe.wait_ge(s["p_kc"], k + 1)
                for hp in range(HP):
                    last = tr(half_words(5)[:, hp * P:(hp + 1) * P],
                              stack[:, 2 * hp:2 * hp + 2, :, :].rearrange("p h a e -> p (h a e)"), ident16[:])
                last.then_inc(s["p_kT"], 1)

            def q_transposed(n):
                pe.wait_ge(s["t_q"], n)
                for hp in range(HP):
                    last = tr(half_words(3)[:, hp * P:(hp + 1) * P],
                              stack[:, 2 * hp:2 * hp + 2, :, :].rearrange("p h a e -> p (h a e)"), ident16[:])
                last.then_inc(s["t_qT"], 1)

            def weighted(k, hp, e):
                if e == 0:
                    pe.wait_ge(s["t_E"], HP * k + hp + 1)
                    if hp == 0:
                        pe.wait_ge(s["t_o"], k + 1)
                h = 2 * hp + e
                for kc in range(NB):
                    last = mm(bank[2][:, h * (HD + 1):(h + 1) * (HD + 1)], big[:, hp % 2, kc, e * P:(e + 1) * P],
                              vs[:, bass.ds(k % B, 1), kc, h, :].rearrange("p o e -> p (o e)"),
                              start=kc == 0, stop=kc == NB - 1, skip_group_check=True)
                if e == 1:
                    last.then_inc(s["t_AV"], 1)

            def pe_attention(k, q):
                hp = q // 2
                if q == 0:
                    pe.wait_ge(s["t_qc"], 2 * (k + 1))
                if q % 2 == 0 and hp < HP:
                    if hp > 0:
                        pe.wait_ge(s["t_E"], HP * k + hp)
                    for kc in range(NB):
                        last = mm(bank[kc // 2][:, (kc % 2) * 2 * P:(kc % 2 + 1) * 2 * P],
                                  kT[:, bass.ds(k % B, 1), hp, kc * P:(kc + 1) * P].rearrange("p o t -> p (o t)"),
                                  qbd[:, hp, :], start=True, stop=True,
                                  skip_group_check=True)
                    last.then_inc(s["t_S"], 1)
                if q % 2 == 1:
                    weighted(k, hp, 0)
                elif q > 0:
                    weighted(k, hp - 1, 1)
                if q == 3:
                    q_transposed(k + 2)

            def pe_project(j, t):
                if 1 <= t <= B:
                    b = t - 1
                    pe.wait_ge(s["t_op"], B * j + b + 1)
                    if b >= 2:
                        pe.wait_ge(s["t_oc"], B * j + b - 1)
                    for c in range(KD):
                        last = tr(bank[b % 2][:, c * P:(c + 1) * P], ga4[:, b, c * P:(c + 1) * P], ident[:])
                    last.then_inc(s["t_oT"], 1)
                if 2 <= t <= B + 1:
                    b = t - 2
                    pe.wait_ge(s["t_oc"], B * j + b + 1)
                    if b == 0:
                        pe.wait_ge(s["t_qc"], 2 * (B * j + B + 1))
                    if b >= 2:
                        pe.wait_ge(s["t_a"], B * j + b - 1)
                    for kc in range(KD):
                        last = mm(bank[3 + b % 2][:, 0:D], uT[:, b % 2, kc, :], wo[:, kc, :], start=kc == 0, stop=kc == KD - 1)
                    last.then_inc(s["t_mo"], 1)

            def pe_norm(n):
                pe.wait_ge(s["t_xn"], n)
                for c in range(KD):
                    last = tr(bank[0][:, c * P:(c + 1) * P], xn[:, c * P:(c + 1) * P], ident[:])
                last.then_inc(s["t_xT"], 1)

            def pe_hidden(n, q, more):
                if q == 0:
                    pe.wait_ge(s["t_us"], n)
                    for c in range(KD):
                        last = mm(bank[2][:, 0:1], usq[:, c, :], ones[:, 0:1], start=c == 0, stop=c == KD - 1)
                    last.then_inc(s["t_nm"], 1)
                if q < 4:
                    half, kc = q // 2, q % 2
                    last = mm(bank[half][:, :], uT[:, 0, kc, :], wf1[:, kc, half * 512:(half + 1) * 512],
                              start=kc == 0, stop=kc == KD - 1)
                    if kc == KD - 1:
                        last.then_inc(s["t_m1"], 1)
                if q in (3, 4):
                    half = q - 3
                    pe.wait_ge(s["t_f1"], 2 * n - 1 + half)
                    for c in range(KF // 2):
                        cc = half * (KF // 2) + c
                        last = tr(bank[2 + half][:, c * P:(c + 1) * P], tmp[:, cc * P:(cc + 1) * P], ident[:])
                    last.then_inc(s["t_fT"], 1)
                if q >= 4:
                    if q == 4:
                        pe.wait_ge(s["t_fc"], 2 * n - 1)
                        pe.wait_ge(s["t_r4"], n)
                    for kc in ((0, 1), (2, 3, 4), (5, 6, 7))[q - 4]:
                        if kc == 4:
                            pe.wait_ge(s["t_fc"], 2 * n)
                        last = mm(bank[4][:, 0:D], fT[:, kc, :], wf2[:, kc, :], start=kc == 0, stop=kc == KF - 1)
                if q == 6:
                    last.then_inc(s["t_m2"], 1)
                    if more:
                        pe_norm(n + 1)

            def pe_gates_T(n, b):
                pe.wait_ge(s["t_X"], n)
                for c in range(KD):
                    last = tr(bank[4][:, c * P:(c + 1) * P], x24[:, b, c * P:(c + 1) * P], ident[:])
                last.then_inc(s["t_XT"], 1)

            def pe_gates(j, b, half):
                n = B * j + b + 1
                if half == 0:
                    pe.wait_ge(s["t_Xc"], n)
                if b >= 2:
                    pe.wait_ge(s["t_xc"], 2 * (n - 2) - 1 + half)
                for gi in range(GC // 2):
                    c = CHUNK[half * (GC // 2) + gi]
                    for kc in range(KD):
                        last = mm(bank[half + 2 * (b % 2)][:, gi * P:(gi + 1) * P], wx[:, kc, c * P:(c + 1) * P], uT[:, b % 2, kc, :],
                                  start=kc == 0, stop=kc == KD - 1, skip_group_check=True)
                last.then_inc(s["t_xw"], 1)
                if half == 1 and b < B - 1:
                    pe_gates_T(n + 1, b + 1)

            def pe_step(m):
                pe.wait_ge(s["l_x"], m)
                pe.wait_ge(s["l_lo"], m)
                for bk, g0, ng, made in GATES:
                    for gi in range(ng):
                        for kc in range(KD):
                            for half in range(2):
                                last = mm(gate_cols(bk, gi, 1)[:, 0, :, 0:2],
                                          wh16[:, half, kc, (g0 + gi) * P:(g0 + gi + 1) * P], h16[:, kc, :, :],
                                          start=gi == 0 and kc == 0 and half == 0, stop=gi == ng - 1 and kc == KD - 1 and half == 1,
                                          skip_group_check=True)
                    last.then_inc(s[made], 1)

            def pe_out(j):
                pe.wait_ge(s["l_hs"], P * (j + 1))
                for b in range(B):
                    for kc in range(KD):
                        last = tr(bank[b][:, kc * P:(kc + 1) * P], hs[:, kc, b, :], ident[:])
                    last.then_inc(s["o_T"], 1)
                pe.wait_ge(s["o_s"], B * (j + 1))

            pe.wait_ge(s["p_kc"], NT + 1)
            pe.wait_ge(s["p_v"], NT + 1)
            pe.wait_ge(s["l_init"], 2)
            q_transposed(1)

            def whole(j, step):
                with pe.Fori(0, B) as b:
                    base = None if step is None else pe.snap(carried(j, b * GAP))
                    for q in range(GAP):
                        if step:
                            step(base + q)
                        pe_attention(B * j + b, q)
                at_slot = ATT

                def slot():
                    nonlocal at_slot
                    if step and at_slot < P - 1:
                        step(carried(j, at_slot))
                    at_slot += 1

                for _ in range(3):
                    slot()
                for t in range(B + 2):
                    slot()
                    pe_project(j, t)
                for _ in range(12):
                    slot()
                slot()
                pe_norm(B * j + 1)
                for b in range(B):
                    for q in range(7):
                        slot()
                        pe_hidden(B * j + b + 1, q, b < B - 1)
                for _ in range(HSLOTS):
                    slot()
                pe_gates_T(B * j + 1, 0)
                for b in range(B):
                    for half in range(2):
                        slot()
                        pe_gates(j, b, half)
                pe.wait_ge(s["t_xc"], 2 * B * (j + 1))
                if step:
                    while at_slot < P - 1:
                        slot()
                    step(carried(j, P - 1))

            whole(0, None)
            with pe.Fori(1, NB) as j:
                whole(j, pe_step)
                pe_out(j - 1)
            with pe.Fori((NB - 1) * P + 1, NB * P + 1) as m:
                pe_step(m)
            pe_out(NB - 1)

        @block.scalar
        def _(act):
            A = nc.scalar.activation
            act.dma_start(wh, w_h.rearrange("(k p) n -> p k n", p=P)).then_inc(s["ld_h"], 16)
            for i, bias in enumerate((b_q, b_k, b_v)):
                act.dma_start(bqkv[:, i, :], bias.partition_broadcast(P)).then_inc(s["ld_b"], 16)
            act.dma_start(bo[:], b_o.partition_broadcast(P)).then_inc(s["ld_b"], 16)
            act.dma_start(bf1[:], b_f1.partition_broadcast(P)).then_inc(s["ld_b"], 16)
            act.dma_start(bf2[:], b_f2.partition_broadcast(P)).then_inc(s["ld_b"], 16)
            for which in range(2):
                at_ = (which * 3 + 2) * D
                for b in range(B):
                    act.dma_start(gates[:, which, b, :], b_ada[at_:at_ + D].partition_broadcast(P)).then_inc(s["ld_b"], 16)
            nc.scalar.preload_act_table_set("natural_log_exp_and_others")
            act.wait_ge(s["ln1z"], 1)
            A(num(f"L{NT}", NT), num(f"z{NT}", NT), ACT.Ln).then_inc(s["lnr"], 1)

            def norm_x(k, b, first):
                if not first:
                    act.wait_ge(s["p_xT"], k)
                A(xn[:], xin[:, bass.ds(k, 1), :].rearrange("p o d -> p (o d)") if not first else xin[:, 0, :], ACT.Identity,
                  scale=kap[:, bass.ds(k, 1)] if not first else kap[:, 0:1],
                  bias=kmn[:, bass.ds(k, 1)] if not first else kmn[:, 0:1]).then_inc(s["p_xn"], 1)
                act.wait_ge(s["p_xT"], k + 1)
                for c in range(KD):
                    last = A(uT[:, 0, c, :], bank[0][:, c * P:(c + 1) * P], ACT.Identity,
                             scale=adac[:, KD + c, bass.ds(b, 1)] if not first else adac[:, KD + c, 0:1],
                             bias=adac[:, c, bass.ds(b, 1)] if not first else adac[:, c, 0:1])
                last.then_inc(s["p_uT"], 1)
                act.wait_ge(s["p_uT"], k + 1)
                A(usq[:, :, :], uT[:, 0, :, :], ACT.Square).then_inc(s["p_usq"], 1)

            act.wait_ge(s["ln1"], 1)
            act.wait_ge(s["ada_s"], 1)
            act.sem_inc(s["p_kc"], 1)
            norm_x(0, 0, True)
            with act.Fori(0, NT) as k:
                act.wait_ge(s["p_lin"], k + 1)
                A(tmp[:, 0:3 * D], lin[:, :, :].rearrange("p a d -> p (a d)"), ACT.Square).then_inc(s["p_sq"], 1)
                norm_x(k + 1, (k + 1) % B, False)
                act.wait_ge(s["p_ss"], k + 1)
                A(num("lss", 51), num("ss", 51), ACT.Ln).then_inc(s["p_ln"], 1)
                act.wait_ge(s["p_ln"], k + 1)
                A(num("rss", 51), num("lss", 51), ACT.Exp, scale=-0.5).then_inc(s["p_r"], 1)
                act.wait_ge(s["p_kT"], k + 2)
                A(kT[:, bass.ds(k % B, 1), :, bass.ds(k // B * P, P)].rearrange("p o h t -> p (o h) t"),
                  half_words(5)[:, 0:HP * P].rearrange("p (h t) -> p h t", h=HP), ACT.Copy).then_inc(s["p_kc"], 1)

            def q_blocks(n, e):
                act.wait_ge(s["t_qT"], n)
                r = slice(64 * e, 64 * e + 64)
                A(qbd[r, :, e * P:(e + 1) * P],
                  half_words(3)[r, 0:HP * P].rearrange("p (h t) -> p h t", h=HP), ACT.Copy).then_inc(s["t_qc"], 1)

            def act_attention(k, q):
                hp = q // 2
                if q % 2 == 0 and hp < HP:
                    act.wait_ge(s["t_S"], HP * k + hp + 1)
                    if hp >= 2:
                        act.wait_ge(s["t_AV"], HP * k + hp - 1)
                    for half in range(2):
                        last = A(big[:, hp % 2, 2 * half:2 * half + 2, :].rearrange("p a b -> p (a b)"), bank[half],
                                 ACT.Exp, scale=1.0 / (math.sqrt(HD) * QK_UP * QK_UP))
                    last.then_inc(s["t_E"], 1)
                if q >= GAP - 2:
                    q_blocks(k + 2, q - (GAP - 2))

            def act_heads(j):
                act.wait_ge(s["t_o"], B * (j + 1) + 1)
                A(tmp[:], o4[:, :, :].rearrange("p b d -> p (b d)"), ACT.Square).then_inc(s["t_sq"], 1)

            def act_heads2(j):
                hold(act, "t_ss", j + 1)
                nc.scalar.preload_act_table_set("natural_log_exp_and_others")
                A(num("lh", B * H), num("mh", B * H), ACT.Ln).then_inc(s["t_lh"], 1)
                act.wait_ge(s["t_lh"], j + 1)
                A(num("rh", B * H), num("lh", B * H), ACT.Exp, scale=-0.5).then_inc(s["t_rh"], 1)
                nc.scalar.preload_act_table_set("exp_and_others")

            def act_project(j, t):
                if 1 <= t <= B:
                    b = t - 1
                    act.wait_ge(s["t_oT"], B * j + b + 1)
                    if b >= 2:
                        act.wait_ge(s["t_mo"], B * j + b - 1)
                    A(uT[:, b % 2, :, :].rearrange("p c t -> p (c t)"), bank[b % 2][:, 0:D], ACT.Copy).then_inc(s["t_oc"], 1)

            def act_squares(j, b, ready, ready_g, done):
                if b > 0:
                    act.wait_ge(s[done], B * j + b)
                act.wait_ge(s[ready], B * j + b + 1)
                A(waste[:, 0:D], a4[:, b], ACT.Square, accum_out=num("n1w", B)[:, b:b + 1])
                act.wait_ge(s[ready_g], B * j + b + 1)
                A(waste[:, D:2 * D], ga4[:, b], ACT.Square, accum_out=num("n2w", B)[:, b:b + 1]).then_inc(s[done], 1)

            def act_tanh(j, ready, done):
                act.wait_ge(s[ready], j + 1)
                A(num("thw", B), num("arw", B), ACT.Tanh).then_inc(s[done], 1)

            def act_scaled(j, b, ready, src, done):
                act.wait_ge(s[ready], j + 1)
                A(x24[:, b], src, ACT.Copy, scale=num("alw", B)[:, b:b + 1]).then_inc(s[done], 1)

            def act_log(j):
                act.wait_ge(s["t_z"], j + 1)
                A(num(f"L{B}", B), num(f"z{B}", B), ACT.Ln).then_inc(s["t_L"], 1)
                nc.scalar.preload_act_table_set("exp_and_others")

            def act_norm(n, b):
                A(xn[:], x24[:, b], ACT.Identity, scale=num("kapw", B)[:, b:b + 1], bias=num("kmnw", B)[:, b:b + 1]).then_inc(s["t_xn"], 1)

            def act_norm2(n, b):
                act.wait_ge(s["t_xT"], n)
                for c in range(KD):
                    last = A(uT[:, 0, c, :], bank[0][:, c * P:(c + 1) * P], ACT.Identity,
                             scale=adac[:, 4 * KD + c, b:b + 1], bias=adac[:, 3 * KD + c, b:b + 1])
                last.then_inc(s["t_uT"], 1)
                act.wait_ge(s["t_uT"], n)
                A(usq[:, :, :], uT[:, 0, :, :], ACT.Square).then_inc(s["t_us"], 1)

            def act_hidden(n, b, q, more):
                if q in (2, 4):
                    half = q // 2 - 1
                    if b > 0 or half > 0:
                        act.wait_ge(s["t_sqf"], 2 * (n - 1) + half)
                    act.wait_ge(s["t_f1"], 2 * n - 1 + half)
                    A(waste, tmp[:, half * 512:(half + 1) * 512], ACT.Square,
                      accum_out=num(f"nf{half}w", B)[:, b:b + 1]).then_inc(s["t_sqf"], 1)
                if q in (3, 4):
                    half = q - 3
                    act.wait_ge(s["t_fT"], 2 * n - 1 + half)
                    A(fT[:, half * (KF // 2):(half + 1) * (KF // 2), :].rearrange("p c t -> p (c t)"), bank[2 + half],
                      ACT.Copy).then_inc(s["t_fc"], 1)
                if q == 5 and more:
                    act_norm(n + 1, b + 1)
                if q == 6 and more:
                    act_norm2(n + 1, b + 1)

            def act_gates_T(n, b):
                act.wait_ge(s["t_XT"], n)
                A(uT[:, b % 2, :, :].rearrange("p c t -> p (c t)"), bank[4][:, 0:D], ACT.Copy).then_inc(s["t_Xc"], 1)

            def act_gates(j, b, half):
                n = B * j + b + 1
                act.wait_ge(s["t_xw"], 2 * n - 1 + half)
                for gi in range(GC // 2):
                    gg = half * (GC // 2) + gi
                    dst = (xw[:, bass.ds(j % 2 * P, P), gg, b] if not isinstance(j, int) else xw[:, 0:P, gg, b])
                    last = A(dst, bank[half + 2 * (b % 2)][:, gi * P:(gi + 1) * P], ACT.Identity, scale=UNIT[gg], bias=blc2[:, gg:gg + 1])
                last.then_inc(s["t_xc"], 1)
                if half == 1 and b < B - 1:
                    act_gates_T(n + 1, b + 1)

            def put_xw(i, counted):
                two = psum[:, 5:7, 0:24].rearrange("p a (c e) -> p a c e", e=3)[:, :, :, 2]
                if isinstance(i, int):
                    fo, gi_ = xw[:, i, 0:4, :], xw[:, i, 4:8, :]
                else:
                    fo, gi_ = (xw[:, bass.ds(i, 1), a:a + 4, :].rearrange("p o g b -> p (o g) b") for a in (0, 4))
                A(two, fo.rearrange("p (a c) b -> p a (c b)", a=2), ACT.Copy)
                A(gate_cols(pA, 0, 4)[:, :, :, 2].rearrange("p g b -> p (g b)"), gi_.rearrange("p g b -> p (g b)"), ACT.Copy).then_inc(s["l_x"], 1)

            def act_step(m):
                act.wait_ge(s["l_gA"], m)
                A(tA[:], gA[:].rearrange("p (c e) -> p e c", e=3)[:, 2], ACT.Tanh).then_inc(s["l_tA"], 1)
                act.wait_ge(s["l_gF"], m)
                A(cmul[:, :, 1], gF[:].rearrange("p (c e) -> p e c", e=3)[:, 2], ACT.Tanh).then_inc(s["l_tF"], 1)
                act.wait_ge(s["l_gO"], m)
                A(tO[:], gO[:].rearrange("p (c e) -> p e c", e=3)[:, 2], ACT.Tanh).then_inc(s["l_tO"], 1)
                act.wait_ge(s["l_c"], m)
                A(tC[:], cnew[:, :, 3], ACT.Tanh).then_inc(s["l_tC"], 1)
                put_xw(m % (2 * P), True)

            act.wait_ge(s["l_init"], 2)
            for e in range(2):
                q_blocks(1, e)
            nc.scalar.preload_act_table_set("exp_and_others")

            def whole(j, step):
                with act.Fori(0, B) as b:
                    base = None if step is None else act.snap(carried(j, b * GAP))
                    for q in range(GAP):
                        if step:
                            step(base + q)
                        act_attention(B * j + b, q)
                at_slot = ATT

                def slot():
                    nonlocal at_slot
                    if step and at_slot < P - 1:
                        step(carried(j, at_slot))
                    at_slot += 1

                slot()
                act_heads(j)
                slot()
                slot()
                act_heads2(j)
                for t in range(B + 2):
                    slot()
                    act_project(j, t)
                    if t >= 4:
                        act_squares(j, t - 4, "t_a", "t_ga", "t_n")
                slot()
                act_squares(j, 2, "t_a", "t_ga", "t_n")
                slot()
                act_squares(j, 3, "t_a", "t_ga", "t_n")
                for _ in range(2):
                    slot()
                act_tanh(j, "t_ar", "t_th")
                for _ in range(2):
                    slot()
                for b in range(B):
                    if b % 2 == 0:
                        slot()
                    act_scaled(j, b, "t_ab", x_tile(j, b), "t_w")
                for _ in range(2):
                    slot()
                act_log(j)
                for _ in range(2):
                    slot()
                act.wait_ge(s["t_km"], j + 1)
                act_norm(B * j + 1, 0)
                slot()
                act_norm2(B * j + 1, 0)
                for b in range(B):
                    for q in range(7):
                        slot()
                        act_hidden(B * j + b + 1, b, q, b < B - 1)
                slot()
                slot()
                for b in range(B):
                    if b % 2 == 0:
                        slot()
                    act_squares(j, b, "t_a2", "t_ga2", "t_n3")
                slot()
                act_tanh(j, "t_ar2", "t_th2")
                for _ in range(2):
                    slot()
                for b in range(B):
                    act_scaled(j, b, "t_ab2", x24[:, b], "t_w2")
                for _ in range(HSLOTS - 7):
                    slot()
                act_gates_T(B * j + 1, 0)
                for b in range(B):
                    for half in range(2):
                        slot()
                        act_gates(j, b, half)
                if step:
                    while at_slot < P - 1:
                        slot()
                    step(carried(j, P - 1))

            whole(0, None)
            act.wait_ge(s["l_x0"], 1)
            put_xw(0, True)
            with act.Fori(1, NB) as j:
                whole(j, act_step)
            with act.Fori((NB - 1) * P + 1, NB * P + 1) as m:
                act_step(m)

        @block.vector
        def _(v):
            d = nc.vector
            d.memset(qbd[:], 0.0).then_inc(s["l_init"], 1)
            d.memset(vs[:, :, :, :, HD:HD + 1], 1.0).then_inc(s["l_init"], 1)
            d.memset(h16[:], 0.0).then_inc(s["l_lo"], 1)
            d.memset(coef[:, :, 0], 0.0).then_inc(s["dinit"], 1)
            d.memset(coef[:, :, 1], 1.0).then_inc(s["dinit"], 1)
            d.memset(cmul[:, :, 0], 0.0).then_inc(s["dinit"], 1)
            d.memset(cmul[:, :, 2], 1.0).then_inc(s["dinit"], 1)
            d.memset(cmul[:, :, 3], 0.5).then_inc(s["dinit"], 1)
            d.memset(cadd[:], 0.0).then_inc(s["dinit"], 1)
            d.memset(xin[:, NT, :], 0.0).then_inc(s["dinit"], 1)
            d.memset(kap[:, NT:], 0.0).then_inc(s["dinit"], 1)
            d.memset(kmn[:, NT:], 0.0).then_inc(s["dinit"], 1)
            v.wait_ge(s["ld_x"], 16 * B)
            v.wait_ge(s["ld_xs"], 16 * 2)
            v.wait_ge(s["dinit"], 9)
            for k in range(NT):
                d.bn_stats(mv6[:], xin[:, k, :]).then_inc(s["vchain"], 1)
                v.wait_ge(s["vchain"], 2 * k + 1)
                d.bn_aggr(mv[:, k, :], mv6[:]).then_inc(s["vchain"], 1)
                v.wait_ge(s["vchain"], 2 * k + 2)
            d.memset(num("one"), 1.0).then_inc(s["st1"], 1)
            nv = 2 * NT

            def link(ins):
                nonlocal nv
                nv += 1
                ins.then_inc(s["vchain"], 1)
                v.wait_ge(s["vchain"], nv)

            v.wait_ge(s["c0t"], 1)
            d.tensor_copy(c0T[:], bank[0][:, 0:KD * B].rearrange("p (k b) -> p k b", b=B)).then_inc(s["c0t_s"], 1)
            v.wait_ge(s["c0t_s"], 1)
            d.tensor_copy(c0B, c0T[:].unsqueeze(3).to_broadcast([P, KD, B, P])).then_inc(s["c0t_s"], 1)
            v.wait_ge(s["adap"], 1)
            link(d.tensor_tensor(adac[:], bank[1][:, 0:6 * KD * B].rearrange("p (c b) -> p c b", b=B),
                                 badac[:].unsqueeze(2).to_broadcast([P, 6 * KD, B]), ALU.add))
            for c in (KD, 4 * KD):
                last = d.tensor_scalar(adac[:, c:c + KD, :], adac[:, c:c + KD, :], 1.0, None, ALU.add)
            last.then_inc(s["ada_s"], 1)
            v.wait_ge(s["gp"], 1)
            v.wait_ge(s["ld_b"], 16 * 14)
            for which in range(2):
                for b in range(B):
                    last = d.tensor_tensor(gates[:, which, b, :], bank[2 + 2 * which + b // 2][:, (b % 2) * D:(b % 2 + 1) * D],
                                           gates[:, which, b, :], ALU.add)
            last.then_inc(s["gp_s"], 1)
            v.wait_ge(s["ld_h"], 16)
            link(d.tensor_reduce(big1[:, 0:1], wh, axis=AX.XY, op=ALU.max))
            link(d.tensor_reduce(big1[:, 1:2], wh, axis=AX.XY, op=ALU.min))
            link(d.tensor_scalar(big1[:, 3:4], big1[:, 1:2], -1.0, 2.0 ** -100, ALU.mult, ALU.max))
            d.tensor_tensor(big1[:, 2:3], big1[:, 0:1], big1[:, 3:4], ALU.max).then_inc(s["pk"], 1)
            v.wait_ge(s["wmax"], 1)
            link(d.tensor_reduce(big1[0:1, 5:6], bank[6][0:1, 0:P], axis=AX.X, op=ALU.max))
            d.tensor_scalar(big1[0:1, 4:5].bitcast(I32), big1[0:1, 5:6].bitcast(I32), 0x7F800000, None, ALU.bitwise_and).then_inc(s["pk"], 1)
            v.wait_ge(s["wmax"], 2)
            link(d.tensor_copy(big1[:, 6:7], bank[6][:, 256:257]))
            link(d.reciprocal(big1[:, 7:8], big1[:, 6:7]))
            v.wait_ge(s["ld_w"], 16 * WLOADS)
            link(d.tensor_scalar(coef[:, :, 2], coef[:, :, 1], big1[:, 6:7], 1.0 / (H_UP * 2.0 ** 14), ALU.mult, ALU.mult))
            link(d.tensor_scalar(big1[:, 6:7], big1[:, 7:8], 2.0 ** 14, None, ALU.mult))
            for g0 in range(GC):
                c = CHUNK[g0]
                src, w = wh[:, :, c * P:(c + 1) * P], tmp[:, 0:KD * P].rearrange("p (k n) -> p k n", k=KD)
                hi, lo = (wh16[:, half, :, g0 * P:(g0 + 1) * P] for half in range(2))
                link(d.tensor_scalar(w, src, big1[:, 6:7], UNIT[g0], ALU.mult, ALU.mult))
                link(d.tensor_copy(hi, w))
                link(d.tensor_tensor(lo, w, hi, ALU.subtract))
            v.wait_ge(s["h0p"], 1)
            for g0 in range(GC):
                d.tensor_scalar(h0c[:, g0, :], bank[0][:, 64 + g0 * B:64 + (g0 + 1) * B], UNIT[g0], None, ALU.mult)
                last = d.tensor_scalar(blc2[:, g0:g0 + 1], blc[:, CHUNK[g0]:CHUNK[g0] + 1], UNIT[g0], None, ALU.mult)
            last.then_inc(s["h0_s"], 1)

            v.wait_ge(s["p_n"], 1)
            d.tensor_copy(num("nu"), bank[1][:, 0:1]).then_inc(s["p_ns"], 1)
            with v.Fori(0, NT) as k:
                n = k + 1
                v.wait_ge(s["p_mm"], n)
                v.wait_ge(s["p_v"], n)
                v.wait_ge(s["p_su"], n)
                for i in range(3):
                    last = d.scalar_tensor_tensor(lin[:, i, :], bank[2 + i][:, 0:D], num("su"), bqkv[:, i, :], ALU.mult, ALU.add)
                last.then_inc(s["p_lin"], 1)
                v.wait_ge(s["p_n"], n + 1)
                d.tensor_copy(num("nu"), bank[1][:, 0:1]).then_inc(s["p_ns"], 1)
                v.wait_ge(s["p_sq"], n)
                d.tensor_reduce(num("ssr", 48), tmp[:, 0:3 * D].rearrange("p (h e) -> p h e", e=HD), axis=AX.X, op=ALU.add).then_inc(s["p_s1"], 1)
                v.wait_ge(s["p_s1"], n)
                d.tensor_reduce(num("tot", 3), num("ssr", 48).rearrange("p (a h) -> p a h", a=3), axis=AX.X, op=ALU.add).then_inc(s["p_s2"], 1)
                d.tensor_scalar(num("ss", 51)[:, 0:48], num("ssr", 48), 1.0, None, ALU.max)
                v.wait_ge(s["p_s2"], n)
                d.tensor_scalar(num("ss", 51)[:, 48:51], num("tot", 3), 1.0, None, ALU.max).then_inc(s["p_ss"], 1)
                v.wait_ge(s["p_r"], n)
                d.tensor_scalar(num("ct", 3), num("rss", 51)[:, 48:51], REACH * HEAD, HEAD, ALU.mult, ALU.min).then_inc(s["p_ct"], 1)
                v.wait_ge(s["p_ct"], n)
                for i in range(3):
                    last = d.tensor_scalar(num("f", 48)[:, i * H:(i + 1) * H], num("rss", 51)[:, i * H:(i + 1) * H],
                                           REACH, num("ct", 3)[:, i:i + 1], ALU.mult, ALU.min)
                last.then_inc(s["p_f"], 1)
                v.wait_ge(s["p_f"], n)
                for i in range(2):
                    last = d.scalar_tensor_tensor(qk[:, i, :].rearrange("p (h e) -> p h e", e=HD), lin[:, i, :].rearrange("p (h e) -> p h e", e=HD),
                                                  QK_UP, num("f", 48)[:, i * H:(i + 1) * H].unsqueeze(2).to_broadcast([P, H, HD]), ALU.mult, ALU.mult)
                last.then_inc(s["p_qk"], 1)
                v.wait_ge(s["p_kT"], n)
                v.wait_ge(s["p_qk"], n)
                q3, k3 = (qk[:, i, :].rearrange("p (h e) -> p h e", e=HD) for i in range(2))
                qh, ql = (qhl[:, bass.ds(k, 1), :, i * HD:(i + 1) * HD].rearrange("p o h e -> p (o h) e") for i in range(2))
                kh, kl = stack[:, :, 0, :], stack[:, :, 1, :]
                d.tensor_copy(qh, q3)
                d.tensor_copy(kh[:, :, 0:HD], k3).then_inc(s["p_h"], 1)
                v.wait_ge(s["p_h"], n)
                d.tensor_tensor(ql, q3, qh, ALU.subtract)
                d.tensor_tensor(kl[:, :, 0:HD], k3, kh[:, :, 0:HD], ALU.subtract).then_inc(s["p_h2"], 1)
                d.tensor_copy(kh[:, :, HD:2 * HD], kh[:, :, 0:HD])
                v.wait_ge(s["p_h2"], n)
                d.tensor_copy(kl[:, :, HD:2 * HD], kl[:, :, 0:HD]).then_inc(s["p_hk"], 1)

            def q_twice(k):
                for dup in range(2):
                    last = d.tensor_copy(stack[:, :, dup, :], qhl[:, bass.ds(k, 1), :, :].rearrange("p o h e -> p (o h) e"))
                last.then_inc(s["t_q"], 1)

            def dve_attention(k, q):
                if q == 1:
                    v.wait_ge(s["t_qT"], k + 1)
                    q_twice((k + 1) % NT)
                if q == GAP - 1:
                    o3 = bank[2][:, 0:H * (HD + 1)].rearrange("p (h e) -> p h e", e=HD + 1)
                    v.wait_ge(s["t_AV"], HP * (k + 1))
                    d.reciprocal(num("rd", H), o3[:, :, HD]).then_inc(s["t_r"], 1)
                    v.wait_ge(s["t_r"], k + 1)
                    d.tensor_tensor(o4[:, bass.ds(k % B, 1), :].rearrange("p o (h e) -> p (o h) e", e=HD), o3[:, :, 0:HD],
                                    num("rd", H).unsqueeze(2).to_broadcast([P, H, HD]), ALU.mult).then_inc(s["t_o"], 1)

            def dve_heads(j):
                v.wait_ge(s["t_sq"], j + 1)
                d.tensor_reduce(num("ssh", B * H), tmp[:].rearrange("p (h e) -> p h e", e=HD), axis=AX.X, op=ALU.add).then_inc(s["t_s1"], 1)
                v.wait_ge(s["t_s1"], j + 1)
                d.tensor_scalar(num("mh", B * H), num("ssh", B * H), 1.0, None, ALU.max).then_inc(s["t_ss"], 1)

            def dve_whole(j):
                v.wait_ge(s["t_f"], j + 1)
                d.tensor_reduce(num("now", B), num("hc", B * H).rearrange("p (b h) -> p b h", b=B), axis=AX.X, op=ALU.add).then_inc(s["t_tot"], 1)

            def dve_project(j, t):
                if t < B:
                    d.tensor_tensor(ga4[:, t].rearrange("p (h e) -> p h e", e=HD), o4[:, t].rearrange("p (h e) -> p h e", e=HD),
                                    num("fr", B * H)[:, t * H:(t + 1) * H].unsqueeze(2).to_broadcast([P, H, HD]), ALU.mult).then_inc(s["t_op"], 1)
                if 2 <= t:
                    b = t - 2
                    if b == 0 and not isinstance(j, int):
                        v.wait_ge(s["o_free"], j)
                    v.wait_ge(s["t_so"], j + 1)
                    v.wait_ge(s["t_mo"], B * j + b + 1)
                    d.scalar_tensor_tensor(a4[:, b], bank[3 + b % 2][:, 0:D], num("sow", B)[:, b:b + 1], bo[:], ALU.mult, ALU.add).then_inc(s["t_a"], 1)

            def dve_dot(j, b, res, ready, done):
                if b > 0:
                    v.wait_ge(s[done], B * j + b)
                v.wait_ge(s[ready], B * j + b + 1)
                d.scalar_tensor_tensor(tmp[:, 0:D], res, 1.0, ga4[:, b], ALU.mult, ALU.mult,
                                       accum_out=num("xaw", B)[:, b:b + 1]).then_inc(s[done], 1)

            def dve_sum(j, b, ready, done):
                v.wait_ge(s[ready], B * j + b + 1)
                d.scalar_tensor_tensor(x24[:, b], ga4[:, b], num("bew", B)[:, b:b + 1], x24[:, b], ALU.mult, ALU.add).then_inc(s[done], 1)
                v.wait_ge(s[done], B * j + b + 1)

            def dve_stats(j, b):
                d.bn_stats(mv6[:], x24[:, b]).then_inc(s["t_s6"], 1)
                hold(v, "t_s6", B * j + b + 1)
                d.bn_aggr(mv4[:, b, :], mv6[:]).then_inc(s["t_st"], 1)

            def dve_hidden(n, b, q):
                if q == 0:
                    v.wait_ge(s["t_nm"], n)
                    d.tensor_copy(num("nuw", B)[:, b:b + 1], bank[2][:, 0:1]).then_inc(s["t_ns"], 1)
                if q in (1, 3):
                    half = q // 2
                    v.wait_ge(s["t_fs"], n)
                    v.wait_ge(s["t_m1"], 2 * n - 1 + half)
                    d.scalar_tensor_tensor(tmp[:, half * 512:(half + 1) * 512], bank[half], num("suw", B)[:, b:b + 1],
                                           bf1[:, half * 512:(half + 1) * 512], ALU.mult, ALU.add).then_inc(s["t_f1"], 1)
                if q == 6:
                    v.wait_ge(s["t_m2"], n)
                    d.tensor_copy(a4[:, b], bank[4][:, 0:D]).then_inc(s["t_r4"], 1)

            def dve_step(m, i):
                v.wait_ge(s["l_A"], m)
                d.tensor_tensor_scan(gA[:], coef[:].rearrange("p c e -> p (c e)"), pA[:, 0:48], 0.0, ALU.mult, ALU.add).then_inc(s["l_gA"], 1)
                v.wait_ge(s["l_F"], m)
                d.tensor_tensor_scan(gF[:], coef[:, 0:8].rearrange("p c e -> p (c e)"), pF[:, 0:24], 0.0, ALU.mult, ALU.add).then_inc(s["l_gF"], 1)
                v.wait_ge(s["l_O"], m)
                d.tensor_tensor_scan(gO[:], coef[:, 0:8].rearrange("p c e -> p (c e)"), pO[:, 0:24], 0.0, ALU.mult, ALU.add).then_inc(s["l_gO"], 1)
                v.wait_ge(s["l_tA"], m)
                d.scalar_tensor_tensor(cadd[:, :, 2], tA[:, 8:16], 1.0, tA[:, 0:8], ALU.add, ALU.mult).then_inc(s["l_ig"], 1)
                v.wait_ge(s["l_tF"], m)
                v.wait_ge(s["l_ig"], m)
                d.tensor_tensor_scan(cnew[:].rearrange("p c e -> p (c e)"), cmul[:].rearrange("p c e -> p (c e)"),
                                     cadd[:].rearrange("p c e -> p (c e)"), 0.0, ALU.mult, ALU.add).then_inc(s["l_c"], 1)
                v.wait_ge(s["l_tO"], m)
                d.tensor_scalar(oU[:], tO[:], 1.0, 0.5 * H_UP, ALU.add, ALU.mult).then_inc(s["l_oU"], 1)
                v.wait_ge(s["l_oU"], m)
                v.wait_ge(s["l_tC"], m)
                hi, lo = (h16[:, :, :, half].rearrange("p k b -> p (k b)") for half in range(2))
                d.tensor_tensor(hi, oU[:], tC[:], ALU.mult).then_inc(s["l_hi"], 1)
                d.tensor_tensor(h32[:], oU[:], tC[:], ALU.mult).then_inc(s["l_h32"], 1)
                v.wait_ge(s["l_h32"], m)
                d.tensor_tensor(lo, h32[:], hi, ALU.subtract).then_inc(s["l_lo"], 1)
                d.tensor_copy(cadd[:, :, 0:2], cnew[:, :, 3:4].to_broadcast([P, KD * B, 2])).then_inc(s["l_cc"], 1)
                d.tensor_copy(hs[:, :, :, i:i + 1] if isinstance(i, int) else hs[:, :, :, bass.ds(i, 1)],
                              h32[:].rearrange("p (k b o) -> p k b o", b=B, o=1)).then_inc(s["l_hs"], 1)

            def dve_out(j):
                v.wait_ge(s["o_free"], j + 1)
                v.wait_ge(s["t_XX"], B * (j + 1))
                for b in range(B):
                    v.wait_ge(s["o_T"], j * B + b + 1)
                    d.scalar_tensor_tensor(ot[:, b * D:(b + 1) * D], bank[b][:, 0:D], 1.0 / H_UP, x_tile(j, b),
                                           ALU.mult, ALU.add).then_inc(s["o_s"], 1)

            def whole(j, step):
                with v.Fori(0, B) as b:
                    base = None if step is None else v.snap(carried(j, b * GAP))
                    first = None if step is None else v.snap(b * GAP)
                    for q in range(GAP):
                        if step:
                            step(base + q, first + q)
                        dve_attention(B * j + b, q)
                at_slot = ATT

                def slot():
                    nonlocal at_slot
                    if step and at_slot < P - 1:
                        step(carried(j, at_slot), at_slot)
                    at_slot += 1

                slot()
                slot()
                dve_heads(j)
                slot()
                dve_whole(j)
                for t in range(B + 2):
                    slot()
                    dve_project(j, t)
                    if t == 4:
                        v.wait_ge(s["ld_xs"], 16 * (j + 1))
                    if t >= 4:
                        dve_dot(j, t - 4, x_tile(j, t - 4), "t_ga", "t_xa")
                for b in (2, 3):
                    slot()
                    dve_dot(j, b, x_tile(j, b), "t_ga", "t_xa")
                for _ in range(4):
                    slot()
                for b in range(B):
                    slot()
                    dve_sum(j, b, "t_w", "t_x2")
                    dve_stats(j, b)
                for _ in range(3):
                    slot()
                for b in range(B):
                    for q in range(7):
                        slot()
                        dve_hidden(B * j + b + 1, b, q)
                slot()
                v.wait_ge(s["t_sf"], j + 1)
                for b in range(B):
                    if b == 2:
                        slot()
                    v.wait_ge(s["t_r4"], B * j + b + 2)
                    d.scalar_tensor_tensor(a4[:, b], a4[:, b], num("sfw", B)[:, b:b + 1], bf2[:], ALU.mult, ALU.add).then_inc(s["t_a2"], 1)
                for b in range(B):
                    if b % 2 == 0:
                        slot()
                    dve_dot(j, b, x24[:, b], "t_ga2", "t_xa2")
                for _ in range(4):
                    slot()
                for b in range(B):
                    if b % 2 == 0:
                        slot()
                    dve_sum(j, b, "t_w2", "t_x3")
                    d.tensor_tensor(x24[:, b], x24[:, b], x_tile(j, b), ALU.add).then_inc(s["t_X"], 1)
                for _ in range(HSLOTS - 10 + 8):
                    slot()
                if step:
                    while at_slot < P - 1:
                        slot()
                    step(carried(j, P - 1), P - 1)

            v.wait_ge(s["p_kT"], NT + 1)
            q_twice(0)
            v.sem_inc(s["t_o"], 1)
            v.sem_inc(s["t_r4"], 1)
            whole(0, None)
            v.wait_ge(s["t_xc"], 2 * B)
            d.tensor_tensor(xw[:, 0], xw[:, 0], h0c[:], ALU.add).then_inc(s["l_x0"], 1)
            with v.Fori(1, NB) as j:
                whole(j, dve_step)
                dve_out(j - 1)
            with v.Fori(0, P) as i:
                dve_step((NB - 1) * P + 1 + i, i)
            dve_out(NB - 1)


_INS = ["x", "cond_1024"] + [f"L0_cond_{n}" for n in ("w_q", "b_q", "w_k", "b_k", "w_v", "b_v", "w_o", "b_o", "w_f1", "b_f1",
                                                        "w_f2", "b_f2", "w_ada", "b_ada")] + ["L1_cond_Wx", "L1_cond_Wh", "L1_cond_b"]


def kernel(**inputs):
    import numpy as _np
    import concourse.bacc as _bacc
    from concourse import mybir as _mybir
    from concourse.bass_utils import run_bass_kernel_spmd as _run

    nc = _bacc.Bacc("TRN2", target_bir_lowering=False, num_devices=1)
    arrays, args = {}, []
    for name in _INS:
        a = _np.ascontiguousarray(inputs[name])
        arrays[f"in_{name}_dram"] = a
        args.append(nc.dram_tensor(f"in_{name}_dram", a.shape, _mybir.dt.from_np(a.dtype), kind="ExternalInput").ap())
    args.append(nc.dram_tensor("out_0_dram", (B, T, D), _mybir.dt.float32, kind="ExternalOutput").ap())
    bass_hyperbolic_block_then_lstm(nc, *args)
    r = _run(nc, [arrays], core_ids=[0])
    return r.results[0]["out_0_dram"]
```

```python
import math
from contextlib import ExitStack

import numpy as np

import concourse.bass as bass
from concourse import mybir

F32 = mybir.dt.float32
F16 = mybir.dt.float16
I32 = mybir.dt.int32
ALU = mybir.AluOpType
ACT = mybir.ActivationFunctionType
AX = mybir.AxisListType

B, T, D, H, FF, P = 4, 512, 256, 16, 1024, 128
HD = D // H
KD = D // P
KF = FF // P
NB = T // P
NT = B * NB
HP = H // 2
GC = 4 * D // P

EPS, LN_EPS = 1e-7, 1e-6
MAX_TANH = float(np.float32(1.0 - 1e-5))
REACH = float(np.arctanh(np.float64(MAX_TANH)))


def _beta(a, b):
    return math.exp(math.lgamma(a) + math.lgamma(b) - math.lgamma(a + b))


HEAD = _beta(HD / 2, 0.5) / _beta(D / 2, 0.5)
TINY = 1e-30
QK_UP = 256.0
V_UP = 4096.0
H_UP = 2.0 ** 14
SERIES_BELOW = 0.01


class Chain:

    def __init__(self, eng, sem, held, per_round):
        self.eng, self.sem, self.held, self.per_round, self.base, self.n = eng, sem, held, per_round, 0, 0

    def round(self, number):
        self.base, self.n = (number - 1) * self.per_round, 0

    def link(self, ins):
        self.n += 1
        ins.then_inc(self.sem, 1)
        self.eng.wait_ge(self.sem, self.base + self.n)
        self.eng.sem_inc(self.held, 1)

    def full(self):
        assert self.n == self.per_round, (self.n, self.per_round)



NUMBERS = 1100

PAIR_SLOTS = 2 * HP
LEAD = 4
ATT = B * PAIR_SLOTS + LEAD
HEADS, HEADS_SUM, HEADS_ROOT, WHOLE, PROJECT = 0, 1, 2, 3, 4
SQUARES = PROJECT + 3
TANH, SCALE, SUM, LOG, NORM = SQUARES + 5, SQUARES + 7, SQUARES + 8, SQUARES + 13, SQUARES + 16
HIDDEN, HIDDEN_SLOTS = NORM + 2, 6
SECOND = tuple(HIDDEN + HIDDEN_SLOTS * 2 * (p + 1) for p in range(2))
GATES = (HIDDEN + HIDDEN_SLOTS * B, SECOND[1] + 6)


def bass_hyperbolic_block_then_lstm(nc, x, cond, w_q, b_q, w_k, b_k, w_v, b_v, w_o, b_o, w_f1, b_f1, w_f2, b_f2,
                                    w_ada, b_ada, w_x, w_h, b_l, out):
    ctx = ExitStack()
    with ctx:
        def sb(name, shape, dt=F32):
            return ctx.enter_context(nc.sbuf_tensor(name, shape, dt))

        def sem(name):
            return ctx.enter_context(nc.semaphore(name))

        wo = sb("wo", [P, KD, D])
        wf1 = sb("wf1", [P, KD, FF])
        wf2 = sb("wf2", [P, KF, D])
        wx = sb("wx", [P, KD, 4 * D])
        wh16 = sb("wh16", [P, 2, KD, 4 * D], F16)
        bo = sb("bo", [P, D])
        bf1 = sb("bf1", [P, FF])
        bf2 = sb("bf2", [P, D])
        blc = sb("blc", [P, GC])
        blc2 = sb("blc2", [P, GC])
        badac = sb("badac", [P, 6 * KD])
        ident = sb("ident", [P, P])
        ident16 = sb("ident16", [P, P], F16)
        ones = sb("ones", [P, P])
        adac = sb("adac", [P, 6 * KD, B])
        gates = sb("gates", [P, 2, B, D])
        cst = sb("cst", [P, 3, NT])
        xs = sb("xs", [P, 2, B, D])
        qhl = sb("qhl", [P, NT, H, 2 * HD], F16)
        kT = sb("kT", [P, B, HP, T], F16)
        vs = sb("vs", [P, B, NB, H, 2 * HD + 1], F16)
        xsq = sb("xsq", [P, NT])
        kap = sb("kap", [P, NT + 1])
        kmn = sb("kmn", [P, NT + 1])
        hs = sb("hs", [P, KD, B, P])
        arena = sb("arena", [P, 2, P * GC * B])
        xw = arena[:, :, :].rearrange("p a (t g b) -> p (a t) g b", g=GC, b=B)
        flat = arena[:, :, :].rearrange("p a n -> p (a n)")
        wada = flat[:, 0:KD * 6 * D].rearrange("p (k n) -> p k n", k=KD)
        xin = flat[:, KD * 6 * D:KD * 6 * D + (NT + 1) * D].rearrange("p (t d) -> p t d", d=D)
        weights = sb("weights", [P, 2, 2, NB, 2 * P], F16)
        wh = weights[:, :, :, :, :].rearrange("p a b c d -> p (a b c d)").bitcast(F32).rearrange("p (k n) -> p k n", k=KD)
        place = sb("place", [P, 4 * B * D])
        wqkv = place[:, 0:1536].rearrange("p (k a d) -> p k a d", k=KD, a=3)
        bqkv = place[:, 1536:2304].rearrange("p (a d) -> p a d", a=3)
        lin = place[:, 2304:3072].rearrange("p (a d) -> p a d", a=3)
        qk = place[:, 3072:3584].rearrange("p (a d) -> p a d", a=2)
        o4, a4, ga4, x24 = (place[:, i * B * D:(i + 1) * B * D].rearrange("p (b d) -> p b d", b=B) for i in range(4))
        waste = place[:, 2 * D:4 * D]
        waste2 = place[:, 0:2 * D]
        vlow = place[:, 2 * B * D:2 * B * D + D].rearrange("p (h e) -> p h e", h=H)
        tmp = sb("tmp", [P, FF])
        xn = sb("xn", [P, D])
        uT = sb("uT", [P, 2, KD, P])
        usq = sb("usq", [P, KD, P])
        fT = sb("fT", [P, KF, P])
        v32 = fT[:, 0:D // P, :].rearrange("p c t -> p (c t)").rearrange("p (h e) -> p h e", h=H)
        c0B = fT[:, :, :].rearrange("p c t -> p (c t)").rearrange("p (k b t) -> p k b t", k=KD, b=B)
        words = sb("words", [P, H * 2 * HD])
        stack = words[:].bitcast(F16).rearrange("p (h a e) -> p h a e", h=H, a=2)
        spare = words[:, 0:D]
        qbd = sb("qbd", [P, HP, 2 * P], F16)
        sc = sb("sc", [P, NUMBERS])
        c0 = xn[0:B, :]
        c0T = sb("c0T", [P, KD, B])
        h0c = sb("h0c", [P, GC, B])
        mv6 = sb("mv6", [P, 6])
        mv = sb("mv", [P, NT, 2])
        mv4 = sb("mv4", [P, B, 2])
        ot = place[:, B * D:2 * B * D]
        big1 = sb("big1", [P, 8])
        h16 = sb("h16", [P, KD, B, 2], F16)
        h32 = sb("h32", [P, KD * B])
        gA = sb("gA", [P, 48])
        gF = sb("gF", [P, 24])
        gO = sb("gO", [P, 24])
        tA = sb("tA", [P, 16])
        tO = sb("tO", [P, 8])
        oU = sb("oU", [P, 8])
        coef = sb("coef", [P, 16, 3])
        cmul = sb("cmul", [P, 8, 4])
        cadd = sb("cadd", [P, 8, 4])
        cnew = sb("cnew", [P, 8, 4])
        tC = sb("tC", [P, 8])

        psum = ctx.enter_context(nc.psum_tensor("psum", [P, 8, 512], F32))
        bank = [psum[:, i, :] for i in range(8)]
        pF, pO, pA = bank[5], bank[6], bank[7]

        def x_tile(j, b):
            return xs[:, j % 2, b, :] if isinstance(j, int) else xs[:, bass.ds(j % 2, 1), b, :].rearrange("p o d -> p (o d)")

        def tile_of(t, b):
            if isinstance(b, int):
                return t[:, b]
            part = t[:, bass.ds(b, 1)]
            return part.rearrange("p o a b c -> p (o a) b c") if len(t.shape) == 5 else part.rearrange("p o a b -> p (o a) b")

        def sums(h, n=1):
            w, at_ = 2 * HD + 1, h % (H // 2)
            return bank[2 + 2 * (h // (H // 2))][:, at_ * w:(at_ + n) * w]

        def half_words(i):
            return bank[i].bitcast(F16)

        names = """achain ada_s adap c0t c0t_s consts dinit gp gp_s h0_s h0p held hsc l_A l_F l_O l_c l_cc l_gA
            l_gF l_gO l_h32 l_hi l_hs l_ig l_init l_lo l_oU l_tA l_tC l_tF l_tO l_x l_x0 ld_b ld_c ld_h ld_w
            ld_x0 ld_x1 ld_x2 ld_x3 ld_xs ln1 ln1z lnr o_T o_d o_free o_s p_ct p_f p_fq p_vh p_vl t_S0 t_S1 t_e0 t_e1 t_l0 t_l1 p_h p_h2 p_hk p_kT p_kc p_lin p_ln p_mm p_n p_ns
            p_qk p_r p_s1 p_s2 p_sq p_ss p_su p_uT p_usq p_v p_xT p_xn pchain pk st1 t_AV t_E t_L t_S t_X
            t_XT t_XX t_Xc t_a t_a2 t_ab t_ab2 t_ar t_ar2 t_f t_f1 t_fT t_fc t_fs t_ga t_ga2 t_km t_lh t_m1
            t_m2 t_mo t_n t_n3 t_nm t_ns t_o t_oT t_oc t_op t_q t_qT t_qc t_r t_r4 t_r2 t_rh t_s1 t_s6 t_sf t_so
            t_sq t_sqf t_ss t_st t_th t_th2 t_tot t_uT t_us t_w t_w2 t_x2 t_x3 t_xT t_xa t_xa2 t_xc t_xn
            t_xw t_z vchain wmax""".split()
        s = {n: sem("s_" + n) for n in names}

        def hold(eng, name, value):
            eng.wait_ge(s[name], value)
            eng.sem_inc(s["held"], 1)

        at = {}

        def num(name, w=1):
            if name not in at:
                at[name] = (sum(v[1] for v in at.values()), w)
                assert sum(v[1] for v in at.values()) <= NUMBERS
            o, w = at[name]
            return sc[:, o:o + w]

        HALF_DOWN, HALF_UP, DOWN = 0, 1, 2

        def power(ch, dst, src, which, w):
            ch.link(nc.gpsimd.tensor_tensor(dst, src, cst[:, which, 0:w], ALU.pow))

        def to_ratio(ch, w, m, var, nsq, done):
            g = nc.gpsimd
            a, b, c = num(f"a{w}", w), num(f"b{w}", w), num(f"c{w}", w)
            nc_, nd = num(f"nc{w}", w), num(f"nd{w}", w)
            ch.link(g.tensor_tensor(a, m, m, ALU.mult))
            ch.link(g.tensor_tensor(b, a, var, ALU.add))
            ch.link(g.tensor_scalar(nsq, b, float(D), None, ALU.mult))
            power(ch, a, nsq, HALF_UP, w)
            ch.link(g.tensor_scalar(nd, a, EPS, None, ALU.max))
            ch.link(g.tensor_scalar(nc_, nd, MAX_TANH, None, ALU.min))
            ch.link(g.tensor_scalar(a, nc_, 1.0, None, ALU.add))
            ch.link(g.tensor_scalar(b, nc_, -1.0, 1.0, ALU.mult, ALU.add))
            power(ch, c, b, DOWN, w)
            g.tensor_tensor(num(f"z{w}", w), a, c, ALU.mult).then_inc(done, 1)

        def to_norm(ch, w, m, var, k_out, km_out, done):
            g = nc.gpsimd
            a, b, c = num(f"a{w}", w), num(f"b{w}", w), num(f"c{w}", w)
            nc_, nd, lam, L = num(f"nc{w}", w), num(f"nd{w}", w), num(f"lam{w}", w), num(f"L{w}", w)
            n2, ser = num(f"n2{w}", w), num(f"ser{w}", w)
            power(ch, a, nd, DOWN, w)
            ch.link(g.tensor_tensor(b, L, a, ALU.mult))
            ch.link(g.tensor_scalar(lam, b, 0.5, None, ALU.mult))
            ch.link(g.tensor_tensor(n2, nc_, nc_, ALU.mult))
            ch.link(g.tensor_scalar(ser, n2, 1.0 / 9, 1.0 / 7, ALU.mult, ALU.add))
            for term in (1.0 / 5, 1.0 / 3, 1.0):
                ch.link(g.tensor_tensor(a, ser, n2, ALU.mult))
                ch.link(g.tensor_scalar(ser, a, term, None, ALU.add))
            ch.link(g.tensor_scalar(c, n2, SERIES_BELOW, None, ALU.is_lt))
            ch.link(g.tensor_tensor(a, ser, lam, ALU.subtract))
            ch.link(g.tensor_tensor(b, a, c, ALU.mult))
            ch.link(g.tensor_tensor(a, lam, b, ALU.add))
            ch.link(g.tensor_tensor(b, a, a, ALU.mult))
            ch.link(g.tensor_tensor(c, b, var, ALU.mult))
            ch.link(g.tensor_scalar(b, c, LN_EPS, None, ALU.add))
            power(ch, c, b, HALF_DOWN, w)
            ch.link(g.tensor_tensor(b, a, c, ALU.mult))
            ch.link(g.tensor_tensor(a, b, m, ALU.mult))
            ch.link(g.tensor_copy(k_out, b))
            g.tensor_scalar(km_out, a, -1.0, None, ALU.mult).then_inc(done, 1)

        def clip(ch, dst, nsq, w, a, b, done=None):
            g = nc.gpsimd
            ch.link(g.tensor_scalar(a, nsq, TINY, None, ALU.max))
            power(ch, b, a, HALF_DOWN, w)
            last = g.tensor_scalar(dst, b, REACH, 1.0, ALU.mult, ALU.min)
            if done is None:
                ch.link(last)
            else:
                last.then_inc(done, 1)

        CHUNK = (2, 3, 4, 5, 6, 7, 0, 1)
        UNIT = (0.5,) * 4 + (1.0,) * 2 + (0.5,) * 2
        GATE_BANKS = ((pA, 4, 4, "l_A"), (pF, 0, 2, "l_F"), (pO, 2, 2, "l_O"))

        def gate_cols(bk, g0, n):
            return bk[:, g0 * 12:(g0 + n) * 12].rearrange("p (g b e) -> p g b e", b=B, e=3)

        WLOADS = 8
        BLOCK_LINKS = 105

        def carried(j, q):
            return (j - 1) * P + q + 1

        def along_attention(eng, j, step, work):
            for q in range(LEAD):
                if step:
                    step(carried(j, q), q)
                work(B * j, 0, q)
            with eng.Fori(0, B - 1) as b:
                base = None if step is None else eng.snap(carried(j, b * PAIR_SLOTS))
                first = None if step is None else eng.snap(b * PAIR_SLOTS)
                for q in range(LEAD, PAIR_SLOTS + LEAD):
                    if step:
                        step(base + q, first + q)
                    work(B * j + b, b, q)
                    if q >= PAIR_SLOTS:
                        work(B * j + b + 1, b + 1, q - PAIR_SLOTS)
            for q in range(LEAD, PAIR_SLOTS + LEAD):
                i = (B - 1) * PAIR_SLOTS + q
                if step:
                    step(carried(j, i), i)
                work(B * j + B - 1, B - 1, q)

        class Slots:

            def __init__(self, j, step):
                self.j, self.step, self.i = j, step, ATT

            def until(self, slot):
                end = min(ATT + slot, P)
                assert self.i <= end or end == P
                while self.i < end:
                    if self.step:
                        self.step(carried(self.j, self.i), self.i)
                    self.i += 1

            def rest(self):
                self.until(P)

        w32 = [t.rearrange("p (a b c) -> p a b c", a=2, b=NB // 2)
               for t in (tmp[:], fT[:, :, :].rearrange("p c t -> p (c t)"))]

        def low_weights(engine, buf, half):
            kcs = slice(half * NB // 2, (half + 1) * NB // 2)
            return engine.tensor_tensor(weights[:, buf, 1, kcs, :], w32[buf][:, half], weights[:, buf, 0, kcs, :], ALU.subtract)

        block = ctx.enter_context(nc.Block())

        @block.sync
        def _(sp):
            sp.dma_start(c0, cond).then_inc(s["ld_c"], 16)
            for j in range(NB):
                sp.dma_start(xin[:, B * j:B * (j + 1), :], x[:, j * P:(j + 1) * P, :].rearrange("b p d -> p b d")).then_inc(s[f"ld_x{j}"], 16)
            for i, w in enumerate((w_q, w_k, w_v)):
                sp.dma_start(wqkv[:, :, i, :], w.rearrange("(k p) n -> p k n", p=P)).then_inc(s["ld_w"], 16)
            sp.dma_start(wo[:], w_o.rearrange("(k p) n -> p k n", p=P)).then_inc(s["ld_w"], 16)
            sp.dma_start(wf1[:], w_f1.rearrange("(k p) n -> p k n", p=P)).then_inc(s["ld_w"], 16)
            sp.dma_start(wf2[:], w_f2.rearrange("(k p) n -> p k n", p=P)).then_inc(s["ld_w"], 16)
            sp.dma_start(wx[:], w_x.rearrange("(k p) n -> p k n", p=P)).then_inc(s["ld_w"], 16)
            sp.dma_start(blc[:], b_l.rearrange("(c p) -> p c", p=P), allow_slow_non_contiguous=True).then_inc(s["ld_w"], 16)
            for j in range(2):
                sp.dma_start(xs[:, j, :, :], x[:, j * P:(j + 1) * P, :].rearrange("b p d -> p b d")).then_inc(s["ld_xs"], 16)
            sp.sem_inc(s["o_free"], 1)

            def out_block(j):
                for b in range(B):
                    sp.wait_ge(s["o_s"], B * j + b + 1)
                    sp.dma_start(out[b, bass.ds(j * P, P), :], ot[:, b * D:(b + 1) * D]).then_inc(s["o_d"], 16)
                sp.wait_ge(s["o_d"], 16 * B * (j + 1))
                sp.sem_inc(s["o_free"], 1)

            with sp.Fori(0, NB - 2) as j:
                out_block(j)
                sp.dma_start(xs[:, bass.ds(j % 2, 1), :, :].rearrange("p o b d -> p (o b) d"),
                             x[:, bass.ds((j + 2) * P, P), :].rearrange("b p d -> p b d")).then_inc(s["ld_xs"], 16)
            with sp.Fori(NB - 2, NB) as j:
                out_block(j)
            sp.wait_ge(s["o_d"], 16 * NT)

        @block.gpsimd
        def _(pool):
            g = nc.gpsimd
            g.memset(ones[:], 1.0).then_inc(s["pchain"], 1)
            hold(pool, "pchain", 1)
            g.affine_select(out=ident[:], in_=ones[:], compare_op=ALU.is_equal, fill=0.0, base=0,
                            pattern=[[-1, P]], channel_multiplier=1).then_inc(s["pchain"], 1)
            hold(pool, "pchain", 2)
            g.tensor_copy(ident16[:], ident[:]).then_inc(s["consts"], 1)
            for i, e in enumerate((-0.5, 0.5, -1.0)):
                g.memset(cst[:, i, :], e).then_inc(s["pchain"], 1)
            hold(pool, "pchain", 5)
            ch = Chain(pool, s["pchain"], s["held"], 0)
            ch.base = 5
            hold(pool, "st1", 1)
            m16, v16 = mv[:, :, 0], mv[:, :, 1]
            to_ratio(ch, NT, m16, v16, xsq[:], s["ln1z"])
            hold(pool, "ln1z", 1)
            hold(pool, "lnr", 1)
            to_norm(ch, NT, m16, v16, kap[:, 0:NT], kmn[:, 0:NT], s["ln1"])

            ch = Chain(pool, s["hsc"], s["held"], 2)
            pool.sem_inc(s["p_v"], 1)
            ch.round(1)
            hold(pool, "p_ns", 1)
            clip(ch, num("su"), num("nu"), 1, num("ca"), num("cb"), s["p_su"])
            with pool.Fori(0, NT) as k:
                ch.round(k + 2)
                hold(pool, "p_ns", k + 2)
                clip(ch, num("su"), num("nu"), 1, num("ca"), num("cb"), s["p_su"])
                hold(pool, "p_f", k + 1)
                vh, vl = (vs[:, bass.ds(k % B, 1), bass.ds(k // B, 1), :, i * (HD + 1):i * (HD + 1) + HD].rearrange("p o r h e -> p (o r h) e")
                          for i in range(2))
                g.tensor_tensor(v32, lin[:, 2, :].rearrange("p (h e) -> p h e", e=HD),
                                num("f", 48)[:, 2 * H:3 * H].unsqueeze(2).to_broadcast([P, H, HD]), ALU.mult).then_inc(s["p_v"], 1)
                hold(pool, "p_v", k + 2)
                g.tensor_copy(vh, v32).then_inc(s["p_vh"], 1)
                hold(pool, "p_vh", k + 1)
                g.tensor_tensor(vl, v32, vh, ALU.subtract).then_inc(s["p_vl"], 1)
                ch.full()

            def mobius(ch, n, b0, b1, nsq_x, th, ar, ab):
                w = b1 - b0
                N = lambda name: num(name + "w", B)[:, b0:b1]
                nsq_x = nsq_x[:, b0:b1]
                clip(ch, N("s1"), N("n1"), w, N("ca"), N("cb"))
                ch.link(g.tensor_scalar(N("ca"), N("n2"), TINY, None, ALU.max))
                power(ch, N("n2i"), N("ca"), HALF_DOWN, w)
                ch.link(g.tensor_tensor(N("cb"), N("ca"), N("n2i"), ALU.mult))
                g.tensor_tensor(N("ar"), N("cb"), N("s1"), ALU.mult).then_inc(s[ar], 1)
                hold(pool, th, n)
                ch.link(g.tensor_tensor(N("fac"), N("th"), N("n2i"), ALU.mult))
                ch.link(g.tensor_tensor(N("y2"), N("th"), N("th"), ALU.mult))
                ch.link(g.tensor_tensor(N("xy"), N("fac"), N("xa"), ALU.mult))
                ch.link(g.tensor_scalar(N("cc"), N("xy"), 2.0, 1.0, ALU.mult, ALU.add))
                ch.link(g.tensor_tensor(N("cd"), N("cc"), N("y2"), ALU.add))
                ch.link(g.tensor_tensor(N("ca"), nsq_x, N("y2"), ALU.mult))
                ch.link(g.tensor_tensor(N("cb"), N("ca"), N("cc"), ALU.add))
                ch.link(g.tensor_scalar(N("ca"), N("cb"), EPS, None, ALU.max))
                power(ch, N("den"), N("ca"), DOWN, w)
                ch.link(g.tensor_tensor(N("al"), N("cd"), N("den"), ALU.mult))
                ch.link(g.tensor_scalar(N("cb"), nsq_x, -1.0, 1.0, ALU.mult, ALU.add))
                ch.link(g.tensor_tensor(N("cc"), N("cb"), N("fac"), ALU.mult))
                g.tensor_tensor(N("be"), N("cc"), N("den"), ALU.mult).then_inc(s[ab], 1)

            def gate_rows(ready, which, j, b0, b1, done):
                for b in range(b0, b1):
                    hold(pool, ready, B * j + b + 1)
                    g.tensor_tensor(ga4[:, b], a4[:, b], gates[:, which, b, :], ALU.mult).then_inc(s[done], 1)

            def pool_block(ch, j):
                n = j + 1
                ch.round(n)
                with pool.Fori(0, B * HP // 2) as i:
                    for odd in range(2):
                        hold(pool, "t_e0", B * HP * j + 2 * i + odd + 2)
                        low_weights(g, odd, 0).then_inc(s["t_l0"], 1)
                hold(pool, "t_rh", n)
                rh, fr = num("rh", B * H), num("fr", B * H)
                ch.link(g.tensor_scalar(fr, rh, REACH, 1.0, ALU.mult, ALU.min))
                ch.link(g.tensor_scalar(fr, fr, 1.0 / HEAD, None, ALU.mult))
                ch.link(g.tensor_tensor(num("ha", B * H), fr, fr, ALU.mult))
                g.tensor_tensor(num("hc", B * H), num("ha", B * H), num("ssh", B * H), ALU.mult).then_inc(s["t_f"], 1)
                hold(pool, "t_tot", n)
                clip(ch, num("sow", B), num("now", B), B, num("caw", B), num("cbw", B), s["t_so"])
                gate_rows("t_a", 0, j, 0, B, "t_ga")
                ch.link(g.tensor_copy(num("xqw", B), xsq[:, bass.ds(B * j, B)] if not isinstance(j, int) else xsq[:, 0:B]))
                hold(pool, "t_n", B * n)
                hold(pool, "t_xa", B * n)
                mobius(ch, n, 0, B, num("xqw", B), "t_th", "t_ar", "t_ab")
                hold(pool, "t_st", B * n)
                to_ratio(ch, B, mv4[:, :, 0], mv4[:, :, 1], num("x2q", B), s["t_z"])
                hold(pool, "t_z", n)
                hold(pool, "t_L", n)
                to_norm(ch, B, mv4[:, :, 0], mv4[:, :, 1], num("kapw", B), num("kmnw", B), s["t_km"])
                def cut_back(b):
                    hold(pool, "t_ns", B * j + b + 1)
                    c1 = slice(b, b + 1)
                    clip(ch, num("suw", B)[:, c1], num("nuw", B)[:, c1], 1, num("ca"), num("cb"), s["t_fs"])

                cut_back(0)
                cut_back(1)
                for p in range(2):
                    b0, b1 = 2 * p, 2 * p + 2
                    pair = slice(b0, b1)
                    hold(pool, "t_sqf", 2 * (B * j + b1))
                    ch.link(g.tensor_tensor(num("nfw", B)[:, pair], num("nf0w", B)[:, pair], num("nf1w", B)[:, pair], ALU.add))
                    clip(ch, num("sfw", B)[:, pair], num("nfw", B)[:, pair], 2, num("caw", B)[:, pair], num("cbw", B)[:, pair], s["t_sf"])
                    if p == 0:
                        cut_back(2)
                    gate_rows("t_a2", 1, j, b0, b1, "t_ga2")
                    hold(pool, "t_n3", B * j + b1)
                    hold(pool, "t_xa2", B * j + b1)
                    mobius(ch, 2 * j + p + 1, b0, b1, num("x2q", B), "t_th2", "t_ar2", "t_ab2")
                    if p == 0:
                        cut_back(3)
                for b in range(B):
                    hold(pool, "t_X", B * j + b + 1)
                    g.tensor_copy(x_tile(j, b), x24[:, b]).then_inc(s["t_XX"], 1)
                ch.full()

            hold(pool, "p_hk", NT)
            pool.sem_inc(s["t_l0"], 2)
            ch = Chain(pool, s["achain"], s["held"], BLOCK_LINKS)
            pool_block(ch, 0)
            with pool.Fori(1, NB) as j:
                pool_block(ch, j)

        @block.tensor
        def _(pe):
            mm, tr = nc.tensor.matmul, nc.tensor.transpose
            pe.wait_ge(s["consts"], 1)
            pe.wait_ge(s["ld_c"], 16 * 3)
            for c in range(KD):
                last = tr(bank[0][:, c * B:(c + 1) * B], c0[:, c * P:(c + 1) * P], ident[0:B, 0:B])
            last.then_inc(s["c0t"], 1)
            pe.wait_ge(s["c0t_s"], 2)
            for c in range(6 * KD):
                for kc in range(KD):
                    last = mm(bank[1][:, c * B:(c + 1) * B], wada[:, kc, c * P:(c + 1) * P], c0T[:, kc, :],
                              start=kc == 0, stop=kc == KD - 1)
            last.then_inc(s["adap"], 1)
            pe.wait_ge(s["pk"], 1)
            tr(bank[6][0:1, 0:P], big1[:, 2:3], ident[:]).then_inc(s["wmax"], 1)
            pe.wait_ge(s["pk"], 2)
            mm(bank[6][:, 256:257], ones[0:1, :], big1[0:1, 4:5], start=True, stop=True).then_inc(s["wmax"], 1)
            for which in range(2):
                for b in range(B):
                    for kc in range(KD):
                        at_ = (which * 3 + 2) * D
                        last = mm(bank[2 + 2 * which + b // 2][:, (b % 2) * D:(b % 2 + 1) * D], c0B[:, kc, b, :],
                                  wada[:, kc, at_:at_ + D], start=kc == 0, stop=kc == KD - 1, skip_group_check=True)
            last.then_inc(s["gp"], 1)

            def norm_x(k, first):
                pe.wait_ge(s["p_xn"], k + 1)
                if not first:
                    pe.wait_ge(s["p_uT"], k)
                for c in range(KD):
                    last = tr(bank[0][:, c * P:(c + 1) * P], xn[:, c * P:(c + 1) * P], ident[:])
                last.then_inc(s["p_xT"], 1)
                pe.wait_ge(s["p_usq"], k + 1)
                if not first:
                    pe.wait_ge(s["p_ns"], k)
                for c in range(KD):
                    last = mm(bank[1][:, 0:1], usq[:, c, :], ones[:, 0:1], start=c == 0, stop=c == KD - 1)
                last.then_inc(s["p_n"], 1)
                if not first:
                    pe.wait_ge(s["p_lin"], k)
                for i in range(3):
                    for kc in range(KD):
                        last = mm(bank[2 + i][:, 0:D], uT[:, 0, kc, :], wqkv[:, kc, i, :], start=kc == 0, stop=kc == KD - 1)
                last.then_inc(s["p_mm"], 1)

            pe.wait_ge(s["gp_s"], 1)
            pe.wait_ge(s["ld_w"], 16 * WLOADS)
            pe.sem_inc(s["p_kT"], 1)
            norm_x(0, True)
            pe.wait_ge(s["ld_h"], 16)
            for gi, c in enumerate(CHUNK):
                for kc in range(KD):
                    last = mm(bank[6][:, 64 + gi * B:64 + (gi + 1) * B], wh[:, kc, c * P:(c + 1) * P], c0T[:, kc, :],
                              start=kc == 0, stop=kc == KD - 1, skip_group_check=True)
            last.then_inc(s["h0p"], 1)
            with pe.Fori(0, NT) as k:
                norm_x(k + 1, False)
                pe.wait_ge(s["p_hk"], k + 1)
                pe.wait_ge(s["p_kc"], k + 1)
                for hp in range(HP):
                    last = tr(half_words(5)[:, hp * P:(hp + 1) * P],
                              stack[:, 2 * hp:2 * hp + 2, :, :].rearrange("p h a e -> p (h a e)"), ident16[:])
                last.then_inc(s["p_kT"], 1)

            def q_transposed(n):
                pe.wait_ge(s["t_q"], n)
                for hp in range(HP):
                    last = tr(half_words(3)[:, hp * P:(hp + 1) * P],
                              stack[:, 2 * hp:2 * hp + 2, :, :].rearrange("p h a e -> p (h a e)"), ident16[:])
                last.then_inc(s["t_qT"], 1)

            def scores(k, b, hp, half):
                if half == 0 and hp in (0, HP // 2):
                    pe.wait_ge(s["t_qc"], 4 * k + (2 if hp == 0 else 4))
                pe.wait_ge(s[f"t_e{half}"], HP * k + hp + 1)
                for i in range(NB // 2):
                    kc = half * (NB // 2) + i
                    last = mm(bank[half][:, i * 2 * P:(i + 1) * 2 * P],
                              tile_of(kT, b)[:, hp, kc * P:(kc + 1) * P],
                              qbd[:, hp, :], start=True, stop=True, skip_group_check=True)
                last.then_inc(s[f"t_S{half}"], 1)

            def weighted(k, b, hp):
                for half in range(2):
                    pe.wait_ge(s[f"t_l{half}"], HP * k + hp + 3)
                if hp % (HP // 2) == 0:
                    pe.wait_ge(s["t_o"], 2 * k + 1 + hp // (HP // 2))
                for e in range(2):
                    h = 2 * hp + e
                    for kc in range(NB):
                        for wl in range(2):
                            last = mm(sums(h), weights[:, hp % 2, wl, kc, e * P:(e + 1) * P], tile_of(vs, b)[:, kc, h, :],
                                      start=kc == 0 and wl == 0, stop=kc == NB - 1 and wl == 1, skip_group_check=True)
                last.then_inc(s["t_AV"], 1)

            def pe_attention(k, b, q):
                hp = q // 2
                if hp < HP:
                    scores(k, b, hp, q % 2)
                if q % 2 == 0 and hp >= 2:
                    weighted(k, b, hp - 2)
                if q == LEAD + 1:
                    pe.wait_ge(s["t_qc"], 4 * (k + 1))
                    q_transposed(k + 2)

            def pe_project(j, t):
                if 1 <= t <= B:
                    b = t - 1
                    pe.wait_ge(s["t_op"], B * j + b + 1)
                    if b >= 2:
                        pe.wait_ge(s["t_oc"], B * j + b - 1)
                    for c in range(KD):
                        last = tr(bank[b % 2][:, c * P:(c + 1) * P], ga4[:, b, c * P:(c + 1) * P], ident[:])
                    last.then_inc(s["t_oT"], 1)
                if 2 <= t <= B + 1:
                    b = t - 2
                    pe.wait_ge(s["t_oc"], B * j + b + 1)
                    if b == 0:
                        pe.wait_ge(s["t_qc"], 4 * (B * j + B + 1))
                    if b >= 2:
                        pe.wait_ge(s["t_a"], B * j + b - 1)
                    for kc in range(KD):
                        last = mm(bank[3 + b % 2][:, 0:D], uT[:, b % 2, kc, :], wo[:, kc, :], start=kc == 0, stop=kc == KD - 1)
                    last.then_inc(s["t_mo"], 1)

            def pe_norm(n):
                pe.wait_ge(s["t_xn"], n)
                for c in range(KD):
                    last = tr(bank[0][:, c * P:(c + 1) * P], xn[:, c * P:(c + 1) * P], ident[:])
                last.then_inc(s["t_xT"], 1)

            def pe_hidden(n, q, more):
                if q == 0:
                    pe.wait_ge(s["t_us"], n)
                    for c in range(KD):
                        last = mm(bank[2][:, 0:1], usq[:, c, :], ones[:, 0:1], start=c == 0, stop=c == KD - 1)
                    last.then_inc(s["t_nm"], 1)
                if q in (2, 4):
                    half = q // 2 - 1
                    pe.wait_ge(s["t_f1"], 2 * n - 1 + half)
                    for c in range(KF // 2):
                        cc = half * (KF // 2) + c
                        last = tr(bank[2 + half][:, c * P:(c + 1) * P], tmp[:, cc * P:(cc + 1) * P], ident[:])
                    last.then_inc(s["t_fT"], 1)
                for part in ((0,), (1, 2), (3,), (), (), ())[q]:
                    half, kc = part // 2, part % 2
                    last = mm(bank[half][:, :], uT[:, 0, kc, :], wf1[:, kc, half * 512:(half + 1) * 512],
                              start=kc == 0, stop=kc == KD - 1)
                    if kc == KD - 1:
                        last.then_inc(s["t_m1"], 1)
                if q == 3:
                    pe.wait_ge(s["t_fc"], 2 * n - 1)
                    pe.wait_ge(s["t_r4"], n)
                for kc in ((), (), (), (0, 1, 2), (3,), (4, 5, 6, 7))[q]:
                    if kc == KF // 2:
                        pe.wait_ge(s["t_fc"], 2 * n)
                    last = mm(bank[4][:, 0:D], fT[:, kc, :], wf2[:, kc, :], start=kc == 0, stop=kc == KF - 1)
                if q == 3 and more:
                    pe_norm(n + 1)
                if q == 5:
                    last.then_inc(s["t_m2"], 1)

            def pe_gates_T(n, b):
                pe.wait_ge(s["t_X"], n)
                for c in range(KD):
                    last = tr(bank[4][:, c * P:(c + 1) * P], x24[:, b, c * P:(c + 1) * P], ident[:])
                last.then_inc(s["t_XT"], 1)

            def pe_gates(j, b, half):
                n = B * j + b + 1
                if half == 0:
                    pe.wait_ge(s["t_Xc"], n)
                if b >= 2:
                    pe.wait_ge(s["t_xc"], 2 * (n - 2) - 1 + half)
                for gi in range(GC // 2):
                    c = CHUNK[half * (GC // 2) + gi]
                    for kc in range(KD):
                        last = mm(bank[half + 2 * (b % 2)][:, gi * P:(gi + 1) * P], wx[:, kc, c * P:(c + 1) * P], uT[:, b % 2, kc, :],
                                  start=kc == 0, stop=kc == KD - 1, skip_group_check=True)
                last.then_inc(s["t_xw"], 1)
                if half == 1 and b % 2 == 0:
                    pe_gates_T(n + 1, b + 1)

            def pe_step(m, i):
                pe.wait_ge(s["l_lo"], m)
                pe.wait_ge(s["l_x"], m)
                for bk, g0, ng, made in GATE_BANKS:
                    for gi in range(ng):
                        for kc in range(KD):
                            for half in range(2):
                                last = mm(gate_cols(bk, gi, 1)[:, 0, :, 0:2],
                                          wh16[:, half, kc, (g0 + gi) * P:(g0 + gi + 1) * P], h16[:, kc, :, :],
                                          start=gi == 0 and kc == 0 and half == 0, stop=gi == ng - 1 and kc == KD - 1 and half == 1,
                                          skip_group_check=True)
                    last.then_inc(s[made], 1)

            def pe_out(j):
                pe.wait_ge(s["l_hs"], P * (j + 1))
                for b in range(B):
                    for kc in range(KD):
                        last = tr(bank[b][:, kc * P:(kc + 1) * P], hs[:, kc, b, :], ident[:])
                    last.then_inc(s["o_T"], 1)
                pe.wait_ge(s["o_s"], B * (j + 1))

            pe.wait_ge(s["p_kc"], NT + 1)
            pe.wait_ge(s["p_vl"], NT)
            pe.wait_ge(s["l_init"], 2)
            q_transposed(1)

            def whole(j, step):
                along_attention(pe, j, step, pe_attention)
                at = Slots(j, step)
                for t in range(B + 2):
                    at.until(PROJECT + t)
                    pe_project(j, t)
                at.until(NORM + 1)
                pe_norm(B * j + 1)
                for b in range(B):
                    for q in range(HIDDEN_SLOTS):
                        at.until(HIDDEN + b * HIDDEN_SLOTS + q)
                        pe_hidden(B * j + b + 1, q, b < B - 1)
                for p in range(2):
                    at.until(GATES[p])
                    if p == 0:
                        pe.wait_ge(s["t_r4"], B * (j + 1) + 1)
                    pe_gates_T(B * j + 2 * p + 1, 2 * p)
                    for i in range(4):
                        at.until(GATES[p] + 1 + i)
                        pe_gates(j, 2 * p + i // 2, i % 2)
                pe.wait_ge(s["t_xc"], 2 * B * (j + 1))
                at.rest()

            pe.sem_inc(s["t_AV"], 2)
            whole(0, None)
            with pe.Fori(1, NB) as j:
                whole(j, pe_step)
                pe_out(j - 1)
            with pe.Fori((NB - 1) * P + 1, NB * P + 1) as m:
                pe_step(m, None)
            pe_out(NB - 1)

        @block.scalar
        def _(act):
            A = nc.scalar.activation
            act.dma_start(wada, w_ada.rearrange("(k p) n -> p k n", p=P)).then_inc(s["ld_c"], 16)
            act.dma_start(badac[:], b_ada.rearrange("(c p) -> p c", p=P), allow_slow_non_contiguous=True).then_inc(s["ld_c"], 16)
            act.dma_start(wh, w_h.rearrange("(k p) n -> p k n", p=P)).then_inc(s["ld_h"], 16)
            for i, bias in enumerate((b_q, b_k, b_v)):
                act.dma_start(bqkv[:, i, :], bias.partition_broadcast(P)).then_inc(s["ld_b"], 16)
            act.dma_start(bo[:], b_o.partition_broadcast(P)).then_inc(s["ld_b"], 16)
            act.dma_start(bf1[:], b_f1.partition_broadcast(P)).then_inc(s["ld_b"], 16)
            act.dma_start(bf2[:], b_f2.partition_broadcast(P)).then_inc(s["ld_b"], 16)
            for which in range(2):
                at_ = (which * 3 + 2) * D
                for b in range(B):
                    act.dma_start(gates[:, which, b, :], b_ada[at_:at_ + D].partition_broadcast(P)).then_inc(s["ld_b"], 16)
            nc.scalar.preload_act_table_set("natural_log_exp_and_others")
            act.wait_ge(s["ln1z"], 1)
            A(num(f"L{NT}", NT), num(f"z{NT}", NT), ACT.Ln).then_inc(s["lnr"], 1)

            def norm_x(k, b, first):
                if not first:
                    act.wait_ge(s["p_xT"], k)
                A(xn[:], xin[:, bass.ds(k, 1), :].rearrange("p o d -> p (o d)") if not first else xin[:, 0, :], ACT.Identity,
                  scale=kap[:, bass.ds(k, 1)] if not first else kap[:, 0:1],
                  bias=kmn[:, bass.ds(k, 1)] if not first else kmn[:, 0:1]).then_inc(s["p_xn"], 1)
                act.wait_ge(s["p_xT"], k + 1)
                for c in range(KD):
                    last = A(uT[:, 0, c, :], bank[0][:, c * P:(c + 1) * P], ACT.Identity,
                             scale=adac[:, KD + c, bass.ds(b, 1)] if not first else adac[:, KD + c, 0:1],
                             bias=adac[:, c, bass.ds(b, 1)] if not first else adac[:, c, 0:1])
                last.then_inc(s["p_uT"], 1)
                act.wait_ge(s["p_uT"], k + 1)
                A(usq[:, :, :], uT[:, 0, :, :], ACT.Square).then_inc(s["p_usq"], 1)

            act.wait_ge(s["ln1"], 1)
            act.wait_ge(s["ada_s"], 1)
            act.sem_inc(s["p_kc"], 1)
            norm_x(0, 0, True)
            with act.Fori(0, NT) as k:
                act.wait_ge(s["p_lin"], k + 1)
                A(tmp[:, 0:3 * D], lin[:, :, :].rearrange("p a d -> p (a d)"), ACT.Square).then_inc(s["p_sq"], 1)
                norm_x(k + 1, (k + 1) % B, False)
                act.wait_ge(s["p_ss"], k + 1)
                A(num("lss", 51), num("ss", 51), ACT.Ln).then_inc(s["p_ln"], 1)
                act.wait_ge(s["p_ln"], k + 1)
                A(num("rss", 51), num("lss", 51), ACT.Exp, scale=-0.5).then_inc(s["p_r"], 1)
                act.wait_ge(s["p_kT"], k + 2)
                A(kT[:, bass.ds(k % B, 1), :, bass.ds(k // B * P, P)].rearrange("p o h t -> p (o h) t"),
                  half_words(5)[:, 0:HP * P].rearrange("p (h t) -> p h t", h=HP), ACT.Copy).then_inc(s["p_kc"], 1)

            def q_blocks(n, e, part):
                act.wait_ge(s["t_qT"], n)
                r, pairs = slice(64 * e, 64 * e + 64), slice(part * HP // 2, (part + 1) * HP // 2)
                A(qbd[r, pairs, e * P:(e + 1) * P],
                  half_words(3)[r, 0:HP * P].rearrange("p (h t) -> p h t", h=HP)[:, pairs, :], ACT.Copy).then_inc(s["t_qc"], 1)

            def exps(k, hp, half):
                n = HP * k + hp + 1
                if half == 0:
                    act.wait_ge(s["t_AV"], n)
                act.wait_ge(s[f"t_l{half}"], n)
                act.wait_ge(s[f"t_S{half}"], n)
                for dst in (w32[hp % 2][:, half], weights[:, hp % 2, 0, half * NB // 2:(half + 1) * NB // 2, :]):
                    last = A(dst.rearrange("p a b -> p (a b)"), bank[half], ACT.Exp, scale=1.0 / (math.sqrt(HD) * QK_UP * QK_UP))
                last.then_inc(s[f"t_e{half}"], 1)

            def act_attention(k, b, q):
                if q % 2 == 1 and q // 2 < HP:
                    exps(k, q // 2, 0)
                if q % 2 == 0 and 1 <= q // 2 <= HP:
                    exps(k, q // 2 - 1, 1)
                if q in (HP + 2, HP + 3):
                    q_blocks(k + 2, q - HP - 2, 0)
                if q in (PAIR_SLOTS + 1, PAIR_SLOTS + 2):
                    q_blocks(k + 2, q - PAIR_SLOTS - 1, 1)

            def act_heads(j):
                act.wait_ge(s["t_o"], 2 * B * (j + 1) + 2)
                A(tmp[:], o4[:, :, :].rearrange("p b d -> p (b d)"), ACT.Square).then_inc(s["t_sq"], 1)

            def act_heads2(j):
                hold(act, "t_ss", j + 1)
                nc.scalar.preload_act_table_set("natural_log_exp_and_others")
                A(num("lh", B * H), num("mh", B * H), ACT.Ln).then_inc(s["t_lh"], 1)
                act.wait_ge(s["t_lh"], j + 1)
                A(num("rh", B * H), num("lh", B * H), ACT.Exp, scale=-0.5).then_inc(s["t_rh"], 1)
                nc.scalar.preload_act_table_set("exp_and_others")

            def act_project(j, t):
                if 1 <= t <= B:
                    b = t - 1
                    act.wait_ge(s["t_oT"], B * j + b + 1)
                    if b >= 2:
                        act.wait_ge(s["t_mo"], B * j + b - 1)
                    A(uT[:, b % 2, :, :].rearrange("p c t -> p (c t)"), bank[b % 2][:, 0:D], ACT.Copy).then_inc(s["t_oc"], 1)

            def act_squares(j, b, ready, ready_g, done):
                if b > 0:
                    act.wait_ge(s[done], B * j + b)
                act.wait_ge(s[ready], B * j + b + 1)
                A(waste2[:, 0:D], a4[:, b], ACT.Square, accum_out=num("n1w", B)[:, b:b + 1])
                act.wait_ge(s[ready_g], B * j + b + 1)
                A(waste2[:, D:2 * D], ga4[:, b], ACT.Square, accum_out=num("n2w", B)[:, b:b + 1]).then_inc(s[done], 1)

            def act_tanh(n, b0, b1, ready, done):
                act.wait_ge(s[ready], n)
                A(num("thw", B)[:, b0:b1], num("arw", B)[:, b0:b1], ACT.Tanh).then_inc(s[done], 1)

            def act_scaled(n, b, ready, src, done):
                act.wait_ge(s[ready], n)
                A(x24[:, b], src, ACT.Copy, scale=num("alw", B)[:, b:b + 1]).then_inc(s[done], 1)

            def act_log(j):
                act.wait_ge(s["t_z"], j + 1)
                A(num(f"L{B}", B), num(f"z{B}", B), ACT.Ln).then_inc(s["t_L"], 1)
                nc.scalar.preload_act_table_set("exp_and_others")

            def act_norm(n, b):
                A(xn[:], x24[:, b], ACT.Identity, scale=num("kapw", B)[:, b:b + 1], bias=num("kmnw", B)[:, b:b + 1]).then_inc(s["t_xn"], 1)

            def act_norm2(n, b):
                act.wait_ge(s["t_xT"], n)
                for c in range(KD):
                    last = A(uT[:, 0, c, :], bank[0][:, c * P:(c + 1) * P], ACT.Identity,
                             scale=adac[:, 4 * KD + c, b:b + 1], bias=adac[:, 3 * KD + c, b:b + 1])
                last.then_inc(s["t_uT"], 1)
                act.wait_ge(s["t_uT"], n)
                A(usq[:, :, :], uT[:, 0, :, :], ACT.Square).then_inc(s["t_us"], 1)

            def f1_square(n, b, half):
                if b > 0 or half > 0:
                    act.wait_ge(s["t_sqf"], 2 * (n - 1) + half)
                act.wait_ge(s["t_f1"], 2 * n - 1 + half)
                A(waste, tmp[:, half * 512:(half + 1) * 512], ACT.Square,
                  accum_out=num(f"nf{half}w", B)[:, b:b + 1]).then_inc(s["t_sqf"], 1)

            def f1_columns(n, half):
                act.wait_ge(s["t_fT"], 2 * n - 1 + half)
                A(fT[:, half * (KF // 2):(half + 1) * (KF // 2), :].rearrange("p c t -> p (c t)"), bank[2 + half],
                  ACT.Copy).then_inc(s["t_fc"], 1)

            def act_hidden(n, b, q, more):
                if q == 2:
                    if more:
                        act_norm(n + 1, b + 1)
                    f1_columns(n, 0)
                if q == 3:
                    f1_square(n, b, 0)
                if q == 4:
                    f1_square(n, b, 1)
                    f1_columns(n, 1)
                if q == 5 and more:
                    act_norm2(n + 1, b + 1)

            def act_gates_T(n, b):
                act.wait_ge(s["t_XT"], n)
                A(uT[:, b % 2, :, :].rearrange("p c t -> p (c t)"), bank[4][:, 0:D], ACT.Copy).then_inc(s["t_Xc"], 1)

            def act_gates(j, b, half):
                n = B * j + b + 1
                act.wait_ge(s["t_xw"], 2 * n - 1 + half)
                for gi in range(GC // 2):
                    gg = half * (GC // 2) + gi
                    dst = (xw[:, bass.ds(j % 2 * P, P), gg, b] if not isinstance(j, int) else xw[:, 0:P, gg, b])
                    last = A(dst, bank[half + 2 * (b % 2)][:, gi * P:(gi + 1) * P], ACT.Identity, scale=UNIT[gg], bias=blc2[:, gg:gg + 1])
                last.then_inc(s["t_xc"], 1)
                if half == 1 and b % 2 == 0:
                    act_gates_T(n + 1, b + 1)

            def put_xw(i):
                two = psum[:, 5:7, 0:24].rearrange("p a (c e) -> p a c e", e=3)[:, :, :, 2]
                if isinstance(i, int):
                    fo, gi_ = xw[:, i, 0:4, :], xw[:, i, 4:8, :]
                else:
                    fo, gi_ = (xw[:, bass.ds(i, 1), a:a + 4, :].rearrange("p o g b -> p (o g) b") for a in (0, 4))
                A(two, fo.rearrange("p (a c) b -> p a (c b)", a=2), ACT.Copy)
                A(gate_cols(pA, 0, 4)[:, :, :, 2].rearrange("p g b -> p (g b)"), gi_.rearrange("p g b -> p (g b)"), ACT.Copy).then_inc(s["l_x"], 1)

            def act_step(m, i):
                act.wait_ge(s["l_gA"], m)
                A(tA[:], gA[:].rearrange("p (c e) -> p e c", e=3)[:, 2], ACT.Tanh).then_inc(s["l_tA"], 1)
                act.wait_ge(s["l_gF"], m)
                A(cmul[:, :, 1], gF[:].rearrange("p (c e) -> p e c", e=3)[:, 2], ACT.Tanh).then_inc(s["l_tF"], 1)
                act.wait_ge(s["l_gO"], m)
                A(tO[:], gO[:].rearrange("p (c e) -> p e c", e=3)[:, 2], ACT.Tanh).then_inc(s["l_tO"], 1)
                act.wait_ge(s["l_c"], m)
                A(tC[:], cnew[:, :, 3], ACT.Tanh).then_inc(s["l_tC"], 1)
                put_xw(m % (2 * P))

            act.wait_ge(s["l_init"], 2)
            for part in range(2):
                for e in range(2):
                    q_blocks(1, e, part)
            act.sem_inc(s["t_e0"], 1)
            act.sem_inc(s["t_e1"], 1)
            nc.scalar.preload_act_table_set("exp_and_others")

            def whole(j, step):
                along_attention(act, j, step, act_attention)
                at = Slots(j, step)
                at.until(HEADS)
                act_heads(j)
                at.until(HEADS_ROOT)
                act_heads2(j)
                for t in range(1, B + 4):
                    at.until(PROJECT + t)
                    act_project(j, t)
                    if PROJECT + t >= SQUARES and PROJECT + t - SQUARES < B:
                        act_squares(j, PROJECT + t - SQUARES, "t_a", "t_ga", "t_n")
                at.until(TANH)
                act_tanh(j + 1, 0, B, "t_ar", "t_th")
                for b in range(B):
                    at.until(SCALE + b // 2)
                    act_scaled(j + 1, b, "t_ab", x_tile(j, b), "t_w")
                at.until(LOG)
                act_log(j)
                at.until(NORM)
                act.wait_ge(s["t_km"], j + 1)
                act_norm(B * j + 1, 0)
                at.until(NORM + 1)
                act_norm2(B * j + 1, 0)

                def second(p, slot):
                    n, b0 = 2 * j + p + 1, 2 * p
                    if slot in (1, 2):
                        act_squares(j, b0 + slot - 1, "t_a2", "t_ga2", "t_n3")
                    if slot == 4:
                        act_tanh(n, b0, b0 + 2, "t_ar2", "t_th2")
                    if slot == 6:
                        for b in (b0, b0 + 1):
                            act_scaled(n, b, "t_ab2", x24[:, b], "t_w2")

                for b in range(B):
                    for q in range(HIDDEN_SLOTS):
                        slot = HIDDEN + b * HIDDEN_SLOTS + q
                        at.until(slot)
                        act_hidden(B * j + b + 1, b, q, b < B - 1)
                        second(0, slot - SECOND[0])
                for slot in range(GATES[0], GATES[1] + 5):
                    at.until(slot)
                    second(1, slot - SECOND[1])
                    for p in range(2):
                        i = slot - GATES[p]
                        if i == 0:
                            act_gates_T(B * j + 2 * p + 1, 2 * p)
                        if 1 <= i <= 4:
                            act_gates(j, 2 * p + (i - 1) // 2, (i - 1) % 2)
                at.rest()

            whole(0, None)
            act.wait_ge(s["l_x0"], 1)
            put_xw(0)
            with act.Fori(1, NB) as j:
                whole(j, act_step)
            with act.Fori((NB - 1) * P + 1, NB * P + 1) as m:
                act_step(m, None)

        @block.vector
        def _(v):
            d = nc.vector
            d.memset(qbd[:], 0.0).then_inc(s["l_init"], 1)
            d.memset(vs[:, :, :, :, HD:HD + 1], V_UP).then_inc(s["l_init"], 1)
            d.memset(h16[:], 0.0).then_inc(s["l_lo"], 1)
            d.memset(coef[:, :, 0], 0.0).then_inc(s["dinit"], 1)
            d.memset(coef[:, :, 1], 1.0).then_inc(s["dinit"], 1)
            d.memset(cmul[:, :, 0], 0.0).then_inc(s["dinit"], 1)
            d.memset(cmul[:, :, 2], 1.0).then_inc(s["dinit"], 1)
            d.memset(cmul[:, :, 3], 0.5).then_inc(s["dinit"], 1)
            d.memset(cadd[:], 0.0).then_inc(s["dinit"], 1)
            d.memset(xin[:, NT, :], 0.0).then_inc(s["dinit"], 1)
            d.memset(kap[:, NT:], 0.0).then_inc(s["dinit"], 1)
            d.memset(kmn[:, NT:], 0.0).then_inc(s["dinit"], 1)
            v.wait_ge(s["dinit"], 9)
            for k in range(NT):
                if k % B == 0:
                    v.wait_ge(s[f"ld_x{k // B}"], 16)
                d.bn_stats(mv6[:], xin[:, k, :]).then_inc(s["vchain"], 1)
                v.wait_ge(s["vchain"], 2 * k + 1)
                d.bn_aggr(mv[:, k, :], mv6[:]).then_inc(s["vchain"], 1)
                v.wait_ge(s["vchain"], 2 * k + 2)
            d.memset(num("one"), 1.0).then_inc(s["st1"], 1)
            nv = 2 * NT

            def link(ins):
                nonlocal nv
                nv += 1
                ins.then_inc(s["vchain"], 1)
                v.wait_ge(s["vchain"], nv)

            v.wait_ge(s["c0t"], 1)
            d.tensor_copy(c0T[:], bank[0][:, 0:KD * B].rearrange("p (k b) -> p k b", b=B)).then_inc(s["c0t_s"], 1)
            v.wait_ge(s["c0t_s"], 1)
            d.tensor_copy(c0B, c0T[:].unsqueeze(3).to_broadcast([P, KD, B, P])).then_inc(s["c0t_s"], 1)
            v.wait_ge(s["ld_h"], 16)
            link(d.tensor_reduce(big1[:, 0:1], wh, axis=AX.XY, op=ALU.max))
            link(d.tensor_reduce(big1[:, 1:2], wh, axis=AX.XY, op=ALU.min))
            link(d.tensor_scalar(big1[:, 3:4], big1[:, 1:2], -1.0, 2.0 ** -100, ALU.mult, ALU.max))
            d.tensor_tensor(big1[:, 2:3], big1[:, 0:1], big1[:, 3:4], ALU.max).then_inc(s["pk"], 1)
            v.wait_ge(s["adap"], 1)
            link(d.tensor_tensor(adac[:], bank[1][:, 0:6 * KD * B].rearrange("p (c b) -> p c b", b=B),
                                 badac[:].unsqueeze(2).to_broadcast([P, 6 * KD, B]), ALU.add))
            for c in (KD, 4 * KD):
                last = d.tensor_scalar(adac[:, c:c + KD, :], adac[:, c:c + KD, :], 1.0, None, ALU.add)
            last.then_inc(s["ada_s"], 1)
            v.wait_ge(s["wmax"], 1)
            link(d.tensor_reduce(big1[0:1, 5:6], bank[6][0:1, 0:P], axis=AX.X, op=ALU.max))
            d.tensor_scalar(big1[0:1, 4:5].bitcast(I32), big1[0:1, 5:6].bitcast(I32), 0x7F800000, None, ALU.bitwise_and).then_inc(s["pk"], 1)
            v.wait_ge(s["wmax"], 2)
            link(d.tensor_copy(big1[:, 6:7], bank[6][:, 256:257]))
            link(d.reciprocal(big1[:, 7:8], big1[:, 6:7]))
            link(d.tensor_scalar(coef[:, :, 2], coef[:, :, 1], big1[:, 6:7], 1.0 / (H_UP * 2.0 ** 14), ALU.mult, ALU.mult))
            link(d.tensor_scalar(big1[:, 6:7], big1[:, 7:8], 2.0 ** 14, None, ALU.mult))
            for g0 in range(GC):
                c = CHUNK[g0]
                src, w = wh[:, :, c * P:(c + 1) * P], tmp[:, 0:KD * P].rearrange("p (k n) -> p k n", k=KD)
                hi, lo = (wh16[:, half, :, g0 * P:(g0 + 1) * P] for half in range(2))
                link(d.tensor_scalar(w, src, big1[:, 6:7], UNIT[g0], ALU.mult, ALU.mult))
                link(d.tensor_copy(hi, w))
                link(d.tensor_tensor(lo, w, hi, ALU.subtract))
            v.wait_ge(s["gp"], 1)
            v.wait_ge(s["ld_b"], 16 * 14)
            for which in range(2):
                for b in range(B):
                    last = d.tensor_tensor(gates[:, which, b, :], bank[2 + 2 * which + b // 2][:, (b % 2) * D:(b % 2 + 1) * D],
                                           gates[:, which, b, :], ALU.add)
            last.then_inc(s["gp_s"], 1)
            v.wait_ge(s["p_n"], 1)
            d.tensor_copy(num("nu"), bank[1][:, 0:1]).then_inc(s["p_ns"], 1)
            with v.Fori(0, NT) as k:
                n = k + 1
                v.wait_ge(s["p_mm"], n)
                v.wait_ge(s["p_v"], n)
                v.wait_ge(s["p_su"], n)
                for i in range(3):
                    last = d.scalar_tensor_tensor(lin[:, i, :], bank[2 + i][:, 0:D], num("su"), bqkv[:, i, :], ALU.mult, ALU.add)
                last.then_inc(s["p_lin"], 1)
                v.wait_ge(s["p_sq"], n)
                d.tensor_reduce(num("ssr", 48), tmp[:, 0:3 * D].rearrange("p (h e) -> p h e", e=HD), axis=AX.X, op=ALU.add).then_inc(s["p_s1"], 1)
                v.wait_ge(s["p_s1"], n)
                d.tensor_reduce(num("tot", 3), num("ssr", 48).rearrange("p (a h) -> p a h", a=3), axis=AX.X, op=ALU.add).then_inc(s["p_s2"], 1)
                d.tensor_scalar(num("ss", 51)[:, 0:48], num("ssr", 48), 1.0, None, ALU.max)
                v.wait_ge(s["p_s2"], n)
                d.tensor_scalar(num("ss", 51)[:, 48:51], num("tot", 3), 1.0, None, ALU.max).then_inc(s["p_ss"], 1)
                v.wait_ge(s["p_n"], n + 1)
                d.tensor_copy(num("nu"), bank[1][:, 0:1]).then_inc(s["p_ns"], 1)
                v.wait_ge(s["p_r"], n)
                d.tensor_scalar(num("ct", 3), num("rss", 51)[:, 48:51], REACH * HEAD, HEAD, ALU.mult, ALU.min).then_inc(s["p_ct"], 1)
                v.wait_ge(s["p_ct"], n)
                for i in range(3):
                    last = d.tensor_scalar(num("f", 48)[:, i * H:(i + 1) * H], num("rss", 51)[:, i * H:(i + 1) * H],
                                           REACH, num("ct", 3)[:, i:i + 1], ALU.mult, ALU.min)
                last.then_inc(s["p_fq"], 1)
                v.wait_ge(s["p_fq"], n)
                d.tensor_scalar(num("f", 48)[:, 2 * H:3 * H], num("f", 48)[:, 2 * H:3 * H], V_UP, None, ALU.mult).then_inc(s["p_f"], 1)
                v.wait_ge(s["p_f"], n)
                for i in range(2):
                    last = d.scalar_tensor_tensor(qk[:, i, :].rearrange("p (h e) -> p h e", e=HD), lin[:, i, :].rearrange("p (h e) -> p h e", e=HD),
                                                  QK_UP, num("f", 48)[:, i * H:(i + 1) * H].unsqueeze(2).to_broadcast([P, H, HD]), ALU.mult, ALU.mult)
                last.then_inc(s["p_qk"], 1)
                v.wait_ge(s["p_kT"], n)
                v.wait_ge(s["p_qk"], n)
                q3, k3 = (qk[:, i, :].rearrange("p (h e) -> p h e", e=HD) for i in range(2))
                qh, ql = (qhl[:, bass.ds(k, 1), :, i * HD:(i + 1) * HD].rearrange("p o h e -> p (o h) e") for i in range(2))
                kh, kl = stack[:, :, 0, :], stack[:, :, 1, :]
                d.tensor_copy(qh, q3)
                d.tensor_copy(kh[:, :, 0:HD], k3).then_inc(s["p_h"], 1)
                v.wait_ge(s["p_h"], n)
                d.tensor_tensor(ql, q3, qh, ALU.subtract)
                d.tensor_tensor(kl[:, :, 0:HD], k3, kh[:, :, 0:HD], ALU.subtract).then_inc(s["p_h2"], 1)
                d.tensor_copy(kh[:, :, HD:2 * HD], kh[:, :, 0:HD])
                v.wait_ge(s["p_h2"], n)
                d.tensor_copy(kl[:, :, HD:2 * HD], kl[:, :, 0:HD]).then_inc(s["p_hk"], 1)

            v.wait_ge(s["ld_w"], 16 * WLOADS)
            v.wait_ge(s["h0p"], 1)
            for g0 in range(GC):
                d.tensor_scalar(h0c[:, g0, :], bank[6][:, 64 + g0 * B:64 + (g0 + 1) * B], UNIT[g0], None, ALU.mult)
                last = d.tensor_scalar(blc2[:, g0:g0 + 1], blc[:, CHUNK[g0]:CHUNK[g0] + 1], UNIT[g0], None, ALU.mult)
            last.then_inc(s["h0_s"], 1)

            def q_twice(k):
                for dup in range(2):
                    last = d.tensor_copy(stack[:, :, dup, :], qhl[:, bass.ds(k, 1), :, :].rearrange("p o h e -> p (o h) e"))
                last.then_inc(s["t_q"], 1)

            def dve_attention(k, b, q):
                if q % 2 == 1 and 1 <= q // 2 <= HP:
                    hp = q // 2 - 1
                    v.wait_ge(s["t_e1"], HP * k + hp + 2)
                    low_weights(d, hp % 2, 1).then_inc(s["t_l1"], 1)
                if q == LEAD:
                    v.wait_ge(s["t_qT"], k + 1)
                    q_twice((k + 1) % NT)
                for half in range(2):
                    if q == (PAIR_SLOTS // 2 + LEAD + 2, PAIR_SLOTS + LEAD - 1)[half]:
                        normalize(k, b, half)

            def normalize(k, b, half):
                heads = slice(half * H // 2, (half + 1) * H // 2)
                three = sums(half * H // 2, H // 2).rearrange("p (h e) -> p h e", e=2 * HD + 1)
                o3 = (o4[:, b] if isinstance(b, int) else o4[:, bass.ds(b, 1), :].rearrange("p o d -> p (o d)")).rearrange("p (h e) -> p h e", e=HD)
                v.wait_ge(s["t_AV"], HP * k + (half + 1) * HP // 2 + 2)
                d.reciprocal(num("rd", H)[:, heads], three[:, :, HD])
                d.tensor_copy(vlow[:, heads, :], three[:, :, HD + 1:]).then_inc(s["t_r"], 1)
                v.wait_ge(s["t_r"], 2 * k + half + 1)
                d.tensor_tensor(vlow[:, heads, :], three[:, :, 0:HD], vlow[:, heads, :], ALU.add).then_inc(s["t_r2"], 1)
                v.wait_ge(s["t_r2"], 2 * k + half + 1)
                d.tensor_tensor(o3[:, heads, :], vlow[:, heads, :], num("rd", H)[:, heads].unsqueeze(2).to_broadcast([P, H // 2, HD]),
                                ALU.mult).then_inc(s["t_o"], 1)

            def dve_heads(j):
                v.wait_ge(s["t_sq"], j + 1)
                d.tensor_reduce(num("ssh", B * H), tmp[:].rearrange("p (h e) -> p h e", e=HD), axis=AX.X, op=ALU.add).then_inc(s["t_s1"], 1)
                v.wait_ge(s["t_s1"], j + 1)
                d.tensor_scalar(num("mh", B * H), num("ssh", B * H), 1.0, None, ALU.max).then_inc(s["t_ss"], 1)

            def dve_whole(j):
                v.wait_ge(s["t_f"], j + 1)
                d.tensor_reduce(num("now", B), num("hc", B * H).rearrange("p (b h) -> p b h", b=B), axis=AX.X, op=ALU.add).then_inc(s["t_tot"], 1)

            def dve_project(j, t):
                if t < B:
                    d.tensor_tensor(ga4[:, t].rearrange("p (h e) -> p h e", e=HD), o4[:, t].rearrange("p (h e) -> p h e", e=HD),
                                    num("fr", B * H)[:, t * H:(t + 1) * H].unsqueeze(2).to_broadcast([P, H, HD]), ALU.mult).then_inc(s["t_op"], 1)
                if 2 <= t:
                    b = t - 2
                    if b == 0 and not isinstance(j, int):
                        v.wait_ge(s["o_free"], j)
                    v.wait_ge(s["t_so"], j + 1)
                    v.wait_ge(s["t_mo"], B * j + b + 1)
                    d.scalar_tensor_tensor(a4[:, b], bank[3 + b % 2][:, 0:D], num("sow", B)[:, b:b + 1], bo[:], ALU.mult, ALU.add).then_inc(s["t_a"], 1)

            def dve_dot(j, b, res, ready, done):
                if b > 0:
                    v.wait_ge(s[done], B * j + b)
                v.wait_ge(s[ready], B * j + b + 1)
                d.scalar_tensor_tensor(spare, res, 1.0, ga4[:, b], ALU.mult, ALU.mult,
                                       accum_out=num("xaw", B)[:, b:b + 1]).then_inc(s[done], 1)

            def dve_sum(j, b, ready, done):
                v.wait_ge(s[ready], B * j + b + 1)
                d.scalar_tensor_tensor(x24[:, b], ga4[:, b], num("bew", B)[:, b:b + 1], x24[:, b], ALU.mult, ALU.add).then_inc(s[done], 1)
                v.wait_ge(s[done], B * j + b + 1)

            def dve_stats(j, b):
                d.bn_stats(mv6[:], x24[:, b]).then_inc(s["t_s6"], 1)
                hold(v, "t_s6", B * j + b + 1)
                d.bn_aggr(mv4[:, b, :], mv6[:]).then_inc(s["t_st"], 1)

            def dve_hidden(n, b, q):
                if q == 0:
                    v.wait_ge(s["t_nm"], n)
                    d.tensor_copy(num("nuw", B)[:, b:b + 1], bank[2][:, 0:1]).then_inc(s["t_ns"], 1)
                if q in (1, 3):
                    half = q // 2
                    v.wait_ge(s["t_fs"], n)
                    v.wait_ge(s["t_m1"], 2 * n - 1 + half)
                    d.scalar_tensor_tensor(tmp[:, half * 512:(half + 1) * 512], bank[half], num("suw", B)[:, b:b + 1],
                                           bf1[:, half * 512:(half + 1) * 512], ALU.mult, ALU.add).then_inc(s["t_f1"], 1)
                if q == 5:
                    v.wait_ge(s["t_m2"], n)
                    d.tensor_copy(a4[:, b], bank[4][:, 0:D]).then_inc(s["t_r4"], 1)

            def dve_step(m, i):
                v.wait_ge(s["l_A"], m)
                d.tensor_tensor_scan(gA[:], coef[:].rearrange("p c e -> p (c e)"), pA[:, 0:48], 0.0, ALU.mult, ALU.add).then_inc(s["l_gA"], 1)
                v.wait_ge(s["l_F"], m)
                d.tensor_tensor_scan(gF[:], coef[:, 0:8].rearrange("p c e -> p (c e)"), pF[:, 0:24], 0.0, ALU.mult, ALU.add).then_inc(s["l_gF"], 1)
                v.wait_ge(s["l_O"], m)
                d.tensor_tensor_scan(gO[:], coef[:, 0:8].rearrange("p c e -> p (c e)"), pO[:, 0:24], 0.0, ALU.mult, ALU.add).then_inc(s["l_gO"], 1)
                v.wait_ge(s["l_tA"], m)
                d.scalar_tensor_tensor(cadd[:, :, 2], tA[:, 8:16], 1.0, tA[:, 0:8], ALU.add, ALU.mult).then_inc(s["l_ig"], 1)
                v.wait_ge(s["l_ig"], m)
                v.wait_ge(s["l_tF"], m)
                d.tensor_tensor_scan(cnew[:].rearrange("p c e -> p (c e)"), cmul[:].rearrange("p c e -> p (c e)"),
                                     cadd[:].rearrange("p c e -> p (c e)"), 0.0, ALU.mult, ALU.add).then_inc(s["l_c"], 1)
                v.wait_ge(s["l_tO"], m)
                d.tensor_scalar(oU[:], tO[:], 1.0, 0.5 * H_UP, ALU.add, ALU.mult).then_inc(s["l_oU"], 1)
                v.wait_ge(s["l_tC"], m)
                v.wait_ge(s["l_oU"], m)
                hi, lo = (h16[:, :, :, half].rearrange("p k b -> p (k b)") for half in range(2))
                d.tensor_tensor(hi, oU[:], tC[:], ALU.mult).then_inc(s["l_hi"], 1)
                d.tensor_tensor(h32[:], oU[:], tC[:], ALU.mult).then_inc(s["l_h32"], 1)
                v.wait_ge(s["l_h32"], m)
                d.tensor_tensor(lo, h32[:], hi, ALU.subtract).then_inc(s["l_lo"], 1)
                d.tensor_copy(cadd[:, :, 0:2], cnew[:, :, 3:4].to_broadcast([P, KD * B, 2])).then_inc(s["l_cc"], 1)
                d.tensor_copy(hs[:, :, :, i:i + 1] if isinstance(i, int) else hs[:, :, :, bass.ds(i, 1)],
                              h32[:].rearrange("p (k b o) -> p k b o", b=B, o=1)).then_inc(s["l_hs"], 1)

            def dve_out(j):
                v.wait_ge(s["o_free"], j + 1)
                v.wait_ge(s["t_XX"], B * (j + 1))
                for b in range(B):
                    v.wait_ge(s["o_T"], j * B + b + 1)
                    d.scalar_tensor_tensor(ot[:, b * D:(b + 1) * D], bank[b][:, 0:D], 1.0 / H_UP, x_tile(j, b),
                                           ALU.mult, ALU.add).then_inc(s["o_s"], 1)

            def whole(j, step):
                along_attention(v, j, step, dve_attention)
                at = Slots(j, step)
                at.until(HEADS_SUM)
                dve_heads(j)
                at.until(WHOLE)
                dve_whole(j)
                for t in range(B + 4):
                    at.until(PROJECT + t)
                    if t < B + 2:
                        dve_project(j, t)
                    if PROJECT + t == SQUARES:
                        v.wait_ge(s["ld_xs"], 16 * (j + 1))
                    if 0 <= PROJECT + t - SQUARES < B:
                        dve_dot(j, PROJECT + t - SQUARES, x_tile(j, PROJECT + t - SQUARES), "t_ga", "t_xa")
                for b in range(B):
                    at.until(SUM + b)
                    dve_sum(j, b, "t_w", "t_x2")
                    dve_stats(j, b)

                def second(p, slot):
                    n, tiles = 2 * j + p + 1, (2 * p, 2 * p + 1)
                    if slot == 0:
                        v.wait_ge(s["t_sf"], n)
                        for b in tiles:
                            v.wait_ge(s["t_r4"], B * j + b + 2)
                            d.scalar_tensor_tensor(a4[:, b], a4[:, b], num("sfw", B)[:, b:b + 1], bf2[:], ALU.mult, ALU.add).then_inc(s["t_a2"], 1)
                    if slot in (1, 2):
                        dve_dot(j, tiles[slot - 1], x24[:, tiles[slot - 1]], "t_ga2", "t_xa2")
                    if slot == 6:
                        for b in tiles:
                            dve_sum(j, b, "t_w2", "t_x3")
                            d.tensor_tensor(x24[:, b], x24[:, b], x_tile(j, b), ALU.add).then_inc(s["t_X"], 1)

                for b in range(B):
                    for q in range(HIDDEN_SLOTS):
                        slot = HIDDEN + b * HIDDEN_SLOTS + q
                        at.until(slot)
                        dve_hidden(B * j + b + 1, b, q)
                        second(0, slot - SECOND[0])
                for slot in range(GATES[0], GATES[1] + 5):
                    at.until(slot)
                    second(1, slot - SECOND[1])
                at.rest()

            v.wait_ge(s["ld_xs"], 16 * 2)
            v.wait_ge(s["p_kT"], NT + 1)
            q_twice(0)
            v.sem_inc(s["t_o"], 2)
            v.sem_inc(s["t_l1"], 2)
            v.sem_inc(s["t_r4"], 1)
            whole(0, None)
            v.wait_ge(s["t_xc"], 2 * B)
            v.wait_ge(s["h0_s"], 1)
            d.tensor_tensor(xw[:, 0], xw[:, 0], h0c[:], ALU.add).then_inc(s["l_x0"], 1)
            with v.Fori(1, NB) as j:
                whole(j, dve_step)
                dve_out(j - 1)
            with v.Fori(0, P) as i:
                dve_step((NB - 1) * P + 1 + i, i)
            dve_out(NB - 1)


_INS = ["x", "cond_1024"] + [f"L0_cond_{n}" for n in ("w_q", "b_q", "w_k", "b_k", "w_v", "b_v", "w_o", "b_o", "w_f1", "b_f1",
                                                        "w_f2", "b_f2", "w_ada", "b_ada")] + ["L1_cond_Wx", "L1_cond_Wh", "L1_cond_b"]


def kernel(**inputs):
    import numpy as _np
    import concourse.bacc as _bacc
    from concourse import mybir as _mybir
    from concourse.bass_utils import run_bass_kernel_spmd as _run

    nc = _bacc.Bacc("TRN2", target_bir_lowering=False, num_devices=1)
    arrays, args = {}, []
    for name in _INS:
        a = _np.ascontiguousarray(inputs[name])
        arrays[f"in_{name}_dram"] = a
        args.append(nc.dram_tensor(f"in_{name}_dram", a.shape, _mybir.dt.from_np(a.dtype), kind="ExternalInput").ap())
    args.append(nc.dram_tensor("out_0_dram", (B, T, D), _mybir.dt.float32, kind="ExternalOutput").ap())
    bass_hyperbolic_block_then_lstm(nc, *args)
    r = _run(nc, [arrays], core_ids=[0])
    return r.results[0]["out_0_dram"]
```
